# Optimizing a Trainium2 kernel written in Bass

```python
import numpy as np
import jax
import jax.numpy as jnp

def _softmax(x, axis=-1):
    return jax.nn.softmax(x, axis=axis)

def _gelu(x):
    return jax.nn.gelu(x, approximate=True)

def _silu(x):
    return jax.nn.silu(x)

def _sigmoid(x):
    return jax.nn.sigmoid(x)

def _layernorm(x, axis=-1, eps=1e-05):
    m = jnp.mean(x, axis=axis, keepdims=True)
    v = jnp.var(x, axis=axis, keepdims=True)
    return (x - m) / jnp.sqrt(v + eps)

def _scatter_add(tgt, idx, src, axis=0):
    return tgt.at[idx].add(src)

def _segment_sum(src, seg, n):
    return jax.ops.segment_sum(src, seg, n)
kernel_name = 'mk_hybrid_d1_jaxref_r8_451470'

def setup_inputs(seed: int=0):
    np.random.seed(seed)
    _w = jnp.asarray

    def _L0_attn_a_setup():
        import jax, jax.numpy as jnp
        import numpy as np
        D_MODEL = 128
        NUM_HEADS = 16
        D_HEAD = D_MODEL // NUM_HEADS
        LAMBDA_INIT = 0.8
        EPS = 1e-05
        key = jax.random.key(seed)
        ks = jax.random.split(key, 10)
        B, N = (2, 256)

        def xav(k, shape):
            fan_in, fan_out = (shape[0], shape[1])
            lim = np.sqrt(6.0 / (fan_in + fan_out))
            return jax.random.uniform(k, shape, jnp.float32, -lim, lim)
        return {'X': jax.random.normal(ks[0], (B, N, D_MODEL), jnp.float32), 'Wq': xav(ks[1], (D_MODEL, 2 * D_MODEL)), 'Wk': xav(ks[2], (D_MODEL, 2 * D_MODEL)), 'Wv': xav(ks[3], (D_MODEL, 2 * D_MODEL)), 'Wo': xav(ks[4], (2 * D_MODEL, D_MODEL)), 'lambda_q1': jax.random.normal(ks[5], (NUM_HEADS, D_HEAD), jnp.float32), 'lambda_k1': jax.random.normal(ks[6], (NUM_HEADS, D_HEAD), jnp.float32), 'lambda_q2': jax.random.normal(ks[7], (NUM_HEADS, D_HEAD), jnp.float32), 'lambda_k2': jax.random.normal(ks[8], (NUM_HEADS, D_HEAD), jnp.float32), 'rms_scale': jnp.ones((2 * D_HEAD,), jnp.float32)}
    _L0_attn_a_in = _L0_attn_a_setup()

    def _L0_attn_b_setup():
        import jax, jax.numpy as jnp
        import numpy as np
        MODEL_DIM = 128
        NUM_HEADS = 16
        HEAD_DIM = MODEL_DIM // NUM_HEADS
        EPS = 1e-12
        CHUNK = 128

        def _pos_elu(t):
            return jax.nn.elu(t) + 1.0

        def _linear_attention(q, k, v):
            b, h, l, d = q.shape
            nc = l // CHUNK
            qc = jnp.moveaxis(q.reshape(b, h, nc, CHUNK, d), 2, 0)
            kc = jnp.moveaxis(k.reshape(b, h, nc, CHUNK, d), 2, 0)
            vc = jnp.moveaxis(v.reshape(b, h, nc, CHUNK, d), 2, 0)
            mask = jnp.tril(jnp.ones((CHUNK, CHUNK), dtype=q.dtype))

            def step(carry, inp):
                S, z = carry
                qb, kb, vb = inp
                scores = jnp.einsum('bhcd,bhsd->bhcs', qb, kb) * mask
                num = jnp.einsum('bhcd,bhde->bhce', qb, S) + jnp.einsum('bhcs,bhse->bhce', scores, vb)
                den = jnp.einsum('bhcd,bhd->bhc', qb, z) + scores.sum(-1)
                out = num / den[..., None] + EPS
                S = S + jnp.einsum('bhsd,bhse->bhde', kb, vb)
                z = z + kb.sum(axis=2)
                return ((S, z), out)
            S0 = jnp.zeros((b, h, d, d), dtype=q.dtype)
            z0 = jnp.zeros((b, h, d), dtype=q.dtype)
            _, outs = jax.lax.scan(step, (S0, z0), (qc, kc, vc))
            return jnp.moveaxis(outs, 0, 1).transpose(0, 3, 1, 2, 4).reshape(b, h * 0 + l // l, 0, 0) if False else outs
        key = jax.random.key(seed)
        kx, kq, kk, kv, ko = jax.random.split(key, 5)
        b, l = (4, 512)
        x = jax.random.normal(kx, (b, l, MODEL_DIM), dtype=jnp.float32)
        Wq = 0.02 * jax.random.normal(kq, (MODEL_DIM, MODEL_DIM), dtype=jnp.float32)
        Wk = 0.02 * jax.random.normal(kk, (MODEL_DIM, MODEL_DIM), dtype=jnp.float32)
        Wv = 0.02 * jax.random.normal(kv, (MODEL_DIM, MODEL_DIM), dtype=jnp.float32)
        Wo = 0.02 * jax.random.normal(ko, (MODEL_DIM, MODEL_DIM), dtype=jnp.float32)
        return {'x': x, 'Wq': Wq, 'Wk': Wk, 'Wv': Wv, 'Wo': Wo}
    _L0_attn_b_in = _L0_attn_b_setup()

    def _L0_ffn_setup():
        import jax, jax.numpy as jnp
        import numpy as np
        TOP_K = 32
        TEMPERATURE = 1.0
        PARAM_SCALE = 0.02

        def _compose_weight(logits, A, B):
            vals, idx = jax.lax.top_k(logits, TOP_K)
            w = jax.nn.softmax(vals / TEMPERATURE)
            A_sel = A[idx]
            B_sel = B[idx]
            return jnp.einsum('k,kir,kro->io', w, A_sel, B_sel)
        key = jax.random.key(seed)
        ks = jax.random.split(key, 7)
        B, S, D, F, P, R = (2, 128, 128, 512, 32, 64)
        x = jax.random.normal(ks[0], (B, S, D), dtype=jnp.float32)
        fc1_A = jax.random.normal(ks[1], (P, D, R), dtype=jnp.float32) * PARAM_SCALE
        fc1_B = jax.random.normal(ks[2], (P, R, F), dtype=jnp.float32) * PARAM_SCALE
        fc2_A = jax.random.normal(ks[3], (P, F, R), dtype=jnp.float32) * PARAM_SCALE
        fc2_B = jax.random.normal(ks[4], (P, R, D), dtype=jnp.float32) * PARAM_SCALE
        fc1_logits = jax.random.normal(ks[5], (P,), dtype=jnp.float32)
        fc2_logits = jax.random.normal(ks[6], (P,), dtype=jnp.float32)
        return {'x': x, 'fc1_A': fc1_A, 'fc1_B': fc1_B, 'fc2_A': fc2_A, 'fc2_B': fc2_B, 'fc1_logits': fc1_logits, 'fc2_logits': fc2_logits}
    _L0_ffn_in = _L0_ffn_setup()
    _d = {'L0_attn_a_X': _L0_attn_a_in['X'], 'L0_attn_a_Wq': _L0_attn_a_in['Wq'], 'L0_attn_a_Wk': _L0_attn_a_in['Wk'], 'L0_attn_a_Wv': _L0_attn_a_in['Wv'], 'L0_attn_a_Wo': _L0_attn_a_in['Wo'], 'L0_attn_a_lambda_q1': _L0_attn_a_in['lambda_q1'], 'L0_attn_a_lambda_k1': _L0_attn_a_in['lambda_k1'], 'L0_attn_a_lambda_q2': _L0_attn_a_in['lambda_q2'], 'L0_attn_a_lambda_k2': _L0_attn_a_in['lambda_k2'], 'L0_attn_a_rms_scale': _L0_attn_a_in['rms_scale'], 'L0_attn_b_Wq': _L0_attn_b_in['Wq'], 'L0_attn_b_Wk': _L0_attn_b_in['Wk'], 'L0_attn_b_Wv': _L0_attn_b_in['Wv'], 'L0_attn_b_Wo': _L0_attn_b_in['Wo'], 'L0_ffn_fc1_A': _L0_ffn_in['fc1_A'], 'L0_ffn_fc1_B': _L0_ffn_in['fc1_B'], 'L0_ffn_fc2_A': _L0_ffn_in['fc2_A'], 'L0_ffn_fc2_B': _L0_ffn_in['fc2_B'], 'L0_ffn_fc1_logits': _L0_ffn_in['fc1_logits'], 'L0_ffn_fc2_logits': _L0_ffn_in['fc2_logits']}
    _x0 = _d['L0_attn_a_X']
    _d['L0_attn_a_X'] = jax.random.normal(jax.random.fold_in(jax.random.key(seed), 1), (8, 256, 128), dtype=_x0.dtype)
    del _x0
    return _d

def reference(L0_attn_a_X, L0_attn_a_Wq, L0_attn_a_Wk, L0_attn_a_Wv, L0_attn_a_Wo, L0_attn_a_lambda_q1, L0_attn_a_lambda_k1, L0_attn_a_lambda_q2, L0_attn_a_lambda_k2, L0_attn_a_rms_scale, L0_attn_b_Wq, L0_attn_b_Wk, L0_attn_b_Wv, L0_attn_b_Wo, L0_ffn_fc1_A, L0_ffn_fc1_B, L0_ffn_fc2_A, L0_ffn_fc2_B, L0_ffn_fc1_logits, L0_ffn_fc2_logits):

    def _L0_attn_a_ref(X, Wq, Wk, Wv, Wo, lambda_q1, lambda_k1, lambda_q2, lambda_k2, rms_scale):
        import jax, jax.numpy as jnp
        import numpy as np
        D_MODEL = 128
        NUM_HEADS = 16
        D_HEAD = D_MODEL // NUM_HEADS
        LAMBDA_INIT = 0.8
        EPS = 1e-05
        B, N, _ = X.shape
        H, Dh = (NUM_HEADS, D_HEAD)
        Q = (X @ Wq).reshape(B, N, H, 2 * Dh).transpose(0, 2, 1, 3)
        K = (X @ Wk).reshape(B, N, H, 2 * Dh).transpose(0, 2, 1, 3)
        V = (X @ Wv).reshape(B, N, H, 2 * Dh).transpose(0, 2, 1, 3)
        Q1, Q2 = (Q[..., :Dh], Q[..., Dh:])
        K1, K2 = (K[..., :Dh], K[..., Dh:])
        lam = jnp.exp(jnp.sum(lambda_q1 * lambda_k1, -1)) - jnp.exp(jnp.sum(lambda_q2 * lambda_k2, -1)) + LAMBDA_INIT
        scaling = 1.0 / np.sqrt(Dh)
        causal = jnp.tril(jnp.ones((N, N), bool))
        neg_inf = jnp.float32(-jnp.inf)
        A1 = jnp.einsum('bhqd,bhkd->bhqk', Q1, K1) * scaling
        A2 = jnp.einsum('bhqd,bhkd->bhqk', Q2, K2) * scaling
        A1 = jnp.where(causal, A1, neg_inf)
        A2 = jnp.where(causal, A2, neg_inf)
        attn = jax.nn.softmax(A1, axis=-1) - lam[None, :, None, None] * jax.nn.softmax(A2, axis=-1)
        O = jnp.einsum('bhqk,bhkd->bhqd', attn, V)
        rms = jnp.sqrt(jnp.mean(O * O, axis=-1, keepdims=True) + EPS)
        O = O / rms * rms_scale
        O = O * (1.0 - LAMBDA_INIT)
        O = O.transpose(0, 2, 1, 3).reshape(B, N, H * 2 * Dh)
        return O @ Wo

    def _L0_attn_b_ref(x, Wq, Wk, Wv, Wo):
        import jax, jax.numpy as jnp
        import numpy as np
        MODEL_DIM = 128
        NUM_HEADS = 16
        HEAD_DIM = MODEL_DIM // NUM_HEADS
        EPS = 1e-12
        CHUNK = 128

        def _pos_elu(t):
            return jax.nn.elu(t) + 1.0

        def _linear_attention(q, k, v):
            b, h, l, d = q.shape
            nc = l // CHUNK
            qc = jnp.moveaxis(q.reshape(b, h, nc, CHUNK, d), 2, 0)
            kc = jnp.moveaxis(k.reshape(b, h, nc, CHUNK, d), 2, 0)
            vc = jnp.moveaxis(v.reshape(b, h, nc, CHUNK, d), 2, 0)
            mask = jnp.tril(jnp.ones((CHUNK, CHUNK), dtype=q.dtype))

            def step(carry, inp):
                S, z = carry
                qb, kb, vb = inp
                scores = jnp.einsum('bhcd,bhsd->bhcs', qb, kb) * mask
                num = jnp.einsum('bhcd,bhde->bhce', qb, S) + jnp.einsum('bhcs,bhse->bhce', scores, vb)
                den = jnp.einsum('bhcd,bhd->bhc', qb, z) + scores.sum(-1)
                out = num / den[..., None] + EPS
                S = S + jnp.einsum('bhsd,bhse->bhde', kb, vb)
                z = z + kb.sum(axis=2)
                return ((S, z), out)
            S0 = jnp.zeros((b, h, d, d), dtype=q.dtype)
            z0 = jnp.zeros((b, h, d), dtype=q.dtype)
            _, outs = jax.lax.scan(step, (S0, z0), (qc, kc, vc))
            return jnp.moveaxis(outs, 0, 1).transpose(0, 3, 1, 2, 4).reshape(b, h * 0 + l // l, 0, 0) if False else outs
        b, l, D = x.shape
        h, d = (NUM_HEADS, HEAD_DIM)
        q = (x @ Wq.T).reshape(b, l, h, d).transpose(0, 2, 1, 3)
        k = (x @ Wk.T).reshape(b, l, h, d).transpose(0, 2, 1, 3)
        v = (x @ Wv.T).reshape(b, l, h, d).transpose(0, 2, 1, 3)
        q = _pos_elu(q)
        k = _pos_elu(k)
        outs = _linear_attention(q, k, v)
        nc = l // CHUNK
        attn = outs.transpose(1, 0, 3, 2, 4).reshape(b, l, D)
        return attn @ Wo.T

    def _L0_ffn_ref(x, fc1_A, fc1_B, fc2_A, fc2_B, fc1_logits, fc2_logits):
        import jax, jax.numpy as jnp
        import numpy as np
        TOP_K = 32
        TEMPERATURE = 1.0
        PARAM_SCALE = 0.02

        def _compose_weight(logits, A, B):
            vals, idx = jax.lax.top_k(logits, TOP_K)
            w = jax.nn.softmax(vals / TEMPERATURE)
            A_sel = A[idx]
            B_sel = B[idx]
            return jnp.einsum('k,kir,kro->io', w, A_sel, B_sel)
        W1 = _compose_weight(fc1_logits, fc1_A, fc1_B)
        W2 = _compose_weight(fc2_logits, fc2_A, fc2_B)
        h = jax.nn.gelu(jnp.einsum('bsd,df->bsf', x, W1))
        return jnp.einsum('bsf,fd->bsd', h, W2)
    x = L0_attn_a_X
    x = x + _L0_attn_a_ref(_layernorm(x, axis=-1), L0_attn_a_Wq, L0_attn_a_Wk, L0_attn_a_Wv, L0_attn_a_Wo, L0_attn_a_lambda_q1, L0_attn_a_lambda_k1, L0_attn_a_lambda_q2, L0_attn_a_lambda_k2, L0_attn_a_rms_scale)
    x = x + _L0_ffn_ref(_layernorm(x, axis=-1), L0_ffn_fc1_A, L0_ffn_fc1_B, L0_ffn_fc2_A, L0_ffn_fc2_B, L0_ffn_fc1_logits, L0_ffn_fc2_logits)
    x = x + _L0_attn_b_ref(_layernorm(x, axis=-1), L0_attn_b_Wq, L0_attn_b_Wk, L0_attn_b_Wv, L0_attn_b_Wo)
    x = x + _L0_ffn_ref(_layernorm(x, axis=-1), L0_ffn_fc1_A, L0_ffn_fc1_B, L0_ffn_fc2_A, L0_ffn_fc2_B, L0_ffn_fc1_logits, L0_ffn_fc2_logits)
    return x

_drawn_inputs = setup_inputs


def setup_inputs(seed=0):
    import zlib

    import numpy as np

    out = dict(_drawn_inputs(seed))
    spreads = {'L0_attn_a_rms_scale': (1.0, 0.2)}
    factors = {'L0_attn_b_Wq': 49.958,
     'L0_attn_b_Wk': 37.628,
     'L0_attn_b_Wv': 5.54,
     'L0_attn_b_Wo': 5.47,
     'L0_ffn_fc1_A': 8.0,
     'L0_ffn_fc1_B': 8.0,
     'L0_ffn_fc2_A': 8.0,
     'L0_ffn_fc2_B': 8.0,
     'L0_ffn_fc1_logits': 8.0,
     'L0_ffn_fc2_logits': 8.0}
    for name, (base, spread) in spreads.items():
        noise = np.random.default_rng([zlib.crc32(name.encode()), seed]).standard_normal(out[name].shape)
        drawn = base * np.exp(spread * noise) if base else spread * noise
        out[name] = jnp.asarray(drawn.astype(out[name].dtype))
    for name, factor in factors.items():
        out[name] = (out[name] * factor).astype(out[name].dtype)
    return out
```

```python
from contextlib import ExitStack

import numpy as np

import concourse.bass as bass
from concourse import mybir

F32 = mybir.dt.float32
BF16 = mybir.dt.bfloat16
ALU = mybir.AluOpType
ACT = mybir.ActivationFunctionType
AX = mybir.AxisListType.X

P = 128
SEQS, SEQ, D = 8, 256, 128
TILES = SEQS * SEQ // P
FIRST = 1
TPS = SEQ // P
HEADS, DH = 16, 8
DV = 2 * DH
MAPS = 2 * HEADS
F = 512
FCH = F // P
PRIMS, R = 32, 64
KR = PRIMS * R // P
LN_EPS = 1e-5
RMS_EPS = 1e-5
LIN_EPS = 1e-12
LAMBDA_INIT = 0.8
SCALE = float(1.0 / np.sqrt(DH))
NEG = -1e30

Q_PART = (0, 0, 1, 1, 0, 2)
K_PART = (0, 1, 0, 1, 2, 0)
TERMS = len(Q_PART)
SROWS = TERMS * DH
SHIFT_ROWS = 2
XROWS = SROWS + SHIFT_ROWS

GMAPS = 16
GROUPS = SEQS * MAPS // GMAPS
UMAPS = 4
UNITS = SEQS * MAPS // UMAPS
UPG = GMAPS // UMAPS
UPS = MAPS // UMAPS
SLOTS = 16
BANKS_U = 3
L_SHIFT, L_EXP, L_PV, L_OT, L_VAUG = 4, 6, 7, 8, 2
L_DEN, L_DIFF, L_SQ, L_MS, L_NORM, L_OPT, L_OPROJ, L_STAT = 16, 17, 18, 19, 20, 22, 23, 23


def live(index, count):
    return not isinstance(index, int) or 0 <= index < count


def past(value):
    return not isinstance(value, int) or value > 0


def repeat(eng, turns, turn):
    turn(0)
    with eng.Fori(1, turns) as it:
        turn(it)


def hybrid_kernel(nc, X, Wq, Wk, Wv, Wo, lq1, lk1, lq2, lk2, rms_scale, bWq, bWk, bWv, bWo,
                  fc1_A, fc1_B, fc2_A, fc2_B, fc1_logits, fc2_logits, out):
    x_tiles = X.rearrange("b (t p) d -> p (b t) d", p=P)
    out_tiles = out.rearrange("b (t p) d -> p (b t) d", p=P)
    parts_dram = nc.dram_tensor("qk_parts", (SEQS, 12, P, SEQ), BF16, kind="Internal").ap()

    with ExitStack() as ctx:
        def sb(name, shape, dt=F32):
            return ctx.enter_context(nc.sbuf_tensor(name, shape, dt))

        def sem(name):
            return ctx.enter_context(nc.semaphore(name))

        ps = ctx.enter_context(nc.psum_tensor("ps", [P, 8, 512], F32))

        xs = sb("xs", [P, TILES, D])
        moments = sb("moments", [P, TILES, 2])
        stats = sb("stats", [P, TILES, 6])
        moments_new = sb("moments_new", [P, 4, 2])
        rstd = sb("rstd", [P, TILES])
        veps = sb("veps", [P, TILES])
        minus_half = sb("minus_half", [P, 64])
        ident = sb("ident", [P, P])
        ident_bf = sb("ident_bf", [P, P], BF16)
        future_bf = sb("future_bf", [P, UMAPS, P], BF16)
        upto = sb("upto", [P, P])
        ones = sb("ones", [P, P])
        wqkv = sb("wqkv", [P, 3, 2 * D])
        wo_raw = sb("wo_raw", [P, 2, D])
        wo = sb("wo", [P, 2, D])
        rms_col = sb("rms_col", [P, 1])
        wb_raw = sb("wb_raw", [P, 4, D])
        wbT = sb("wbT", [P, 4, D])
        lam_in = sb("lam_in", [P, 4, HEADS * DH])
        lam_prod = sb("lam_prod", [P, 2, HEADS * DH])
        lam_sum = sb("lam_sum", [P, 2, HEADS])
        lam_exp = sb("lam_exp", [P, 2, HEADS])
        lam = sb("lam", [P, HEADS])
        logits = sb("logits", [P, 2, PRIMS])
        lg_negmax = sb("lg_negmax", [P, 2])
        lg_exp = sb("lg_exp", [P, 2, PRIMS])
        lg_sum = sb("lg_sum", [P, 2])
        lg_inv = sb("lg_inv", [P, 2])
        mix = sb("mix", [P, 2, PRIMS])
        mix_col = sb("mix_col", [P, 2, KR])
        w1 = sb("w1", [P, F])
        w2 = sb("w2", [P, FCH, D])
        values = sb("values", [P, TILES, 2 * D])
        xn1 = sb("xn1", [P, 2, TPS, D])
        xnT1 = sb("xnT1", [P, 2, SEQ])
        qk_parts = sb("qk_parts_sb", [P, 2, 12, SEQ], BF16)
        qk_rest = sb("qk_rest", [P, 2, 2, 512])
        a1T = sb("a1T", [P, KR, P])
        a2T = sb("a2T", [P, 4, F])
        stack01 = sb("stack01", [64, 2, 2, GMAPS, SEQ], BF16)
        arena = sb("arena", [P, 20480])

        def carve(at, shape, dt=F32, parts=P):
            n = int(np.prod(shape))
            words = n if dt == F32 else n // 2
            ap = arena[0:parts, at:at + words]
            if dt != F32:
                ap = ap.bitcast(dt)
            names = "abcdef"[:len(shape)]
            if len(shape) > 1:
                ap = ap.rearrange(f"p ({' '.join(names)}) -> p {' '.join(names)}",
                                  **{k: s for k, s in zip(names[1:], shape[1:])})
            return ap, at + words

        a1, at = carve(0, (PRIMS * R,))
        b1, at = carve(at, (KR, F))
        a2, at = carve(at, (FCH, PRIMS * R))
        b2, at = carve(at, (KR, D))

        stack23, at = carve(0, (2, 2, GMAPS, SEQ), BF16, 64)
        vaug, at = carve(at, (2, TPS, HEADS, 32))
        probs, at = carve(at, (2, BANKS_U, 512))
        ot_sb, at = carve(at, (2, SEQ))
        o_sb, at = carve(at, (2, TPS, MAPS, DV + 1))
        rowmax, at = carve(at, (2, TPS, GMAPS))
        shift, at = carve(at, (2, SHIFT_ROWS, SEQ), BF16, GMAPS)
        rden, at = carve(at, (TPS, MAPS))
        rden2, at = carve(at, (TPS, HEADS))
        o1, at = carve(at, (TPS, HEADS, DV))
        o2, at = carve(at, (TPS, HEADS, DV))
        osq, at = carve(at, (TPS, HEADS, DV))
        o_n, at = carve(at, (TPS, HEADS, DV))
        msum, at = carve(at, (TPS * HEADS,))
        mrms, at = carve(at, (TPS * HEADS,))
        oT, at = carve(at, (TPS, 2, P))

        def q_stack(slot):
            return stack01[:, slot, 0] if slot < 2 else stack23[:, slot - 2, 0]

        def k_stack(slot):
            return stack01[:, slot, 1] if slot < 2 else stack23[:, slot - 2, 1]

        x_in = [sem(f"x_in{i}") for i in range(4)]
        w_in = sem("w_in")
        tick_pool, tick_dve = sem("tick_pool"), sem("tick_dve")
        small_in = sem("small_in")
        rms_in = sem("rms_in")
        factors_in = [sem(f"factors_in{i}") for i in range(4)]
        consts = sem("consts")
        half_done = sem("half_done")
        stats_done = sem("stats_done")
        moments_done = sem("moments_done")
        veps_done = sem("veps_done")
        rstd_done = sem("rstd_done")
        xn_done = sem("xn_done")
        xT_done = sem("xT_done")
        xnT_done = sem("xnT_done")
        proj_done = sem("proj_done")
        high_done = sem("high_done")
        rest_done = sem("rest_done")
        mid_done = sem("mid_done")
        low_done = sem("low_done")
        v_done = sem("v_done")
        parts_out = [sem(f"parts_out{i}") for i in range(2)]
        stack_in = [sem(f"stack_in{i}") for i in range(4)]
        s_lg = sem("s_lg")
        s_lge = sem("s_lge")
        s_mix = sem("s_mix")
        s_lam = sem("s_lam")
        s_lame = sem("s_lame")
        wbT_ps = sem("wbT_ps")
        wbT_done = sem("wbT_done")
        wo_done = sem("wo_done")
        fT_ps = sem("fT_ps")
        fT_done = sem("fT_done")
        fT_done_act = sem("fT_done_act")
        acc_done = sem("acc_done")
        w12_done = sem("w12_done")

        def load_stack(eng, g, slot):
            half = slot % 2
            seq = (g - half) // 2 if isinstance(g, int) else g
            for t in range(TERMS):
                for side, part in ((0, Q_PART[t]), (1, K_PART[t])):
                    src = parts_dram[seq, 4 * part + 2 * side + half].rearrange("(m d) t -> d m t", d=DH)
                    dst = q_stack(slot) if side == 0 else k_stack(slot)
                    eng.dma_start(dst[DH * t:DH * (t + 1)], src).then_inc(stack_in[slot], 16)

        def carry_wait(eng, tick):
            eng.sem_inc(tick, 1)

        def token_moments(dve, tick, tile, n, stats_sem, aggr_sem, k, first=0):
            if past(k):
                dve.wait_ge(aggr_sem, first + 2 * k)
            carry_wait(dve, tick)
            for t in range(n):
                last = nc.vector.bn_stats(stats[:, t, :], xs[:, tile + t, :])
            last.then_inc(stats_sem, 1)
            dve.wait_ge(stats_sem, k + 1)
            carry_wait(dve, tick)
            for t in range(n):
                last = nc.vector.bn_aggr(moments_new[:, t, :], stats[:, t, :])
            last.then_inc(aggr_sem, 1)
            dve.wait_ge(aggr_sem, first + 2 * k + 1)
            nc.vector.tensor_scalar(moments[:, bass.ds(tile, n), :], moments_new[:, 0:n, :], 1.0, None,
                                    op0=ALU.mult).then_inc(aggr_sem, 1)

        FGROUPS = 4 + KR

        with nc.Block() as block:
            @block.sync
            def _(sp):
                sp.dma_start(xs[:, 0:4, :], x_tiles[:, 0:4, :]).then_inc(x_in[0], 16)
                for i, w in enumerate((Wq, Wk, Wv)):
                    sp.dma_start(wqkv[:, i, :], w).then_inc(w_in, 16)
                for i in range(1, 4):
                    sp.dma_start(xs[:, 4 * i:4 * i + 4, :], x_tiles[:, 4 * i:4 * i + 4, :]).then_inc(x_in[i], 16)
                for i, w in enumerate((bWq, bWk, bWv, bWo)):
                    sp.dma_start(wb_raw[:, i, :], w).then_inc(small_in, 16)
                sp.dma_start(wo_raw[:, :, :], Wo.rearrange("(c p) n -> p c n", p=P)).then_inc(small_in, 16)
                for i, w in enumerate((lq1, lk1, lq2, lk2)):
                    sp.dma_start(lam_in[:, i, :],
                                 w.rearrange("h d -> (h d)").partition_broadcast(P)).then_inc(small_in, 16)
                for i, w in enumerate((fc1_logits, fc2_logits)):
                    sp.dma_start(logits[:, i, :], w.partition_broadcast(P)).then_inc(small_in, 16)
                for i in range(P // DV):
                    sp.dma_start(rms_col[DV * i:DV * (i + 1), :],
                                 rms_scale.rearrange("(p a) -> p a", a=1)).then_inc(rms_in, 16)
                with sp.Fori(0, SEQS // 2) as it:
                    for u in range(2):
                        sp.wait_ge(low_done, 2 * (2 * it + u) + 2)
                        sp.dma_start(parts_dram[2 * it + u].rearrange("c p t -> p c t"),
                                     qk_parts[:, u]).then_inc(parts_out[u], 16)
                for u in range(2):
                    sp.wait_ge(parts_out[u], 16 * SEQS // 2)
                sp.wait_ge(consts, 7)
                for g in range(2):
                    load_stack(sp, g, g)

            @block.gpsimd
            def _(pool):
                nc.gpsimd.memset(minus_half[:], -0.5).then_inc(half_done, 1)
                nc.gpsimd.memset(ident[:], 0.0)
                nc.gpsimd.memset(upto[:], 1.0)
                nc.gpsimd.memset(ones[:], 1.0)
                nc.gpsimd.memset(future_bf[:], 0.0).then_inc(consts, 1)
                pool.wait_ge(consts, 1)
                nc.gpsimd.affine_select(out=ident[:], in_=ident[:], compare_op=ALU.not_equal, fill=1.0,
                                        base=0, pattern=[[-1, P]], channel_multiplier=1).then_inc(consts, 1)
                nc.gpsimd.affine_select(out=upto[:], in_=upto[:], compare_op=ALU.is_ge, fill=0.0,
                                        base=0, pattern=[[1, P]], channel_multiplier=-1).then_inc(consts, 1)
                nc.gpsimd.affine_select(out=future_bf[:], in_=future_bf[:], compare_op=ALU.is_ge, fill=NEG,
                                        base=0, pattern=[[0, UMAPS], [-1, P]],
                                        channel_multiplier=1).then_inc(consts, 1)
                pool.wait_ge(consts, 2)
                nc.gpsimd.tensor_copy(ident_bf[:], ident[:]).then_inc(consts, 1)
                for i in range(4):
                    c = slice(4 * i, 4 * i + 4)
                    pool.wait_ge(moments_done, 4 * i + 4)
                    nc.gpsimd.tensor_scalar(veps[:, c], moments[:, c, 1], LN_EPS, None,
                                            op0=ALU.add).then_inc(veps_done, 1)
                    pool.wait_ge(veps_done, i + 1)
                    pool.wait_ge(half_done, 1)
                    nc.gpsimd.tensor_tensor(rstd[:, c], veps[:, c], minus_half[:, 0:4],
                                            op=ALU.pow).then_inc(rstd_done, 1)
                pair = float(np.array([0x3F803F80], np.uint32).view(np.float32)[0])
                for slot in range(2):
                    nc.gpsimd.memset(k_stack(slot).rearrange("p m t -> p (m t)").bitcast(F32),
                                     pair).then_inc(consts, 1)
                def turn(it):
                    for u in range(2):
                        for side in range(2):
                            pool.wait_ge(mid_done, 2 * (2 * it + u) + side + 1)
                            nc.gpsimd.tensor_tensor(
                                qk_parts[:, u, 8 + 2 * side:10 + 2 * side, :].rearrange("p c t -> p (c t)"),
                                qk_rest[:, u, side, :],
                                qk_parts[:, u, 4 + 2 * side:6 + 2 * side, :].rearrange("p c t -> p (c t)"),
                                op=ALU.subtract).then_inc(low_done, 1)

                repeat(pool, SEQS // 2, turn)

            @block.scalar
            def _(act):
                act.dma_start(a1, fc1_A.rearrange("k d r -> d k r")).then_inc(factors_in[0], 16)
                act.dma_start(b1, fc1_B.rearrange("k r f -> (k r) f").rearrange("(c p) f -> p c f", p=P))\
                   .then_inc(factors_in[1], 16)
                for c in range(FCH):
                    act.dma_start(a2[:, c, :], fc2_A[:, c * P:(c + 1) * P, :].rearrange("k f r -> f k r"))\
                       .then_inc(factors_in[2], 16)
                act.dma_start(b2, fc2_B.rearrange("k r f -> (k r) f").rearrange("(c p) f -> p c f", p=P))\
                   .then_inc(factors_in[3], 16)
                for i in range(2):
                    act.wait_ge(s_lg, 2)
                    nc.scalar.activation(lg_exp[:, i, :], logits[:, i, :], ACT.Exp, bias=lg_negmax[:, i:i + 1],
                                         accum_out=lg_sum[:, i:i + 1]).then_inc(s_lge, 1)
                act.wait_ge(s_lam, 2)
                nc.scalar.activation(lam_exp[:], lam_sum[:], ACT.Exp).then_inc(s_lame, 1)
                def turn(it):
                    for u in range(2):
                        b = 2 * it + u
                        act.wait_ge(xT_done, b + 1)
                        nc.scalar.copy(xnT1[:, u, :], ps[:, 4 * u, 0:SEQ]).then_inc(xnT_done, 1)
                    for u in range(2):
                        b = 2 * it + u
                        if past(it):
                            act.wait_ge(parts_out[u], 16 * it)
                        for side in range(2):
                            act.wait_ge(proj_done, 3 * b + side + 1)
                            nc.scalar.copy(
                                qk_parts[:, u, 2 * side:2 * side + 2, :].rearrange("p c t -> p (c t)"),
                                ps[:, 4 * u + 1 + side, :]).then_inc(high_done, 1)
                        act.wait_ge(proj_done, 3 * b + 3)
                        nc.scalar.copy(values[:, bass.ds(2 * b, 2), :].rearrange("p a b -> p (a b)"),
                                       ps[:, 4 * u + 3, :]).then_inc(v_done, 1)

                repeat(act, SEQS // 2, turn)
                act.wait_ge(wbT_ps, 1)
                nc.scalar.copy(wbT[:].rearrange("p a b -> p (a b)"), ps[:, 4, :]).then_inc(wbT_done, 1)
                for i in range(5, FGROUPS, 2):
                    act.wait_ge(fT_ps, i + 1)
                    if i >= 8:
                        act.wait_ge(acc_done, i - 3)
                    nc.scalar.activation(a2T[:, (i - 4) % 4, :], ps[:, i % 2, :], ACT.Copy,
                                         scale=mix_col[:, 1, i - 4:i - 3]).then_inc(fT_done_act, 1)
                act.wait_ge(acc_done, FGROUPS)
                nc.scalar.copy(w2[:].rearrange("p a b -> p (a b)"), ps[:, 3, :]).then_inc(w12_done, 1)

            @block.vector
            def _(dve):
                for t in range(TILES):
                    if t % 4 == 0:
                        dve.wait_ge(x_in[t // 4], 16)
                    nc.vector.bn_stats(stats[:, t, :], xs[:, t, :]).then_inc(stats_done, 1)
                    if t % 4 == 3:
                        for j in range(t - 3, t + 1):
                            dve.wait_ge(stats_done, t + 1)
                            nc.vector.bn_aggr(moments[:, j, :], stats[:, j, :]).then_inc(moments_done, 1)
                dve.wait_ge(small_in, 16 * 11)
                for i in range(2):
                    nc.vector.tensor_reduce(out=lg_negmax[:, i:i + 1], in_=logits[:, i, :], axis=AX, op=ALU.max,
                                            negate=True).then_inc(s_lg, 1)
                for i in range(2):
                    nc.vector.tensor_tensor(lam_prod[:, i, :], lam_in[:, 2 * i, :], lam_in[:, 2 * i + 1, :],
                                            op=ALU.mult).then_inc(s_mix, 1)
                for i in range(2):
                    dve.wait_ge(s_mix, i + 1)
                    nc.vector.tensor_reduce(out=lam_sum[:, i, :],
                                            in_=lam_prod[:, i, :].rearrange("p (h d) -> p h d", d=DH),
                                            axis=AX, op=ALU.add).then_inc(s_lam, 1)
                dve.wait_ge(s_lge, 2)
                nc.vector.reciprocal(lg_inv[:], lg_sum[:]).then_inc(s_mix, 1)
                dve.wait_ge(s_mix, 3)
                for i in range(2):
                    nc.vector.tensor_scalar(mix[:, i, :], lg_exp[:, i, :], lg_inv[:, i:i + 1], None,
                                            op0=ALU.mult).then_inc(s_mix, 1)
                dve.wait_ge(s_mix, 5)
                for k in range(2):
                    half = slice(64 * k, 64 * k + 64)
                    nc.vector.tensor_copy(mix_col[half], mix[half].rearrange("p i (c k) -> p i c k", k=2)[:, :, :, k])\
                        .then_inc(s_mix, 1)
                dve.wait_ge(s_lame, 1)
                nc.vector.scalar_tensor_tensor(out=lam[:], in0=lam_exp[:, 0, :], scalar=LAMBDA_INIT,
                                               in1=lam_exp[:, 1, :], op0=ALU.add, op1=ALU.subtract)\
                    .then_inc(s_lam, 1)
                dve.wait_ge(rms_in, 16 * P // DV)
                nc.vector.tensor_scalar(wo[:], wo_raw[:], rms_col[:, 0:1], 1.0 - LAMBDA_INIT,
                                        op0=ALU.mult, op1=ALU.mult).then_inc(wo_done, 1)
                def turn(it):
                    dve.wait_ge(rstd_done, it + 1)
                    if past(it):
                        dve.wait_ge(xT_done, 2 * it)
                    for u in range(2):
                        for t in range(TPS):
                            tile = 2 * (2 * it + u) + t
                            last = nc.vector.tensor_scalar(xn1[:, u, t, :], xs[:, tile, :],
                                                           moments[:, tile, 0:1], rstd[:, bass.ds(tile, 1)],
                                                           op0=ALU.subtract, op1=ALU.mult)
                        last.then_inc(xn_done, 1)
                    for u in range(2):
                        b = 2 * it + u
                        for side in range(2):
                            dve.wait_ge(high_done, 2 * b + side + 1)
                            if past(it):
                                dve.wait_ge(low_done, 4 * it)
                            nc.vector.tensor_tensor(
                                qk_rest[:, u, side, :], ps[:, 4 * u + 1 + side, :],
                                qk_parts[:, u, 2 * side:2 * side + 2, :].rearrange("p c t -> p (c t)"),
                                op=ALU.subtract).then_inc(rest_done, 1)
                        for side in range(2):
                            dve.wait_ge(rest_done, 2 * b + side + 1)
                            nc.vector.tensor_copy(
                                qk_parts[:, u, 4 + 2 * side:6 + 2 * side, :].rearrange("p c t -> p (c t)"),
                                qk_rest[:, u, side, :]).then_inc(mid_done, 1)

                repeat(dve, SEQS // 2, turn)
                for i in [0, 1, 2, 3] + list(range(4, FGROUPS, 2)):
                    dve.wait_ge(fT_ps, i + 1)
                    if i < 4:
                        nc.vector.tensor_tensor(
                            a1T[:, 4 * i:4 * i + 4, :], ps[:, i % 2, :].rearrange("p (c d) -> p c d", c=4),
                            mix_col[:, 0, 4 * i:4 * i + 4].unsqueeze(2).to_broadcast([P, 4, P]),
                            op=ALU.mult).then_inc(fT_done, 1)
                    else:
                        if i >= 8:
                            dve.wait_ge(acc_done, i - 3)
                        nc.vector.tensor_scalar(a2T[:, (i - 4) % 4, :], ps[:, i % 2, :],
                                                mix_col[:, 1, i - 4:i - 3], None,
                                                op0=ALU.mult).then_inc(fT_done, 1)
                dve.wait_ge(acc_done, 4)
                nc.vector.tensor_copy(w1[:], ps[:, 2, :]).then_inc(w12_done, 1)

            @block.tensor
            def _(pe):
                pe.wait_ge(consts, 5)
                pe.wait_ge(w_in, 16 * 3)
                def turn(it):
                    for u in range(2):
                        b = 2 * it + u
                        pe.wait_ge(xn_done, b + 1)
                        if past(it):
                            pe.wait_ge(xnT_done, 2 * it)
                        for t in range(TPS):
                            last = nc.tensor.transpose(ps[:, 4 * u, t * P:(t + 1) * P], xn1[:, u, t, :], ident[:])
                        last.then_inc(xT_done, 1)
                    for u in range(2):
                        b = 2 * it + u
                        pe.wait_ge(xnT_done, b + 1)
                        if past(it):
                            pe.wait_ge(rest_done, 4 * it)
                        for side in range(2):
                            for c in range(2):
                                last = nc.tensor.matmul(ps[:, 4 * u + 1 + side, c * SEQ:(c + 1) * SEQ],
                                                        wqkv[:, side, c * P:(c + 1) * P], xnT1[:, u, :],
                                                        start=True, stop=True)
                            last.then_inc(proj_done, 1)
                        if past(it):
                            pe.wait_ge(v_done, 2 * it)
                        for t in range(TPS):
                            last = nc.tensor.matmul(ps[:, 4 * u + 3, t * 256:(t + 1) * 256],
                                                    xnT1[:, u, t * P:(t + 1) * P], wqkv[:, 2, :],
                                                    start=True, stop=True)
                        last.then_inc(proj_done, 1)

                repeat(pe, SEQS // 2, turn)
                pe.wait_ge(rest_done, 2 * SEQS)
                pe.wait_ge(v_done, SEQS)
                pe.wait_ge(small_in, 16 * 11)
                for i in range(4):
                    last = nc.tensor.transpose(ps[:, 4, i * P:(i + 1) * P], wb_raw[:, i, :], ident[:])
                last.then_inc(wbT_ps, 1)

                def factor_transposes(i):
                    if i >= 2:
                        if i - 2 < 4 or i % 2 == 0:
                            pe.wait_ge(fT_done, min(i - 1, 4) + max(0, (i - 2 - 4) // 2 + 1))
                        else:
                            pe.wait_ge(fT_done_act, (i - 2 - 5) // 2 + 1)
                    for j in range(4):
                        if i < 4:
                            c = 4 * i + j
                            src = a1[:, c * P:(c + 1) * P]
                        else:
                            src = a2[:, j, (i - 4) * P:(i - 3) * P]
                        last = nc.tensor.transpose(ps[:, i % 2, j * P:(j + 1) * P], src, ident[:])
                    last.then_inc(fT_ps, 1)

                def factor_products(i):
                    if i < 4 or i % 2 == 0:
                        pe.wait_ge(fT_done, min(i + 1, 4) + max(0, (i - 4) // 2 + 1))
                    else:
                        pe.wait_ge(fT_done_act, (i - 5) // 2 + 1)
                    for j in range(4):
                        if i < 4:
                            c = 4 * i + j
                            last = nc.tensor.matmul(ps[:, 2, :], a1T[:, c, :], b1[:, c, :],
                                                    start=(c == 0), stop=(c == KR - 1))
                        else:
                            c = i - 4
                            last = nc.tensor.matmul(ps[:, 3, j * P:(j + 1) * P], a2T[:, c % 4, j * P:(j + 1) * P],
                                                    b2[:, c, :], start=(c == 0 and j == 0),
                                                    stop=(c == KR - 1), skip_group_check=True)
                    last.then_inc(acc_done, 1)

                for i in range(FGROUPS + 2):
                    if i == 0:
                        pe.wait_ge(factors_in[0], 16)
                    if i == 2:
                        pe.wait_ge(factors_in[1], 16)
                    if i == 4:
                        pe.wait_ge(factors_in[2], 16 * FCH)
                    if i == 6:
                        pe.wait_ge(factors_in[3], 16)
                    if i < FGROUPS:
                        factor_transposes(i)
                    if i >= 2:
                        factor_products(i - 2)

        ones_23 = sem("ones_23")
        vaug_const = sem("vaug_const")
        vaug_done = sem("vaug_done")
        shift_in = [sem(f"shift_in{i}") for i in range(4)]
        scored = sem("scored")
        maxed = sem("maxed")
        maxT_done = sem("maxT_done")
        shift_hi = sem("shift_hi")
        shift_lo = sem("shift_lo")
        scoredT = sem("scoredT")
        exp_done = sem("exp_done")
        masked = sem("masked")
        pv_done = sem("pv_done")
        ot_copied = sem("ot_copied")
        ott_done = sem("ott_done")
        o_copied = sem("o_copied")
        rden_done = sem("rden_done")
        post = sem("post")
        sq_done = sem("sq_done")
        ms_raw = sem("ms_raw")
        ms_done = sem("ms_done")
        normed = sem("normed")
        nT_done = sem("nT_done")
        oT_done = sem("oT_done")
        oproj_done = sem("oproj_done")
        resid_done = sem("resid_done")
        st2_done = sem("st2_done")
        mom2_done = sem("mom2_done")
        rms_pw = sem("rms_pw")

        S_BANK, T_BANK, O_BANK, OT_BANK, M_BANK = 0, 2, 4, 6, 7

        def turns(eng, emit):
            for j in range(SLOTS):
                emit(0, j)
            with eng.Fori(1, UNITS // SLOTS) as it:
                for j in range(SLOTS):
                    emit(it, j)
            for j in range(L_STAT - UPS + 1):
                emit(UNITS // SLOTS, j)

        def unit(it, j, lag):
            return SLOTS * it + j - lag

        def group(it, j, lag):
            return (SLOTS // UPG) * it + (j - lag) // UPG

        def seq(it, j, lag):
            return (SLOTS // UPS) * it + (j - lag) // UPS

        def oprojs_before(it, j):
            return (SLOTS // UPS) * it + (j - L_OPROJ - 1) // UPS + 1

        def shifts_before(it, j):
            return (SLOTS // UPG) * it + (j - L_SHIFT - 1) // UPG + 1

        with nc.Block() as block:
            @block.sync
            def _(sp):
                sp.wait_ge(ones_23, 2)
                load_stack(sp, 2, 2)
                load_stack(sp, 3, 3)

                def store_shift(g, slot):
                    sp.wait_ge(shift_lo, g + 1)
                    for part in range(SHIFT_ROWS):
                        sp.dma_start(q_stack(slot)[SROWS + part:SROWS + part + 1], shift[:, slot % 2, part, :])\
                          .then_inc(shift_in[slot], 16)

                store_shift(0, 0)
                with sp.Fori(0, GROUPS // 4 - 1) as it:
                    for k in range(4):
                        g = 4 * it + k
                        store_shift(g + 1, (k + 1) % 4)
                        sp.wait_ge(scoredT, BANKS_U * UPG * (g + 1))
                        load_stack(sp, 2 * (it + 1) + k // 2, k)
                for g in range(GROUPS - 4, GROUPS - 1):
                    store_shift(g + 1, (g + 1) % 4)

            @block.gpsimd
            def _(pool):
                for started in (post, normed, rms_pw):
                    pool.sem_inc(started, FIRST)
                pair = float(np.array([0x3F803F80], np.uint32).view(np.float32)[0])
                for slot in (2, 3):
                    nc.gpsimd.memset(k_stack(slot).rearrange("p m t -> p (m t)").bitcast(F32),
                                     pair).then_inc(ones_23, 1)
                nc.gpsimd.memset(vaug[:, :, :, :, DV:32], 0.0).then_inc(vaug_const, 1)
                pool.wait_ge(vaug_const, 1)
                nc.gpsimd.memset(vaug[:, :, :, :, DV:DV + 1], 1.0).then_inc(vaug_const, 1)

                def emit(it, j):
                    b = seq(it, j, L_VAUG)
                    if (j - L_VAUG) % UPS == 0 and live(b, SEQS):
                        if past(b - 1):
                            pool.wait_ge(pv_done, UPS * (b - 1))
                        v = (j - L_VAUG) // UPS % 2
                        src = values[:, bass.ds(2 * b, 2), :].rearrange("p t (h d) -> p t h d", h=HEADS)
                        nc.gpsimd.tensor_copy(vaug[:, v, :, :, 0:DV], src).then_inc(vaug_done, 1)
                    n = unit(it, j, L_EXP)
                    if live(n, UNITS):
                        r = (j - L_EXP) % 2
                        for s in range(BANKS_U):
                            pool.wait_ge(exp_done, BANKS_U * n + s + 1)
                            carry_wait(pool, tick_pool)
                            if s < 2:
                                diag = probs[:, r, s, :].rearrange("p (m q) -> p m q", m=2)[:, :, 0:P]
                            else:
                                diag = probs[:, r, s, :].rearrange("p (m q) -> p m q", m=UMAPS)
                            nc.gpsimd.affine_select(out=diag, in_=diag, compare_op=ALU.is_ge, fill=0.0, base=0,
                                                    pattern=[[0, 2 if s < 2 else UMAPS], [1, P]],
                                                    channel_multiplier=-1).then_inc(masked, 1)
                    b = seq(it, j, L_DEN)
                    if (j - L_DEN) % UPS == 0 and live(b, SEQS):
                        v = (j - L_DEN) // UPS % 2
                        num = o_sb[:, v].rearrange("p t (h c) d -> p (t h) c d", c=2)
                        inv = rden.rearrange("p t (h c) -> p (t h) c", c=2)
                        pool.wait_ge(rden_done, b + 1)
                        if past(b):
                            pool.wait_ge(post, FIRST + 4 * b)
                            pool.wait_ge(normed, FIRST + b)
                        nc.gpsimd.tensor_tensor(rden2, rden.rearrange("p t (h c) -> p t h c", c=2)[:, :, :, 1],
                                                lam[:].unsqueeze(1).to_broadcast([P, TPS, HEADS]),
                                                op=ALU.mult).then_inc(post, 1)
                        nc.gpsimd.tensor_tensor(o1.rearrange("p t h d -> p (t h) d"), num[:, :, 0, 0:DV],
                                                inv[:, :, 0:1].to_broadcast([P, TPS * HEADS, DV]),
                                                op=ALU.mult).then_inc(post, 1)
                    b = seq(it, j, L_DIFF)
                    if (j - L_DIFF) % UPS == 0 and live(b, SEQS):
                        v = (j - L_DIFF) // UPS % 2
                        num = o_sb[:, v].rearrange("p t (h c) d -> p (t h) c d", c=2)
                        pool.wait_ge(post, FIRST + 4 * b + 1)
                        nc.gpsimd.tensor_tensor(
                            o2.rearrange("p t h d -> p (t h) d"), num[:, :, 1, 0:DV],
                            rden2.rearrange("p t h -> p (t h)").unsqueeze(2).to_broadcast([P, TPS * HEADS, DV]),
                            op=ALU.mult).then_inc(post, 1)
                        pool.wait_ge(post, FIRST + 4 * b + 3)
                        nc.gpsimd.tensor_tensor(o1, o1, o2, op=ALU.subtract).then_inc(post, 1)
                    b = seq(it, j, L_SQ)
                    if (j - L_SQ) % UPS == 0 and live(b, SEQS):
                        pool.wait_ge(post, FIRST + 4 * b + 4)
                        if past(b):
                            pool.wait_ge(ms_raw, FIRST + b)
                        nc.gpsimd.tensor_tensor(osq, o1, o1, op=ALU.mult).then_inc(sq_done, 1)
                    b = seq(it, j, L_NORM)
                    if (j - L_NORM) % UPS == 0 and live(b, SEQS):
                        pool.wait_ge(ms_done, b + 1)
                        if past(b):
                            pool.wait_ge(normed, FIRST + b)
                        nc.gpsimd.tensor_tensor(mrms, msum, minus_half[:, 0:TPS * HEADS],
                                                op=ALU.pow).then_inc(rms_pw, 1)
                        pool.wait_ge(rms_pw, FIRST + b + 1)
                        if past(b):
                            pool.wait_ge(nT_done, FIRST + b)
                        nc.gpsimd.tensor_tensor(
                            o_n.rearrange("p t h d -> p (t h) d"), o1.rearrange("p t h d -> p (t h) d"),
                            mrms.unsqueeze(2).to_broadcast([P, TPS * HEADS, DV]),
                            op=ALU.mult).then_inc(normed, 1)

                turns(pool, emit)

            @block.scalar
            def _(act):
                def emit(it, j):
                    n = unit(it, j, L_EXP)
                    if live(n, UNITS):
                        r = (j - L_EXP) % 2
                        if past(n - 1):
                            act.wait_ge(pv_done, n - 1)
                        for s in range(BANKS_U):
                            act.wait_ge(scoredT, BANKS_U * n + s + 1)
                            bank = T_BANK + (j - L_EXP + s) % 2
                            nc.scalar.activation(probs[:, r, s, :], ps[:, bank, :], ACT.Exp,
                                                 scale=SCALE).then_inc(exp_done, 1)
                            g = group(it, j, L_SHIFT)
                            if s == 0 and (j - L_SHIFT) % UPG == 0 and live(g, GROUPS):
                                shift_high(it, j)
                    g = group(it, j, L_SHIFT)
                    if not live(n, UNITS) and (j - L_SHIFT) % UPG == 0 and live(g, GROUPS):
                        shift_high(it, j)
                    n = unit(it, j, L_PV)
                    if live(n, UNITS):
                        r = (j - L_PV) % 2
                        act.wait_ge(pv_done, n + 1)
                        if past(n - 1):
                            act.wait_ge(ott_done, n - 1)
                        nc.scalar.copy(ot_sb[:, r, :], ps[:, O_BANK + r, 0:SEQ]).then_inc(ot_copied, 1)
                    b = seq(it, j, L_OPT)
                    if (j - L_OPT) % UPS == 0 and live(b, SEQS):
                        act.wait_ge(nT_done, FIRST + b + 1)
                        nc.scalar.copy(oT.rearrange("p a b c -> p (a b c)"), ps[:, M_BANK, :])\
                            .then_inc(oT_done, 1)

                def shift_high(it, j):
                    g, k = group(it, j, L_SHIFT), (j - L_SHIFT) // UPG
                    act.wait_ge(maxT_done, g + 1)
                    if past(g - 1):
                        act.wait_ge(shift_in[(k - 2) % 4], 32 * (it + (k - 2) // 4 + 1))
                    nc.scalar.activation(shift[:, k % 2, 0, :], ps[0:GMAPS, M_BANK, 0:SEQ], ACT.Copy,
                                         scale=-1.0).then_inc(shift_hi, 1)

                turns(act, emit)

            @block.vector
            def _(dve):
                for started in (ms_raw, resid_done, mom2_done):
                    dve.sem_inc(started, FIRST)

                def emit(it, j):
                    n = unit(it, j, 0)
                    if live(n, UNITS):
                        uu, gs = j % UPG, j // UPG % 2
                        for s in range(BANKS_U):
                            bank = S_BANK + (j + s) % 2
                            dve.wait_ge(scored, BANKS_U * n + s + 1)
                            if s == 0:
                                dst = rowmax[:, gs, 0, UMAPS * uu:UMAPS * uu + UMAPS]
                            else:
                                dst = rowmax[:, gs, 1, UMAPS * uu + 2 * s - 2:UMAPS * uu + 2 * s]
                            nc.vector.tensor_reduce(
                                out=dst, in_=ps[:, bank, :].rearrange("p (m k) -> p m k", m=UMAPS if s == 0 else 2),
                                axis=AX, op=ALU.max).then_inc(maxed, 1)
                    g = group(it, j, L_SHIFT)
                    if (j - L_SHIFT) % UPG == 0 and live(g, GROUPS):
                        k = (j - L_SHIFT) // UPG
                        dve.wait_ge(shift_hi, g + 1)
                        nc.vector.scalar_tensor_tensor(
                            out=shift[:, k % 2, 1, :], in0=ps[0:GMAPS, M_BANK, 0:SEQ], scalar=-1.0,
                            in1=shift[:, k % 2, 0, :], op0=ALU.mult, op1=ALU.subtract).then_inc(shift_lo, 1)
                    n = unit(it, j, L_OT)
                    if live(n, UNITS):
                        u, v = (j - L_OT) % UPS, (j - L_OT) // UPS % 2
                        dve.wait_ge(ott_done, n + 1)
                        src = ps[:, OT_BANK, 0:TPS * P].rearrange("p (t m d) -> p t m d", t=TPS, m=UMAPS)
                        nc.vector.tensor_copy(o_sb[:, v, :, UMAPS * u:UMAPS * u + UMAPS, :],
                                              src[:, :, :, 0:DV + 1]).then_inc(o_copied, 1)
                    b = seq(it, j, L_DEN)
                    if (j - L_DEN) % UPS == 0 and live(b, SEQS):
                        v = (j - L_DEN) // UPS % 2
                        dve.wait_ge(o_copied, UPS * (b + 1))
                        if past(b):
                            dve.wait_ge(post, FIRST + 4 * b)
                        nc.vector.reciprocal(rden, o_sb[:, v, :, :, DV]).then_inc(rden_done, 1)
                    b = seq(it, j, L_MS)
                    if (j - L_MS) % UPS == 0 and live(b, SEQS):
                        dve.wait_ge(sq_done, b + 1)
                        if past(b):
                            dve.wait_ge(rms_pw, FIRST + b)
                        nc.vector.tensor_reduce(out=msum, in_=osq.rearrange("p t h d -> p (t h) d"), axis=AX,
                                                op=ALU.add).then_inc(ms_raw, 1)
                        dve.wait_ge(ms_raw, FIRST + b + 1)
                        nc.vector.tensor_scalar(msum, msum, 1.0 / DV, RMS_EPS, op0=ALU.mult,
                                                op1=ALU.add).then_inc(ms_done, 1)
                    b = seq(it, j, L_OPROJ)
                    if (j - L_OPROJ) % UPS == 0 and live(b, SEQS):
                        dve.wait_ge(oproj_done, b + 1)
                        x2 = xs[:, bass.ds(2 * b, 2), :].rearrange("p t d -> p (t d)")
                        nc.vector.tensor_tensor(x2, ps[:, M_BANK, 0:TPS * D], x2, op=ALU.add)\
                            .then_inc(resid_done, 1)
                    b = seq(it, j, L_STAT)
                    if (j - L_STAT) % UPS == 0 and live(b, SEQS):
                        dve.wait_ge(resid_done, FIRST + b + 1)
                        token_moments(dve, tick_dve, TPS * b, TPS, st2_done, mom2_done, b, FIRST)

                turns(dve, emit)

            @block.tensor
            def _(pe):
                pe.sem_inc(nT_done, FIRST)

                def score_bank(it, j, s):
                    n = unit(it, j, 0)
                    slot, m0 = j // UPG % 4, UMAPS * (j % UPG)
                    q, k = q_stack(slot), k_stack(slot)
                    bank = ps[:, S_BANK + (j + s) % 2, :]
                    if s == 0 and j % UPG == 0:
                        pe.wait_ge(stack_in[slot], 2 * TERMS * 16 * (it + 1))
                    if past(BANKS_U * n + s - 1):
                        pe.wait_ge(maxed, BANKS_U * n + s - 1)
                    if s == 0:
                        for m in range(UMAPS):
                            nc.tensor.matmul(bank[:, m * P:(m + 1) * P], q[0:SROWS, m0 + m, 0:P],
                                             k[0:SROWS, m0 + m, 0:P], start=(m == 0), stop=False,
                                             skip_group_check=True)
                        nc.tensor.matmul(bank, ident_bf[:], future_bf[:].rearrange("p m k -> p (m k)"),
                                         start=False, stop=True, skip_group_check=True).then_inc(scored, 1)
                    else:
                        for m in range(2):
                            nc.tensor.matmul(bank[:, m * SEQ:(m + 1) * SEQ], q[0:SROWS, m0 + 2 * s - 2 + m, P:SEQ],
                                             k[0:SROWS, m0 + 2 * s - 2 + m, :], start=(m == 0), stop=False,
                                             skip_group_check=True)
                        nc.tensor.matmul(bank.rearrange("p (m k) -> p m k", m=2)[:, :, P:SEQ], ident_bf[:],
                                         future_bf[:, 0:2, :], start=False, stop=True,
                                         skip_group_check=True).then_inc(scored, 1)

                def shifted_bank(it, j, s):
                    n = unit(it, j, L_EXP)
                    jj = j - L_EXP
                    slot, m0 = jj // UPG % 4, UMAPS * (jj % UPG)
                    q, k = q_stack(slot), k_stack(slot)
                    bank = ps[:, T_BANK + (jj + s) % 2, :]
                    if s == 0 and jj % UPG == 0:
                        pe.wait_ge(shift_in[slot], 32 * (it + jj // SLOTS + 1))
                    if past(BANKS_U * n + s - 1):
                        pe.wait_ge(exp_done, BANKS_U * n + s - 1)
                    if s < 2:
                        for m in range(2):
                            last = nc.tensor.matmul(bank[:, m * SEQ:(m + 1) * SEQ], k[0:XROWS, m0 + 2 * s + m, 0:P],
                                                    q[0:XROWS, m0 + 2 * s + m, :], start=True, stop=True)
                    else:
                        for m in range(UMAPS):
                            last = nc.tensor.matmul(bank[:, m * P:(m + 1) * P], k[0:XROWS, m0 + m, P:SEQ],
                                                    q[0:XROWS, m0 + m, P:SEQ], start=True, stop=True)
                    last.then_inc(scoredT, 1)

                def weigh_values(it, j):
                    n = unit(it, j, L_PV)
                    jj = j - L_PV
                    r, v = jj % 2, jj // UPS % 2
                    pe.wait_ge(masked, BANKS_U * (n + 1))
                    if jj % UPS == 0:
                        pe.wait_ge(vaug_done, seq(it, j, L_PV) + 1)
                    if past(n - 1):
                        pe.wait_ge(ot_copied, n - 1)
                    for m in range(UMAPS):
                        head = 2 * (jj % UPS) + m // 2
                        nc.tensor.matmul(ps[32 * m:32 * m + 32, O_BANK + r, 0:SEQ], vaug[:, v, 0, head, :],
                                         probs[:, r, m // 2, m % 2 * SEQ:m % 2 * SEQ + SEQ],
                                         start=True, stop=False, skip_group_check=True)
                    for m in range(UMAPS):
                        head = 2 * (jj % UPS) + m // 2
                        last = nc.tensor.matmul(ps[32 * m:32 * m + 32, O_BANK + r, P:SEQ], vaug[:, v, 1, head, :],
                                                probs[:, r, 2, m * P:(m + 1) * P],
                                                start=False, stop=True, skip_group_check=True)
                    last.then_inc(pv_done, 1)

                def emit(it, j):
                    for s in range(BANKS_U):
                        if live(unit(it, j, 0), UNITS):
                            score_bank(it, j, s)
                        if live(unit(it, j, L_EXP), UNITS):
                            shifted_bank(it, j, s)
                        g = group(it, j, L_SHIFT)
                        if s == 0 and (j - L_SHIFT) % UPG == 0 and live(g, GROUPS):
                            k = (j - L_SHIFT) // UPG
                            pe.wait_ge(maxed, BANKS_U * UPG * (g + 1))
                            if past(shifts_before(it, j)):
                                pe.wait_ge(shift_lo, shifts_before(it, j))
                            if past(oprojs_before(it, j)):
                                pe.wait_ge(resid_done, FIRST + oprojs_before(it, j))
                            for t in range(TPS):
                                last = nc.tensor.transpose(ps[0:GMAPS, M_BANK, t * P:(t + 1) * P],
                                                           rowmax[:, k % 2, t, :], ident[:])
                            last.then_inc(maxT_done, 1)
                    if live(unit(it, j, L_PV), UNITS):
                        weigh_values(it, j)
                    n = unit(it, j, L_OT)
                    if live(n, UNITS):
                        pe.wait_ge(ot_copied, n + 1)
                        if past(n):
                            pe.wait_ge(o_copied, n)
                        for t in range(TPS):
                            last = nc.tensor.transpose(ps[:, OT_BANK, t * P:(t + 1) * P],
                                                       ot_sb[:, (j - L_OT) % 2, t * P:(t + 1) * P], ident[:])
                        last.then_inc(ott_done, 1)
                    b = seq(it, j, L_OPT)
                    if (j - L_OPT) % UPS == 0 and live(b, SEQS):
                        pe.wait_ge(normed, FIRST + b + 1)
                        if past(shifts_before(it, j)):
                            pe.wait_ge(shift_lo, min(shifts_before(it, j), GROUPS)
                                       if isinstance(it, int) else shifts_before(it, j))
                        if past(b):
                            pe.wait_ge(resid_done, FIRST + b)
                        flat = o_n.rearrange("p t h d -> p t (h d)")
                        for t in range(TPS):
                            for c in range(2):
                                last = nc.tensor.transpose(ps[:, M_BANK, (2 * t + c) * P:(2 * t + c + 1) * P],
                                                           flat[:, t, c * P:(c + 1) * P], ident[:])
                        last.then_inc(nT_done, 1)
                    b = seq(it, j, L_OPROJ)
                    if (j - L_OPROJ) % UPS == 0 and live(b, SEQS):
                        pe.wait_ge(oT_done, b + 1)
                        for t in range(TPS):
                            for c in range(2):
                                last = nc.tensor.matmul(ps[:, M_BANK, t * D:(t + 1) * D], oT[:, t, c, :],
                                                        wo[:, c, :], start=(c == 0), stop=(c == 1))
                        last.then_inc(oproj_done, 1)

                pe.wait_ge(vaug_const, 2)
                turns(pe, emit)

        def feed_forward(tag, store):
            BT = 4
            BLOCKS = TILES // BT
            at = 0
            hT, at = carve(at, (2, FCH, BT * P))
            xn, at = carve(at, (2, BT, D))
            xnT, at = carve(at, (2, BT * P))
            f_veps, f_rstd = sem(f"{tag}_veps"), sem(f"{tag}_rstd")
            f_xn, f_xT, f_xnT = sem(f"{tag}_xn"), sem(f"{tag}_xT"), sem(f"{tag}_xnT")
            f_up, f_gelu, f_down = sem(f"{tag}_up"), sem(f"{tag}_gelu"), sem(f"{tag}_down")
            f_res, f_st, f_mom = sem(f"{tag}_res"), sem(f"{tag}_st"), sem(f"{tag}_mom")
            stored = sem(f"{tag}_stored")

            with nc.Block() as block:
                @block.gpsimd
                def _(pool):
                    nc.gpsimd.tensor_scalar(veps[:], moments[:, :, 1], LN_EPS, None, op0=ALU.add)\
                        .then_inc(f_veps, 1)
                    pool.wait_ge(f_veps, 1)
                    nc.gpsimd.tensor_tensor(rstd[:], veps[:], minus_half[:, 0:TILES], op=ALU.pow)\
                        .then_inc(f_rstd, 1)

                @block.vector
                def _(dve):
                    dve.wait_ge(f_rstd, 1)
                    def turn(it):
                        if past(it):
                            dve.wait_ge(f_xT, 2 * it)
                        for u in range(2):
                            for t in range(BT):
                                tile = BT * (2 * it + u) + t
                                last = nc.vector.tensor_scalar(xn[:, u, t, :], xs[:, tile, :],
                                                               moments[:, tile, 0:1], rstd[:, bass.ds(tile, 1)],
                                                               op0=ALU.subtract, op1=ALU.mult)
                            last.then_inc(f_xn, 1)
                        for u in range(2):
                            k = 2 * it + u
                            x4 = xs[:, bass.ds(BT * k, BT), :].rearrange("p t d -> p (t d)")
                            dve.wait_ge(f_down, k + 1)
                            nc.vector.tensor_tensor(x4, ps[:, 6 + u, :], x4, op=ALU.add).then_inc(f_res, 1)
                            if not store:
                                dve.wait_ge(f_res, k + 1)
                                token_moments(dve, tick_dve, BT * k, BT, f_st, f_mom, k)

                    repeat(dve, BLOCKS // 2, turn)

                @block.scalar
                def _(act):
                    def turn(it):
                        for u in range(2):
                            act.wait_ge(f_xT, 2 * it + u + 1)
                            nc.scalar.copy(xnT[:, u, :], ps[:, u, :]).then_inc(f_xnT, 1)
                        for u in range(2):
                            k = 2 * it + u
                            if past(it):
                                act.wait_ge(f_down, 2 * it)
                            for c in range(FCH):
                                act.wait_ge(f_up, FCH * k + c + 1)
                                nc.scalar.activation(hT[:, u, c, :], ps[:, 2 + c, :],
                                                     ACT.Gelu_apprx_tanh).then_inc(f_gelu, 1)

                    repeat(act, BLOCKS // 2, turn)

                @block.tensor
                def _(pe):
                    def turn(it):
                        for u in range(2):
                            pe.wait_ge(f_xn, 2 * it + u + 1)
                            if past(it):
                                pe.wait_ge(f_xnT, 2 * it)
                            for t in range(BT):
                                last = nc.tensor.transpose(ps[:, u, t * P:(t + 1) * P], xn[:, u, t, :], ident[:])
                            last.then_inc(f_xT, 1)
                        for u in range(2):
                            k = 2 * it + u
                            pe.wait_ge(f_xnT, k + 1)
                            for c in range(FCH):
                                if u or past(it):
                                    pe.wait_ge(f_gelu, FCH * (k - 1) + c + 1)
                                nc.tensor.matmul(ps[:, 2 + c, :], w1[:, c * P:(c + 1) * P], xnT[:, u, :],
                                                 start=True, stop=True).then_inc(f_up, 1)
                        for u in range(2):
                            k = 2 * it + u
                            pe.wait_ge(f_gelu, FCH * (k + 1))
                            if past(it):
                                pe.wait_ge(f_res, 2 * it)
                            for t in range(BT):
                                for c in range(FCH):
                                    last = nc.tensor.matmul(ps[:, 6 + u, t * D:(t + 1) * D],
                                                            hT[:, u, c, t * P:(t + 1) * P], w2[:, c, :],
                                                            start=(c == 0), stop=(c == FCH - 1))
                            last.then_inc(f_down, 1)

                    repeat(pe, BLOCKS // 2, turn)

                if store:
                    @block.sync
                    def _(sp):
                        with sp.Fori(0, BLOCKS) as k:
                            sp.wait_ge(f_res, k + 1)
                            sp.dma_start(out_tiles[:, bass.ds(BT * k, BT), :], xs[:, bass.ds(BT * k, BT), :])\
                              .then_inc(stored, 16)
                        sp.wait_ge(stored, 16 * BLOCKS)

        def linear_attend():
            E1 = DH + 1
            EG = 3
            at = 0
            xn, at = carve(at, (2, TPS, D))
            xnT, at = carve(at, (2, TPS * P))
            low, at = carve(at, (2, TPS, 2 * D))
            phi, at = carve(at, (2, TPS, 2 * D))
            vb, at = carve(at, (2, TPS, D))
            kv, at = carve(at, (2, TPS, E1, D))
            prod, at = carve(at, (2, E1, D))
            nd, at = carve(at, (2, TPS, E1, HEADS))
            inv, at = carve(at, (2, TPS, HEADS))
            o, at = carve(at, (2, TPS, D))
            oT_l, at = carve(at, (2, TPS * P))
            names = ("veps rstd xn xT xnT qkv low exp phi v kv pre prod nd inv oraw o oT oTs out res st mom").split()
            L = {k: sem(f"l_{k}") for k in names}
            MID, BACK = 2, 3

            def slots(eng, emit):
                for m in range(4):
                    emit(m // 2, m % 2)
                with eng.Fori(2, SEQS // 2) as it:
                    for u in range(2):
                        emit(it, u)
                for m in range(BACK):
                    emit(SEQS // 2 + m // 2, m % 2)

            with nc.Block() as block:
                @block.gpsimd
                def _(pool):
                    nc.gpsimd.tensor_scalar(veps[:], moments[:, :, 1], LN_EPS, None, op0=ALU.add)\
                        .then_inc(L["veps"], 1)
                    pool.wait_ge(L["veps"], 1)
                    nc.gpsimd.tensor_tensor(rstd[:], veps[:], minus_half[:, 0:TILES], op=ALU.pow)\
                        .then_inc(L["rstd"], 1)

                    def emit(it, u):
                        b = 2 * it + u
                        if live(b, SEQS):
                            for t in range(TPS):
                                pool.wait_ge(L["phi"], TPS * b + t + 1)
                                pool.wait_ge(L["v"], TPS * b + t + 1)
                                if past(b - 1):
                                    pool.wait_ge(L["pre"], 2 * EG * (b - 1))
                                kh = phi[:, u, t, D:2 * D].rearrange("p (h d) -> p h d", d=DH)
                                vh = vb[:, u, t, :].rearrange("p (h e) -> p e h", e=DH)
                                nc.gpsimd.tensor_tensor(
                                    kv[:, u, t, 0:DH, :].rearrange("p e (h d) -> p e h d", d=DH),
                                    kh.unsqueeze(1).to_broadcast([P, DH, HEADS, DH]),
                                    vh.unsqueeze(3).to_broadcast([P, DH, HEADS, DH]), op=ALU.mult)\
                                    .then_inc(L["kv"], 1)
                                nc.gpsimd.tensor_copy(kv[:, u, t, DH, :], phi[:, u, t, D:2 * D])\
                                    .then_inc(L["kv"], 1)
                        b = 2 * it + u - MID
                        if live(b, SEQS):
                            pool.wait_ge(L["inv"], b + 1)
                            if past(b - 1):
                                pool.wait_ge(L["oT"], b - 1)
                            for t in range(TPS):
                                last = nc.gpsimd.tensor_tensor(
                                    o[:, u, t, :].rearrange("p (h e) -> p e h", e=DH), nd[:, u, t, 0:DH, :],
                                    inv[:, u, t, :].unsqueeze(1).to_broadcast([P, DH, HEADS]), op=ALU.mult)
                            last.then_inc(L["oraw"], 1)
                            pool.wait_ge(L["oraw"], b + 1)
                            carry_wait(pool, tick_pool)
                            nc.gpsimd.tensor_scalar(o[:, u], o[:, u], LIN_EPS, None, op0=ALU.add)\
                                .then_inc(L["o"], 1)

                    slots(pool, emit)

                @block.scalar
                def _(act):
                    def emit(it, u):
                        b = 2 * it + u
                        if live(b, SEQS):
                            act.wait_ge(L["xT"], b + 1)
                            if past(b - 1):
                                act.wait_ge(L["qkv"], TPS * (b - 1))
                            nc.scalar.copy(xnT[:, u, :], ps[:, 0, 0:TPS * P]).then_inc(L["xnT"], 1)
                            for t in range(TPS):
                                act.wait_ge(L["qkv"], TPS * b + t + 1)
                                if past(b - 1):
                                    act.wait_ge(L["kv"], 2 * TPS * (b - 1))
                                act.wait_ge(L["low"], TPS * b + t + 1)
                                nc.scalar.copy(vb[:, u, t, :], ps[:, 1 + t, 2 * D:3 * D]).then_inc(L["v"], 1)
                                nc.scalar.activation(low[:, u, t, :], low[:, u, t, :], ACT.Exp)\
                                    .then_inc(L["exp"], 1)
                        b = 2 * it + u - BACK
                        if live(b, SEQS):
                            act.wait_ge(L["oT"], b + 1)
                            if past(b - 1):
                                act.wait_ge(L["out"], FIRST + b - 1)
                            nc.scalar.copy(oT_l[:, (u - BACK) % 2, :], ps[:, 7, 0:TPS * P]).then_inc(L["oTs"], 1)

                    slots(act, emit)

                @block.vector
                def _(dve):
                    dve.wait_ge(L["rstd"], 1)

                    def emit(it, u):
                        b = 2 * it + u
                        if live(b, SEQS):
                            if past(b - 1):
                                dve.wait_ge(L["xT"], b - 1)
                            for t in range(TPS):
                                tile = TPS * b + t
                                last = nc.vector.tensor_scalar(xn[:, u, t, :], xs[:, tile, :],
                                                               moments[:, tile, 0:1], rstd[:, bass.ds(tile, 1)],
                                                               op0=ALU.subtract, op1=ALU.mult)
                            last.then_inc(L["xn"], 1)
                        b = 2 * it + u - MID
                        if live(b, SEQS):
                            for t in range(TPS):
                                qb = phi[:, u, t, 0:D].unsqueeze(1).to_broadcast([P, EG, D])
                                for e in range(EG):
                                    i = EG * t + e
                                    dve.wait_ge(L["pre"], 2 * EG * b + i + 1)
                                    if past(TPS * b + t - 1):
                                        dve.wait_ge(L["nd"], TPS * b + t - 1)
                                    nc.vector.tensor_tensor(
                                        prod[:, t, EG * e:EG * e + EG, :],
                                        ps[:, 3 + (2 * EG * u + i) % 4, 0:EG * D].rearrange("p (e d) -> p e d", e=EG),
                                        qb, op=ALU.mult).then_inc(L["prod"], 1)
                            for t in range(TPS):
                                dve.wait_ge(L["prod"], 2 * EG * b + EG * (t + 1))
                                if past(b - 1):
                                    dve.wait_ge(L["oraw"], b - 1)
                                nc.vector.tensor_reduce(
                                    out=nd[:, u, t].rearrange("p e h -> p (e h)"),
                                    in_=prod[:, t].rearrange("p e (h d) -> p (e h) d", d=DH), axis=AX,
                                    op=ALU.add).then_inc(L["nd"], 1)
                            dve.wait_ge(L["nd"], TPS * (b + 1))
                            nc.vector.reciprocal(inv[:, u], nd[:, u, :, DH, :]).then_inc(L["inv"], 1)
                        b = 2 * it + u
                        if live(b, SEQS):
                            for t in range(TPS):
                                dve.wait_ge(L["qkv"], TPS * b + t + 1)
                                nc.vector.tensor_scalar(low[:, u, t, :], ps[:, 1 + t, 0:2 * D], 0.0, None,
                                                        op0=ALU.min).then_inc(L["low"], 1)
                            for t in range(TPS):
                                dve.wait_ge(L["exp"], TPS * b + t + 1)
                                if past(b - 1):
                                    dve.wait_ge(L["kv"], 2 * TPS * (b - 1))
                                nc.vector.scalar_tensor_tensor(
                                    out=phi[:, u, t, :], in0=ps[:, 1 + t, 0:2 * D], scalar=0.0,
                                    in1=low[:, u, t, :], op0=ALU.max, op1=ALU.add).then_inc(L["phi"], 1)
                        b = 2 * it + u - BACK
                        if live(b, SEQS):
                            dve.wait_ge(L["out"], FIRST + b + 1)
                            x2 = xs[:, bass.ds(2 * b, 2), :].rearrange("p t d -> p (t d)")
                            nc.vector.tensor_tensor(x2, ps[:, 7, 256:256 + TPS * D], x2, op=ALU.add)\
                                .then_inc(L["res"], 1)
                            dve.wait_ge(L["res"], b + 1)
                            token_moments(dve, tick_dve, TPS * b, TPS, L["st"], L["mom"], b)

                    slots(dve, emit)

                @block.tensor
                def _(pe):
                    pe.sem_inc(L["out"], FIRST)

                    def emit(it, u):
                        b = 2 * it + u
                        if live(b, SEQS):
                            pe.wait_ge(L["xn"], b + 1)
                            if past(b):
                                pe.wait_ge(L["xnT"], b)
                            for t in range(TPS):
                                last = nc.tensor.transpose(ps[:, 0, t * P:(t + 1) * P], xn[:, u, t, :], ident[:])
                            last.then_inc(L["xT"], 1)
                        c = 2 * it + u - MID
                        for i in range(2 * EG):
                            if i == 2 and live(b, SEQS):
                                for t in range(TPS):
                                    pe.wait_ge(L["xnT"], b + 1)
                                    if past(b):
                                        pe.wait_ge(L["phi"], TPS * b)
                                    nc.tensor.matmul(ps[:, 1 + t, 0:3 * D], xnT[:, u, t * P:(t + 1) * P],
                                                     wbT[:, 0:3, :].rearrange("p a b -> p (a b)"),
                                                     start=True, stop=True).then_inc(L["qkv"], 1)
                            if live(c, SEQS):
                                t, e = i // EG, i % EG
                                pe.wait_ge(L["kv"], 2 * TPS * c + 2 * (t + 1))
                                if past(2 * EG * c + i - 3):
                                    pe.wait_ge(L["prod"], 2 * EG * c + i - 3)
                                bank = ps[:, 3 + (2 * EG * u + i) % 4, 0:EG * D]
                                rows = kv[:, u, t, EG * e:EG * e + EG, :].rearrange("p e d -> p (e d)")
                                last = nc.tensor.matmul(bank, upto[:], rows, start=True, stop=(t == 0))
                                if t == 1:
                                    rows = kv[:, u, 0, EG * e:EG * e + EG, :].rearrange("p e d -> p (e d)")
                                    last = nc.tensor.matmul(bank, ones[:], rows, start=False, stop=True)
                                last.then_inc(L["pre"], 1)
                        b = 2 * it + u - BACK
                        if live(b, SEQS):
                            w = (u - BACK) % 2
                            pe.wait_ge(L["o"], b + 1)
                            if past(b):
                                pe.wait_ge(L["res"], b)
                            for t in range(TPS):
                                last = nc.tensor.transpose(ps[:, 7, t * P:(t + 1) * P], o[:, w, t, :], ident[:])
                            last.then_inc(L["oT"], 1)
                            pe.wait_ge(L["oTs"], b + 1)
                            for t in range(TPS):
                                last = nc.tensor.matmul(ps[:, 7, 256 + t * D:256 + (t + 1) * D],
                                                        oT_l[:, w, t * P:(t + 1) * P], wbT[:, 3, :],
                                                        start=True, stop=True)
                            last.then_inc(L["out"], 1)

                    slots(pe, emit)

        feed_forward("f1", False)
        linear_attend()
        feed_forward("f2", True)


_INS = ['L0_attn_a_X', 'L0_attn_a_Wq', 'L0_attn_a_Wk', 'L0_attn_a_Wv', 'L0_attn_a_Wo',
        'L0_attn_a_lambda_q1', 'L0_attn_a_lambda_k1', 'L0_attn_a_lambda_q2', 'L0_attn_a_lambda_k2',
        'L0_attn_a_rms_scale', 'L0_attn_b_Wq', 'L0_attn_b_Wk', 'L0_attn_b_Wv', 'L0_attn_b_Wo',
        'L0_ffn_fc1_A', 'L0_ffn_fc1_B', 'L0_ffn_fc2_A', 'L0_ffn_fc2_B', 'L0_ffn_fc1_logits',
        'L0_ffn_fc2_logits']
_OUTS = [((SEQS, SEQ, D), 'float32')]


def kernel(**inputs):
    import numpy as _np
    import concourse.bacc as _bacc
    from concourse import mybir as _mybir
    from concourse.bass_utils import run_bass_kernel_spmd as _run

    nc = _bacc.Bacc("TRN2", target_bir_lowering=False, num_devices=1)
    arrays, args = {}, []
    for name in _INS:
        a = _np.ascontiguousarray(inputs[name])
        arrays[f"in_{name}_dram"] = a
        args.append(nc.dram_tensor(f"in_{name}_dram", a.shape, _mybir.dt.from_np(a.dtype), kind="ExternalInput").ap())
    for i, (shape, dtype) in enumerate(_OUTS):
        dt = _mybir.dt.from_np(_np.dtype(dtype))
        args.append(nc.dram_tensor(f"out_{i}_dram", shape, dt, kind="ExternalOutput").ap())
    hybrid_kernel(nc, *args)
    r = _run(nc, [arrays], core_ids=[0])
    return r.results[0]["out_0_dram"]
```

```python
from contextlib import ExitStack

import numpy as np

import concourse.bass as bass
from concourse import mybir

F32 = mybir.dt.float32
BF16 = mybir.dt.bfloat16
I32 = mybir.dt.int32
ALU = mybir.AluOpType
ACT = mybir.ActivationFunctionType
AX = mybir.AxisListType.X

P = 128
SEQS, SEQ, D = 8, 256, 128
TILES = SEQS * SEQ // P
FIRST = 1
TPS = SEQ // P
HEADS, DH = 16, 8
DV = 2 * DH
MAPS = 2 * HEADS
F = 512
FCH = F // P
PRIMS, R = 32, 64
KR = PRIMS * R // P
LN_EPS = 1e-5
RMS_EPS = 1e-5
LIN_EPS = 1e-12
LAMBDA_INIT = 0.8
SCALE = float(1.0 / np.sqrt(DH))
NEG = -1e30

Q_PART = (0, 0, 1, 1, 0, 2)
K_PART = (0, 1, 0, 1, 2, 0)
TERMS = len(Q_PART)
SHIFT_ROWS = 2
SROWS = 96
XROWS = P

GMAPS = 16
GROUPS = SEQS * MAPS // GMAPS
UMAPS = 4
UNITS = SEQS * MAPS // UMAPS
UPG = GMAPS // UMAPS
UPS = MAPS // UMAPS
SLOTS = 16
BANKS_U = 3
L_SHIFT, L_EXP, L_PV, L_OT, L_VAUG = 4, 6, 7, 8, 5
L_DEN, L_DIFF, L_SQ, L_MS, L_NORM, L_OPT, L_OPROJ, L_STAT = 15, 16, 17, 18, 21, 22, 23, 23
ROOT_SEED = 0x5F3759DF
ROOT_STEPS, ROOT_FIRST = 11, 2
POINTS = 4


def live(index, count):
    return not isinstance(index, int) or 0 <= index < count


def past(value):
    return not isinstance(value, int) or value > 0


def repeat(eng, turns, turn):
    turn(0)
    with eng.Fori(1, turns) as it:
        turn(it)


def hybrid_kernel(nc, X, Wq, Wk, Wv, Wo, lq1, lk1, lq2, lk2, rms_scale, bWq, bWk, bWv, bWo,
                  fc1_A, fc1_B, fc2_A, fc2_B, fc1_logits, fc2_logits, out):
    x_tiles = X.rearrange("b (t p) d -> p (b t) d", p=P)
    out_tiles = out.rearrange("b (t p) d -> p (b t) d", p=P)
    parts_dram = nc.dram_tensor("qk_parts", (SEQS, 12, P, SEQ), BF16, kind="Internal").ap()

    with ExitStack() as ctx:
        def sb(name, shape, dt=F32):
            return ctx.enter_context(nc.sbuf_tensor(name, shape, dt))

        def sem(name):
            return ctx.enter_context(nc.semaphore(name))

        ps = ctx.enter_context(nc.psum_tensor("ps", [P, 8, 512], F32))

        xs = sb("xs", [P, TILES, D])
        moments = sb("moments", [P, TILES, 2])
        stats = sb("stats", [P, TILES, 6])
        moments_new = sb("moments_new", [P, 4, 2])
        rstd = sb("rstd", [P, TILES])
        std = sb("std", [P, TILES])
        eps = sb("eps", [P, 1])
        ident = sb("ident", [P, P])
        ident_bf = sb("ident_bf", [P, P], BF16)
        future_bf = sb("future_bf", [P, UMAPS, P], BF16)
        upto = sb("upto", [P, P])
        ones = sb("ones", [P, P])
        wqkv = sb("wqkv", [P, 3, 2 * D])
        wo_raw = sb("wo_raw", [P, 2, D])
        wo = sb("wo", [P, 2, D])
        rms_col = sb("rms_col", [P, 1])
        wb_raw = sb("wb_raw", [P, 4, D])
        wbT = sb("wbT", [P, 4, D])
        lam_in = sb("lam_in", [P, 4, HEADS * DH])
        lam_prod = sb("lam_prod", [P, 2, HEADS * DH])
        lam_sum = sb("lam_sum", [P, 2, HEADS])
        lam_exp = sb("lam_exp", [P, 2, HEADS])
        lam = sb("lam", [P, HEADS])
        logits = sb("logits", [P, 2, PRIMS])
        lg_negmax = sb("lg_negmax", [P, 2])
        lg_exp = sb("lg_exp", [P, 2, PRIMS])
        lg_sum = sb("lg_sum", [P, 2])
        lg_inv = sb("lg_inv", [P, 2])
        mix = sb("mix", [P, 2, PRIMS])
        mix_col = sb("mix_col", [P, 2, KR])
        w1 = sb("w1", [P, F])
        w2 = sb("w2", [P, FCH, D])
        values = sb("values", [P, TILES, HEADS, DV + 1])
        xn1 = sb("xn1", [P, 2, TPS, D])
        xnT1 = sb("xnT1", [P, 2, SEQ])
        qk_parts = sb("qk_parts_sb", [P, 2, 12, SEQ], BF16)
        qk_rest = sb("qk_rest", [P, 2, 2, 512])
        a1T = sb("a1T", [P, KR, P])
        a2T = sb("a2T", [P, 4, F])
        stack01 = sb("stack01", [P, 2, 2, GMAPS, SEQ], BF16)
        arena = sb("arena", [P, 20480])

        def carve(at, shape, dt=F32, parts=P):
            n = int(np.prod(shape))
            words = n if dt == F32 else n // 2
            ap = arena[0:parts, at:at + words]
            if dt != F32:
                ap = ap.bitcast(dt)
            names = "abcdef"[:len(shape)]
            if len(shape) > 1:
                ap = ap.rearrange(f"p ({' '.join(names)}) -> p {' '.join(names)}",
                                  **{k: s for k, s in zip(names[1:], shape[1:])})
            return ap, at + words

        a1, at = carve(0, (PRIMS * R,))
        b1, at = carve(at, (KR, F))
        a2, at = carve(at, (FCH, PRIMS * R))
        b2, at = carve(at, (KR, D))

        stack23, at = carve(0, (2, 2, GMAPS, SEQ), BF16)
        vaug, at = carve(at, (2, TPS, HEADS, DV + 1))
        probs, at = carve(at, (2, BANKS_U, 512))
        ot_sb, at = carve(at, (2, SEQ))
        o_sb, at = carve(at, (2, TPS, MAPS, DV + 1))
        rowmax, at = carve(at, (2, TPS, GMAPS))
        shift, at = carve(at, (2, SHIFT_ROWS, SEQ), BF16, GMAPS)
        rden, at = carve(at, (TPS, MAPS))
        rden2, at = carve(at, (TPS, HEADS))
        o1, at = carve(at, (TPS, HEADS, DV))
        o2, at = carve(at, (TPS, HEADS, DV))
        osq, at = carve(at, (TPS, HEADS, DV))
        o_n, at = carve(at, (TPS, HEADS, DV))
        msum, at = carve(at, (TPS * HEADS,))
        mrms, at = carve(at, (TPS * HEADS,))
        root_half, at = carve(at, (TPS * HEADS,))
        root_tmp, at = carve(at, (TPS * HEADS,))
        oT, at = carve(at, (TPS, 2, P))

        def q_stack(slot):
            return stack01[:, slot, 0] if slot < 2 else stack23[:, slot - 2, 0]

        def k_stack(slot):
            return stack01[:, slot, 1] if slot < 2 else stack23[:, slot - 2, 1]

        def fill_stacks(pool, slot, filled, before):
            pair = float(np.array([0x3F803F80], np.uint32).view(np.float32)[0])
            q, k = (s.rearrange("p m t -> p (m t)").bitcast(F32) for s in (q_stack(slot), k_stack(slot)))
            nc.gpsimd.memset(q, 0.0).then_inc(filled, 1)
            nc.gpsimd.memset(k, pair).then_inc(filled, 1)
            pool.wait_ge(filled, before + 2)
            nc.gpsimd.memset(k[0:SROWS], 0.0).then_inc(filled, 1)

        x_in = [sem(f"x_in{i}") for i in range(4)]
        w_in = sem("w_in")
        tick_pool, tick_dve = sem("tick_pool"), sem("tick_dve")
        small_in = sem("small_in")
        rms_in = sem("rms_in")
        factors_in = [sem(f"factors_in{i}") for i in range(4)]
        consts = sem("consts")
        eps_done = sem("eps_done")
        stats_done = sem("stats_done")
        moments_done = sem("moments_done")
        std_done = sem("std_done")
        rstd_done = sem("rstd_done")
        xn_done = sem("xn_done")
        xT_done = sem("xT_done")
        xnT_done = sem("xnT_done")
        proj_done = sem("proj_done")
        high_done = sem("high_done")
        rest_done = sem("rest_done")
        mid_done = sem("mid_done")
        low_done = sem("low_done")
        v_done = sem("v_done")
        parts_out = [sem(f"parts_out{i}") for i in range(2)]
        stack_in = [sem(f"stack_in{i}") for i in range(4)]
        s_lg = sem("s_lg")
        s_lge = sem("s_lge")
        s_mix = sem("s_mix")
        s_lam = sem("s_lam")
        s_lame = sem("s_lame")
        wbT_ps = sem("wbT_ps")
        wbT_done = sem("wbT_done")
        wo_done = sem("wo_done")
        fT_ps = sem("fT_ps")
        fT_done = sem("fT_done")
        fT_done_act = sem("fT_done_act")
        acc_done = sem("acc_done")
        w12_done = sem("w12_done")

        def load_stack(eng, g, slot):
            half = slot % 2
            seq = (g - half) // 2 if isinstance(g, int) else g
            for t in range(TERMS):
                for side, part in ((0, Q_PART[t]), (1, K_PART[t])):
                    src = parts_dram[seq, 4 * part + 2 * side + half].rearrange("(m d) t -> d m t", d=DH)
                    dst = q_stack(slot) if side == 0 else k_stack(slot)
                    eng.dma_start(dst[DH * t:DH * (t + 1)], src).then_inc(stack_in[slot], 16)

        def carry_wait(eng, tick):
            eng.sem_inc(tick, 1)

        def token_moments(dve, tick, tile, n, stats_sem, aggr_sem, k, first=0):
            if past(k):
                dve.wait_ge(aggr_sem, first + 2 * k)
            carry_wait(dve, tick)
            for t in range(n):
                last = nc.vector.bn_stats(stats[:, t, :], xs[:, tile + t, :])
            last.then_inc(stats_sem, 1)
            dve.wait_ge(stats_sem, k + 1)
            carry_wait(dve, tick)
            for t in range(n):
                last = nc.vector.bn_aggr(moments_new[:, t, :], stats[:, t, :])
            last.then_inc(aggr_sem, 1)
            dve.wait_ge(aggr_sem, first + 2 * k + 1)
            nc.vector.tensor_scalar(moments[:, bass.ds(tile, n), :], moments_new[:, 0:n, :], 1.0, None,
                                    op0=ALU.mult).then_inc(aggr_sem, 1)

        FGROUPS = 4 + KR

        with nc.Block() as block:
            @block.sync
            def _(sp):
                sp.dma_start(xs[:, 0:4, :], x_tiles[:, 0:4, :]).then_inc(x_in[0], 16)
                for i, w in enumerate((Wq, Wk, Wv)):
                    sp.dma_start(wqkv[:, i, :], w).then_inc(w_in, 16)
                for i in range(1, 4):
                    sp.dma_start(xs[:, 4 * i:4 * i + 4, :], x_tiles[:, 4 * i:4 * i + 4, :]).then_inc(x_in[i], 16)
                for i, w in enumerate((bWq, bWk, bWv, bWo)):
                    sp.dma_start(wb_raw[:, i, :], w).then_inc(small_in, 16)
                sp.dma_start(wo_raw[:, :, :], Wo.rearrange("(c p) n -> p c n", p=P)).then_inc(small_in, 16)
                for i, w in enumerate((lq1, lk1, lq2, lk2)):
                    sp.dma_start(lam_in[:, i, :],
                                 w.rearrange("h d -> (h d)").partition_broadcast(P)).then_inc(small_in, 16)
                for i, w in enumerate((fc1_logits, fc2_logits)):
                    sp.dma_start(logits[:, i, :], w.partition_broadcast(P)).then_inc(small_in, 16)
                for i in range(P // DV):
                    sp.dma_start(rms_col[DV * i:DV * (i + 1), :],
                                 rms_scale.rearrange("(p a) -> p a", a=1)).then_inc(rms_in, 16)
                sp.dma_start(a1, fc1_A.rearrange("k d r -> d k r")).then_inc(factors_in[0], 16)
                for it in range(SEQS // 2):
                    c = KR // 4 * it
                    sp.dma_start(b1[:, c:c + KR // 4], fc1_B.rearrange("k r f -> (k r) f")
                                 .rearrange("(c p) f -> p c f", p=P)[:, c:c + KR // 4]).then_inc(factors_in[1], 16)
                    sp.dma_start(a2[:, it, :], fc2_A[:, it * P:(it + 1) * P, :].rearrange("k f r -> f k r"))\
                      .then_inc(factors_in[2], 16)
                    for u in range(2):
                        sp.wait_ge(low_done, 2 * (2 * it + u) + 2)
                        sp.dma_start(parts_dram[2 * it + u].rearrange("c p t -> p c t"),
                                     qk_parts[:, u]).then_inc(parts_out[u], 16)
                sp.dma_start(b2, fc2_B.rearrange("k r f -> (k r) f").rearrange("(c p) f -> p c f", p=P))\
                  .then_inc(factors_in[3], 16)
                for u in range(2):
                    sp.wait_ge(parts_out[u], 16 * SEQS // 2)
                sp.wait_ge(consts, 11)
                for g in range(2):
                    load_stack(sp, g, g)

            @block.gpsimd
            def _(pool):
                nc.gpsimd.memset(eps[:], LN_EPS).then_inc(eps_done, 1)
                nc.gpsimd.memset(ident[:], 0.0)
                nc.gpsimd.memset(upto[:], 1.0)
                nc.gpsimd.memset(ones[:], 1.0)
                nc.gpsimd.memset(future_bf[:], 0.0).then_inc(consts, 1)
                pool.wait_ge(consts, 1)
                nc.gpsimd.affine_select(out=ident[:], in_=ident[:], compare_op=ALU.not_equal, fill=1.0,
                                        base=0, pattern=[[-1, P]], channel_multiplier=1).then_inc(consts, 1)
                nc.gpsimd.affine_select(out=upto[:], in_=upto[:], compare_op=ALU.is_ge, fill=0.0,
                                        base=0, pattern=[[1, P]], channel_multiplier=-1).then_inc(consts, 1)
                nc.gpsimd.affine_select(out=future_bf[:], in_=future_bf[:], compare_op=ALU.is_ge, fill=NEG,
                                        base=0, pattern=[[0, UMAPS], [-1, P]],
                                        channel_multiplier=1).then_inc(consts, 1)
                pool.wait_ge(consts, 2)
                nc.gpsimd.tensor_copy(ident_bf[:], ident[:]).then_inc(consts, 1)
                nc.gpsimd.memset(values[:, :, :, DV], 1.0)
                for slot in range(2):
                    fill_stacks(pool, slot, consts, 5 + 3 * slot)
                def turn(it):
                    for u in range(2):
                        for side in range(2):
                            pool.wait_ge(mid_done, 2 * (2 * it + u) + side + 1)
                            nc.gpsimd.tensor_tensor(
                                qk_parts[:, u, 8 + 2 * side:10 + 2 * side, :].rearrange("p c t -> p (c t)"),
                                qk_rest[:, u, side, :],
                                qk_parts[:, u, 4 + 2 * side:6 + 2 * side, :].rearrange("p c t -> p (c t)"),
                                op=ALU.subtract).then_inc(low_done, 1)

                repeat(pool, SEQS // 2, turn)

            @block.scalar
            def _(act):
                act.wait_ge(eps_done, 1)
                for i in range(4):
                    c = slice(4 * i, 4 * i + 4)
                    act.wait_ge(moments_done, 4 * i + 4)
                    nc.scalar.activation(std[:, c], moments[:, c, 1], ACT.Sqrt, bias=eps[:, 0:1]).then_inc(std_done, 1)
                def turn(it):
                    for u in range(2):
                        b = 2 * it + u
                        act.wait_ge(xT_done, b + 1)
                        nc.scalar.copy(xnT1[:, u, :], ps[:, 4 * u, 0:SEQ]).then_inc(xnT_done, 1)
                    for u in range(2):
                        b = 2 * it + u
                        if past(it):
                            act.wait_ge(parts_out[u], 16 * it)
                        for side in range(2):
                            act.wait_ge(proj_done, 3 * b + side + 1)
                            nc.scalar.copy(
                                qk_parts[:, u, 2 * side:2 * side + 2, :].rearrange("p c t -> p (c t)"),
                                ps[:, 4 * u + 1 + side, :]).then_inc(high_done, 1)
                        act.wait_ge(proj_done, 3 * b + 3)
                        for t in range(TPS):
                            last = nc.scalar.copy(values[:, TPS * b + t, :, 0:DV],
                                                  ps[:, 4 * u + 3, t * 256:(t + 1) * 256]
                                                  .rearrange("p (h d) -> p h d", h=HEADS))
                        last.then_inc(v_done, 1)

                repeat(act, SEQS // 2, turn)
                for i in range(2):
                    act.wait_ge(s_lg, 2)
                    nc.scalar.activation(lg_exp[:, i, :], logits[:, i, :], ACT.Exp, bias=lg_negmax[:, i:i + 1],
                                         accum_out=lg_sum[:, i:i + 1]).then_inc(s_lge, 1)
                act.wait_ge(s_lam, 2)
                nc.scalar.activation(lam_exp[:], lam_sum[:], ACT.Exp).then_inc(s_lame, 1)
                act.wait_ge(wbT_ps, 1)
                nc.scalar.copy(wbT[:].rearrange("p a b -> p (a b)"), ps[:, 4, :]).then_inc(wbT_done, 1)
                act.wait_ge(s_mix, 7)
                for i in range(5, FGROUPS, 2):
                    act.wait_ge(fT_ps, i + 1)
                    if i >= 8:
                        act.wait_ge(acc_done, i - 3)
                    nc.scalar.activation(a2T[:, (i - 4) % 4, :], ps[:, i % 2, :], ACT.Copy,
                                         scale=mix_col[:, 1, i - 4:i - 3]).then_inc(fT_done_act, 1)
                act.wait_ge(acc_done, FGROUPS)
                nc.scalar.copy(w2[:].rearrange("p a b -> p (a b)"), ps[:, 3, :]).then_inc(w12_done, 1)

            @block.vector
            def _(dve):
                for t in range(TILES):
                    if t % 4 == 0:
                        dve.wait_ge(x_in[t // 4], 16)
                    nc.vector.bn_stats(stats[:, t, :], xs[:, t, :]).then_inc(stats_done, 1)
                    if t % 4 == 3:
                        for j in range(t - 3, t + 1):
                            dve.wait_ge(stats_done, t + 1)
                            nc.vector.bn_aggr(moments[:, j, :], stats[:, j, :]).then_inc(moments_done, 1)
                for i in range(4):
                    c = slice(4 * i, 4 * i + 4)
                    dve.wait_ge(std_done, i + 1)
                    nc.vector.reciprocal(rstd[:, c], std[:, c]).then_inc(rstd_done, 1)
                def turn(it):
                    dve.wait_ge(rstd_done, it + 1)
                    if past(it):
                        dve.wait_ge(xT_done, 2 * it)
                    for u in range(2):
                        for t in range(TPS):
                            tile = 2 * (2 * it + u) + t
                            last = nc.vector.tensor_scalar(xn1[:, u, t, :], xs[:, tile, :],
                                                           moments[:, tile, 0:1], rstd[:, bass.ds(tile, 1)],
                                                           op0=ALU.subtract, op1=ALU.mult)
                        last.then_inc(xn_done, 1)
                    for u in range(2):
                        b = 2 * it + u
                        for side in range(2):
                            dve.wait_ge(high_done, 2 * b + side + 1)
                            if past(it):
                                dve.wait_ge(low_done, 4 * it)
                            nc.vector.tensor_tensor(
                                qk_rest[:, u, side, :], ps[:, 4 * u + 1 + side, :],
                                qk_parts[:, u, 2 * side:2 * side + 2, :].rearrange("p c t -> p (c t)"),
                                op=ALU.subtract).then_inc(rest_done, 1)
                        for side in range(2):
                            dve.wait_ge(rest_done, 2 * b + side + 1)
                            nc.vector.tensor_copy(
                                qk_parts[:, u, 4 + 2 * side:6 + 2 * side, :].rearrange("p c t -> p (c t)"),
                                qk_rest[:, u, side, :]).then_inc(mid_done, 1)

                repeat(dve, SEQS // 2, turn)
                dve.wait_ge(small_in, 16 * 11)
                for i in range(2):
                    nc.vector.tensor_reduce(out=lg_negmax[:, i:i + 1], in_=logits[:, i, :], axis=AX, op=ALU.max,
                                            negate=True).then_inc(s_lg, 1)
                for i in range(2):
                    nc.vector.tensor_tensor(lam_prod[:, i, :], lam_in[:, 2 * i, :], lam_in[:, 2 * i + 1, :],
                                            op=ALU.mult).then_inc(s_mix, 1)
                for i in range(2):
                    dve.wait_ge(s_mix, i + 1)
                    nc.vector.tensor_reduce(out=lam_sum[:, i, :],
                                            in_=lam_prod[:, i, :].rearrange("p (h d) -> p h d", d=DH),
                                            axis=AX, op=ALU.add).then_inc(s_lam, 1)
                dve.wait_ge(s_lge, 2)
                nc.vector.reciprocal(lg_inv[:], lg_sum[:]).then_inc(s_mix, 1)
                dve.wait_ge(s_mix, 3)
                for i in range(2):
                    nc.vector.tensor_scalar(mix[:, i, :], lg_exp[:, i, :], lg_inv[:, i:i + 1], None,
                                            op0=ALU.mult).then_inc(s_mix, 1)
                dve.wait_ge(s_mix, 5)
                for k in range(2):
                    half = slice(64 * k, 64 * k + 64)
                    nc.vector.tensor_copy(mix_col[half], mix[half].rearrange("p i (c k) -> p i c k", k=2)[:, :, :, k])\
                        .then_inc(s_mix, 1)
                dve.wait_ge(s_lame, 1)
                nc.vector.scalar_tensor_tensor(out=lam[:], in0=lam_exp[:, 0, :], scalar=LAMBDA_INIT,
                                               in1=lam_exp[:, 1, :], op0=ALU.add, op1=ALU.subtract)\
                    .then_inc(s_lam, 1)
                dve.wait_ge(rms_in, 16 * P // DV)
                nc.vector.tensor_scalar(wo[:], wo_raw[:], rms_col[:, 0:1], 1.0 - LAMBDA_INIT,
                                        op0=ALU.mult, op1=ALU.mult).then_inc(wo_done, 1)
                dve.wait_ge(s_mix, 7)
                for i in [0, 1, 2, 3] + list(range(4, FGROUPS, 2)):
                    dve.wait_ge(fT_ps, i + 1)
                    if i < 4:
                        nc.vector.tensor_tensor(
                            a1T[:, 4 * i:4 * i + 4, :], ps[:, i % 2, :].rearrange("p (c d) -> p c d", c=4),
                            mix_col[:, 0, 4 * i:4 * i + 4].unsqueeze(2).to_broadcast([P, 4, P]),
                            op=ALU.mult).then_inc(fT_done, 1)
                    else:
                        if i >= 8:
                            dve.wait_ge(acc_done, i - 3)
                        nc.vector.tensor_scalar(a2T[:, (i - 4) % 4, :], ps[:, i % 2, :],
                                                mix_col[:, 1, i - 4:i - 3], None,
                                                op0=ALU.mult).then_inc(fT_done, 1)
                dve.wait_ge(acc_done, 4)
                nc.vector.tensor_copy(w1[:], ps[:, 2, :]).then_inc(w12_done, 1)

            @block.tensor
            def _(pe):
                pe.wait_ge(consts, 5)
                pe.wait_ge(w_in, 16 * 3)
                def turn(it):
                    for u in range(2):
                        b = 2 * it + u
                        pe.wait_ge(xn_done, b + 1)
                        if past(it):
                            pe.wait_ge(xnT_done, 2 * it)
                        for t in range(TPS):
                            last = nc.tensor.transpose(ps[:, 4 * u, t * P:(t + 1) * P], xn1[:, u, t, :], ident[:])
                        last.then_inc(xT_done, 1)
                    for u in range(2):
                        b = 2 * it + u
                        pe.wait_ge(xnT_done, b + 1)
                        if past(it):
                            pe.wait_ge(rest_done, 4 * it)
                        for side in range(2):
                            for c in range(2):
                                last = nc.tensor.matmul(ps[:, 4 * u + 1 + side, c * SEQ:(c + 1) * SEQ],
                                                        wqkv[:, side, c * P:(c + 1) * P], xnT1[:, u, :],
                                                        start=True, stop=True)
                            last.then_inc(proj_done, 1)
                        if past(it):
                            pe.wait_ge(v_done, 2 * it)
                        for t in range(TPS):
                            last = nc.tensor.matmul(ps[:, 4 * u + 3, t * 256:(t + 1) * 256],
                                                    xnT1[:, u, t * P:(t + 1) * P], wqkv[:, 2, :],
                                                    start=True, stop=True)
                        last.then_inc(proj_done, 1)

                repeat(pe, SEQS // 2, turn)
                pe.wait_ge(rest_done, 2 * SEQS)
                pe.wait_ge(v_done, SEQS)
                pe.wait_ge(small_in, 16 * 11)
                for i in range(4):
                    last = nc.tensor.transpose(ps[:, 4, i * P:(i + 1) * P], wb_raw[:, i, :], ident[:])
                last.then_inc(wbT_ps, 1)

                def factor_transposes(i):
                    if i >= 2:
                        if i - 2 < 4 or i % 2 == 0:
                            pe.wait_ge(fT_done, min(i - 1, 4) + max(0, (i - 2 - 4) // 2 + 1))
                        else:
                            pe.wait_ge(fT_done_act, (i - 2 - 5) // 2 + 1)
                    for j in range(4):
                        if i < 4:
                            c = 4 * i + j
                            src = a1[:, c * P:(c + 1) * P]
                        else:
                            src = a2[:, j, (i - 4) * P:(i - 3) * P]
                        last = nc.tensor.transpose(ps[:, i % 2, j * P:(j + 1) * P], src, ident[:])
                    last.then_inc(fT_ps, 1)

                def factor_products(i):
                    if i < 4 or i % 2 == 0:
                        pe.wait_ge(fT_done, min(i + 1, 4) + max(0, (i - 4) // 2 + 1))
                    else:
                        pe.wait_ge(fT_done_act, (i - 5) // 2 + 1)
                    for j in range(4):
                        if i < 4:
                            c = 4 * i + j
                            last = nc.tensor.matmul(ps[:, 2, :], a1T[:, c, :], b1[:, c, :],
                                                    start=(c == 0), stop=(c == KR - 1))
                        else:
                            c = i - 4
                            last = nc.tensor.matmul(ps[:, 3, j * P:(j + 1) * P], a2T[:, c % 4, j * P:(j + 1) * P],
                                                    b2[:, c, :], start=(c == 0 and j == 0),
                                                    stop=(c == KR - 1), skip_group_check=True)
                    last.then_inc(acc_done, 1)

                for i in range(FGROUPS + 2):
                    if i == 0:
                        pe.wait_ge(factors_in[0], 16)
                    if i == 2:
                        pe.wait_ge(factors_in[1], 16 * KR // 4)
                    if i == 4:
                        pe.wait_ge(factors_in[2], 16 * FCH)
                    if i == 6:
                        pe.wait_ge(factors_in[3], 16)
                    if i < FGROUPS:
                        factor_transposes(i)
                    if i >= 2:
                        factor_products(i - 2)

        filled_23 = sem("filled_23")
        vaug_done = sem("vaug_done")
        cleared = sem("cleared")
        shift_in = [sem(f"shift_in{i}") for i in range(4)]
        scored = sem("scored")
        maxed = sem("maxed")
        maxT_done = sem("maxT_done")
        shift_hi = sem("shift_hi")
        shift_lo = sem("shift_lo")
        scoredT = sem("scoredT")
        exp_done = sem("exp_done")
        masked = sem("masked")
        pv_done = sem("pv_done")
        ot_copied = sem("ot_copied")
        ott_done = sem("ott_done")
        o_copied = sem("o_copied")
        rden_done = sem("rden_done")
        post = sem("post")
        sq_done = sem("sq_done")
        ms_raw = sem("ms_raw")
        ms_done = sem("ms_done")
        normed = sem("normed")
        nT_done = sem("nT_done")
        oT_done = sem("oT_done")
        oproj_done = sem("oproj_done")
        resid_done = sem("resid_done")
        st2_done = sem("st2_done")
        mom2_done = sem("mom2_done")
        root = sem("root")

        S_BANK, T_BANK, O_BANK, OT_BANK, M_BANK = 0, 2, 4, 6, 7

        def turns(eng, emit):
            for j in range(SLOTS):
                emit(0, j)
            with eng.Fori(1, UNITS // SLOTS) as it:
                for j in range(SLOTS):
                    emit(it, j)
            for j in range(L_STAT - UPS + 1):
                emit(UNITS // SLOTS, j)

        def unit(it, j, lag):
            return SLOTS * it + j - lag

        def group(it, j, lag):
            return (SLOTS // UPG) * it + (j - lag) // UPG

        def seq(it, j, lag):
            return (SLOTS // UPS) * it + (j - lag) // UPS

        def oprojs_before(it, j):
            return (SLOTS // UPS) * it + (j - L_OPROJ - 1) // UPS + 1

        def shifts_before(it, j):
            return (SLOTS // UPG) * it + (j - L_SHIFT - 1) // UPG + 1

        with nc.Block() as block:
            @block.sync
            def _(sp):
                sp.wait_ge(filled_23, 6)
                load_stack(sp, 2, 2)

                def store_shift(g, slot):
                    sp.wait_ge(shift_lo, g + 1)
                    for part in range(SHIFT_ROWS):
                        sp.dma_start(q_stack(slot)[SROWS + part:SROWS + part + 1], shift[:, slot % 2, part, :])\
                          .then_inc(shift_in[slot], 16)

                store_shift(0, 0)
                load_stack(sp, 3, 3)
                with sp.Fori(0, GROUPS // 4 - 1) as it:
                    for k in range(4):
                        g = 4 * it + k
                        store_shift(g + 1, (k + 1) % 4)
                        sp.wait_ge(scoredT, BANKS_U * UPG * (g + 1))
                        load_stack(sp, 2 * (it + 1) + k // 2, k)
                for g in range(GROUPS - 4, GROUPS - 1):
                    store_shift(g + 1, (g + 1) % 4)

            @block.gpsimd
            def _(pool):
                for started in (post, normed):
                    pool.sem_inc(started, FIRST)
                for slot in (2, 3):
                    fill_stacks(pool, slot, filled_23, 3 * (slot - 2))

                def emit(it, j):
                    n = unit(it, j, L_EXP)
                    if live(n, UNITS):
                        r = (j - L_EXP) % 2
                        for s in range(BANKS_U):
                            pool.wait_ge(exp_done, BANKS_U * n + s + 1)
                            carry_wait(pool, tick_pool)
                            if s < 2:
                                diag = probs[:, r, s, :].rearrange("p (m q) -> p m q", m=2)[:, :, 0:P]
                            else:
                                diag = probs[:, r, s, :].rearrange("p (m q) -> p m q", m=UMAPS)
                            nc.gpsimd.affine_select(out=diag, in_=diag, compare_op=ALU.is_ge, fill=0.0, base=0,
                                                    pattern=[[0, 2 if s < 2 else UMAPS], [1, P]],
                                                    channel_multiplier=-1).then_inc(masked, 1)
                    b = seq(it, j, L_DEN)
                    if (j - L_DEN) % UPS == 0 and live(b, SEQS):
                        v = (j - L_DEN) // UPS % 2
                        num = o_sb[:, v].rearrange("p t (h c) d -> p (t h) c d", c=2)
                        inv = rden.rearrange("p t (h c) -> p (t h) c", c=2)
                        pool.wait_ge(rden_done, b + 1)
                        if past(b):
                            pool.wait_ge(post, FIRST + 4 * b)
                            pool.wait_ge(normed, FIRST + b)
                        nc.gpsimd.tensor_tensor(rden2, rden.rearrange("p t (h c) -> p t h c", c=2)[:, :, :, 1],
                                                lam[:].unsqueeze(1).to_broadcast([P, TPS, HEADS]),
                                                op=ALU.mult).then_inc(post, 1)
                        nc.gpsimd.tensor_tensor(o1.rearrange("p t h d -> p (t h) d"), num[:, :, 0, 0:DV],
                                                inv[:, :, 0:1].to_broadcast([P, TPS * HEADS, DV]),
                                                op=ALU.mult).then_inc(post, 1)
                    b = seq(it, j, L_DIFF)
                    if (j - L_DIFF) % UPS == 0 and live(b, SEQS):
                        v = (j - L_DIFF) // UPS % 2
                        num = o_sb[:, v].rearrange("p t (h c) d -> p (t h) c d", c=2)
                        pool.wait_ge(post, FIRST + 4 * b + 1)
                        nc.gpsimd.tensor_tensor(
                            o2.rearrange("p t h d -> p (t h) d"), num[:, :, 1, 0:DV],
                            rden2.rearrange("p t h -> p (t h)").unsqueeze(2).to_broadcast([P, TPS * HEADS, DV]),
                            op=ALU.mult).then_inc(post, 1)
                        pool.wait_ge(post, FIRST + 4 * b + 3)
                        nc.gpsimd.tensor_tensor(o1, o1, o2, op=ALU.subtract).then_inc(post, 1)
                    b = seq(it, j, L_SQ)
                    if (j - L_SQ) % UPS == 0 and live(b, SEQS):
                        pool.wait_ge(post, FIRST + 4 * b + 4)
                        if past(b):
                            pool.wait_ge(ms_raw, FIRST + b)
                        nc.gpsimd.tensor_tensor(osq, o1, o1, op=ALU.mult).then_inc(sq_done, 1)
                    b = seq(it, j, L_NORM)
                    if (j - L_NORM) % UPS == 0 and live(b, SEQS):
                        pool.wait_ge(root, FIRST + ROOT_STEPS * (b + 1))
                        if past(b):
                            pool.wait_ge(nT_done, FIRST + b)
                        nc.gpsimd.tensor_tensor(
                            o_n.rearrange("p t h d -> p (t h) d"), o1.rearrange("p t h d -> p (t h) d"),
                            mrms.unsqueeze(2).to_broadcast([P, TPS * HEADS, DV]),
                            op=ALU.mult).then_inc(normed, 1)

                turns(pool, emit)

            @block.scalar
            def _(act):
                def emit(it, j):
                    n = unit(it, j, L_EXP)
                    if live(n, UNITS):
                        r = (j - L_EXP) % 2
                        if past(n - 1):
                            act.wait_ge(pv_done, n - 1)
                        for s in range(BANKS_U):
                            act.wait_ge(scoredT, BANKS_U * n + s + 1)
                            bank = T_BANK + (j - L_EXP + s) % 2
                            nc.scalar.activation(probs[:, r, s, :], ps[:, bank, :], ACT.Exp,
                                                 scale=SCALE).then_inc(exp_done, 1)
                            g = group(it, j, L_SHIFT)
                            if s == 0 and (j - L_SHIFT) % UPG == 0 and live(g, GROUPS):
                                shift_high(it, j)
                    g = group(it, j, L_SHIFT)
                    if not live(n, UNITS) and (j - L_SHIFT) % UPG == 0 and live(g, GROUPS):
                        shift_high(it, j)
                    n = unit(it, j, L_PV)
                    if live(n, UNITS):
                        r = (j - L_PV) % 2
                        act.wait_ge(pv_done, n + 1)
                        if past(n - 1):
                            act.wait_ge(ott_done, n - 1)
                        nc.scalar.copy(ot_sb[:, r, :], ps[:, O_BANK + r, 0:SEQ]).then_inc(ot_copied, 1)
                    b = seq(it, j, L_VAUG)
                    if (j - L_VAUG) % UPS == 0 and live(b, SEQS):
                        if past(b - 1):
                            act.wait_ge(pv_done, UPS * (b - 1))
                        nc.scalar.copy(vaug[:, (j - L_VAUG) // UPS % 2].rearrange("p t h d -> p t (h d)"),
                                       values[:, bass.ds(TPS * b, TPS), :, :].rearrange("p t h d -> p t (h d)"))\
                            .then_inc(vaug_done, 1)
                    b = seq(it, j, L_OPT)
                    if (j - L_OPT) % UPS == 0 and live(b, SEQS):
                        act.wait_ge(nT_done, FIRST + b + 1)
                        nc.scalar.copy(oT.rearrange("p a b c -> p (a b c)"), ps[:, M_BANK, :])\
                            .then_inc(oT_done, 1)

                def shift_high(it, j):
                    g, k = group(it, j, L_SHIFT), (j - L_SHIFT) // UPG
                    act.wait_ge(maxT_done, g + 1)
                    if past(g - 1):
                        act.wait_ge(shift_in[(k - 2) % 4], 32 * (it + (k - 2) // 4 + 1))
                    nc.scalar.activation(shift[:, k % 2, 0, :], ps[0:GMAPS, M_BANK, 0:SEQ], ACT.Copy,
                                         scale=-1.0).then_inc(shift_hi, 1)

                turns(act, emit)

            @block.vector
            def _(dve):
                for started in (ms_raw, resid_done, mom2_done, root):
                    dve.sem_inc(started, FIRST)
                nc.vector.memset(ps[:, O_BANK:O_BANK + 2, 0:SEQ], 0.0).then_inc(cleared, 1)

                def root_step(it, j, point):
                    for step in range(ROOT_STEPS):
                        at = POINTS - 1 + step
                        lag = L_MS + at // POINTS
                        b = seq(it, j, lag)
                        if at % POINTS != point or (j - lag) % UPS or not live(b, SEQS):
                            continue
                        dve.wait_ge(root, FIRST + ROOT_STEPS * b + step)
                        if step == 0:
                            dve.wait_ge(ms_done, b + 1)
                            nc.vector.tensor_scalar(root_half, msum, -0.5, None, op0=ALU.mult)
                            last = nc.vector.tensor_scalar(root_tmp.bitcast(I32), msum.bitcast(I32), 1, None,
                                                           op0=ALU.logical_shift_right)
                        elif step == 1:
                            if past(b):
                                dve.wait_ge(normed, FIRST + b)
                            last = nc.vector.tensor_scalar(mrms.bitcast(I32), root_tmp.bitcast(I32), -1.0,
                                                           float(ROOT_SEED), op0=ALU.mult, op1=ALU.add)
                        elif (step - ROOT_FIRST) % 3 == 0:
                            last = nc.vector.tensor_tensor(root_tmp, mrms, mrms, op=ALU.mult)
                        elif (step - ROOT_FIRST) % 3 == 1:
                            last = nc.vector.tensor_tensor(root_tmp, root_tmp, root_half, op=ALU.mult)
                        else:
                            last = nc.vector.scalar_tensor_tensor(out=mrms, in0=root_tmp, scalar=1.5, in1=mrms,
                                                                  op0=ALU.add, op1=ALU.mult)
                        last.then_inc(root, 1)

                def emit(it, j):
                    n = unit(it, j, 0)
                    if live(n, UNITS):
                        uu, gs = j % UPG, j // UPG % 2
                        for s in range(BANKS_U):
                            bank = S_BANK + (j + s) % 2
                            dve.wait_ge(scored, BANKS_U * n + s + 1)
                            if s == 0:
                                dst = rowmax[:, gs, 0, UMAPS * uu:UMAPS * uu + UMAPS]
                            else:
                                dst = rowmax[:, gs, 1, UMAPS * uu + 2 * s - 2:UMAPS * uu + 2 * s]
                            nc.vector.tensor_reduce(
                                out=dst, in_=ps[:, bank, :].rearrange("p (m k) -> p m k", m=UMAPS if s == 0 else 2),
                                axis=AX, op=ALU.max).then_inc(maxed, 1)
                            root_step(it, j, s)
                    else:
                        for s in range(BANKS_U):
                            root_step(it, j, s)
                    g = group(it, j, L_SHIFT)
                    if (j - L_SHIFT) % UPG == 0 and live(g, GROUPS):
                        k = (j - L_SHIFT) // UPG
                        dve.wait_ge(shift_hi, g + 1)
                        nc.vector.scalar_tensor_tensor(
                            out=shift[:, k % 2, 1, :], in0=ps[0:GMAPS, M_BANK, 0:SEQ], scalar=-1.0,
                            in1=shift[:, k % 2, 0, :], op0=ALU.mult, op1=ALU.subtract).then_inc(shift_lo, 1)
                    n = unit(it, j, L_OT)
                    if live(n, UNITS):
                        u, v = (j - L_OT) % UPS, (j - L_OT) // UPS % 2
                        dve.wait_ge(ott_done, n + 1)
                        src = ps[:, OT_BANK, 0:TPS * P].rearrange("p (t m d) -> p t m d", t=TPS, m=UMAPS)
                        nc.vector.tensor_copy(o_sb[:, v, :, UMAPS * u:UMAPS * u + UMAPS, :],
                                              src[:, :, :, 0:DV + 1]).then_inc(o_copied, 1)
                    b = seq(it, j, L_DEN)
                    if (j - L_DEN) % UPS == 0 and live(b, SEQS):
                        v = (j - L_DEN) // UPS % 2
                        dve.wait_ge(o_copied, UPS * (b + 1))
                        if past(b):
                            dve.wait_ge(post, FIRST + 4 * b)
                        nc.vector.reciprocal(rden, o_sb[:, v, :, :, DV]).then_inc(rden_done, 1)
                    b = seq(it, j, L_MS)
                    if (j - L_MS) % UPS == 0 and live(b, SEQS):
                        dve.wait_ge(sq_done, b + 1)
                        if past(b):
                            dve.wait_ge(root, FIRST + ROOT_STEPS * b)
                        nc.vector.tensor_reduce(out=msum, in_=osq.rearrange("p t h d -> p (t h) d"), axis=AX,
                                                op=ALU.add).then_inc(ms_raw, 1)
                        dve.wait_ge(ms_raw, FIRST + b + 1)
                        nc.vector.tensor_scalar(msum, msum, 1.0 / DV, RMS_EPS, op0=ALU.mult,
                                                op1=ALU.add).then_inc(ms_done, 1)
                    root_step(it, j, POINTS - 1)
                    b = seq(it, j, L_OPROJ)
                    if (j - L_OPROJ) % UPS == 0 and live(b, SEQS):
                        dve.wait_ge(oproj_done, b + 1)
                        x2 = xs[:, bass.ds(2 * b, 2), :].rearrange("p t d -> p (t d)")
                        nc.vector.tensor_tensor(x2, ps[:, M_BANK, 0:TPS * D], x2, op=ALU.add)\
                            .then_inc(resid_done, 1)
                    b = seq(it, j, L_STAT)
                    if (j - L_STAT) % UPS == 0 and live(b, SEQS):
                        dve.wait_ge(resid_done, FIRST + b + 1)
                        token_moments(dve, tick_dve, TPS * b, TPS, st2_done, mom2_done, b, FIRST)

                turns(dve, emit)

            @block.tensor
            def _(pe):
                pe.sem_inc(nT_done, FIRST)

                def score_bank(it, j, s):
                    n = unit(it, j, 0)
                    slot, m0 = j // UPG % 4, UMAPS * (j % UPG)
                    q, k = q_stack(slot), k_stack(slot)
                    bank = ps[:, S_BANK + (j + s) % 2, :]
                    if s == 0 and j % UPG == 0:
                        pe.wait_ge(stack_in[slot], 2 * TERMS * 16 * (it + 1))
                    if past(BANKS_U * n + s - 1):
                        pe.wait_ge(maxed, BANKS_U * n + s - 1)
                    if s == 0:
                        for m in range(UMAPS):
                            nc.tensor.matmul(bank[:, m * P:(m + 1) * P], q[0:SROWS, m0 + m, 0:P],
                                             k[0:SROWS, m0 + m, 0:P], start=(m == 0), stop=False,
                                             skip_group_check=True)
                        nc.tensor.matmul(bank, ident_bf[:], future_bf[:].rearrange("p m k -> p (m k)"),
                                         start=False, stop=True, skip_group_check=True).then_inc(scored, 1)
                    else:
                        for m in range(2):
                            nc.tensor.matmul(bank[:, m * SEQ:(m + 1) * SEQ], q[0:SROWS, m0 + 2 * s - 2 + m, P:SEQ],
                                             k[0:SROWS, m0 + 2 * s - 2 + m, :], start=(m == 0), stop=False,
                                             skip_group_check=True)
                        nc.tensor.matmul(bank.rearrange("p (m k) -> p m k", m=2)[:, :, P:SEQ], ident_bf[:],
                                         future_bf[:, 0:2, :], start=False, stop=True,
                                         skip_group_check=True).then_inc(scored, 1)

                def shifted_bank(it, j, s):
                    n = unit(it, j, L_EXP)
                    jj = j - L_EXP
                    slot, m0 = jj // UPG % 4, UMAPS * (jj % UPG)
                    q, k = q_stack(slot), k_stack(slot)
                    bank = ps[:, T_BANK + (jj + s) % 2, :]
                    if s == 0 and jj % UPG == 0:
                        pe.wait_ge(shift_in[slot], 32 * (it + jj // SLOTS + 1))
                    if past(BANKS_U * n + s - 1):
                        pe.wait_ge(exp_done, BANKS_U * n + s - 1)
                    if s < 2:
                        for m in range(2):
                            last = nc.tensor.matmul(bank[:, m * SEQ:(m + 1) * SEQ], k[0:XROWS, m0 + 2 * s + m, 0:P],
                                                    q[0:XROWS, m0 + 2 * s + m, :], start=True, stop=True)
                    else:
                        for m in range(UMAPS):
                            last = nc.tensor.matmul(bank[:, m * P:(m + 1) * P], k[0:XROWS, m0 + m, P:SEQ],
                                                    q[0:XROWS, m0 + m, P:SEQ], start=True, stop=True)
                    last.then_inc(scoredT, 1)

                def weigh_values(it, j):
                    n = unit(it, j, L_PV)
                    jj = j - L_PV
                    r, v = jj % 2, jj // UPS % 2
                    pe.wait_ge(masked, BANKS_U * (n + 1))
                    if jj % UPS == 0:
                        pe.wait_ge(vaug_done, seq(it, j, L_PV) + 1)
                    if past(n - 1):
                        pe.wait_ge(ot_copied, n - 1)
                    for m in range(UMAPS):
                        head = 2 * (jj % UPS) + m // 2
                        nc.tensor.matmul(ps[32 * m:32 * m + DV + 1, O_BANK + r, 0:SEQ], vaug[:, v, 0, head, :],
                                         probs[:, r, m // 2, m % 2 * SEQ:m % 2 * SEQ + SEQ],
                                         start=True, stop=False, skip_group_check=True)
                    for m in range(UMAPS):
                        head = 2 * (jj % UPS) + m // 2
                        last = nc.tensor.matmul(ps[32 * m:32 * m + DV + 1, O_BANK + r, P:SEQ],
                                                vaug[:, v, 1, head, :],
                                                probs[:, r, 2, m * P:(m + 1) * P],
                                                start=False, stop=True, skip_group_check=True)
                    last.then_inc(pv_done, 1)

                def emit(it, j):
                    for s in range(BANKS_U):
                        if live(unit(it, j, 0), UNITS):
                            score_bank(it, j, s)
                        if live(unit(it, j, L_EXP), UNITS):
                            shifted_bank(it, j, s)
                        g = group(it, j, L_SHIFT)
                        if s == 0 and (j - L_SHIFT) % UPG == 0 and live(g, GROUPS):
                            k = (j - L_SHIFT) // UPG
                            pe.wait_ge(maxed, BANKS_U * UPG * (g + 1))
                            if past(shifts_before(it, j)):
                                pe.wait_ge(shift_lo, shifts_before(it, j))
                            if past(oprojs_before(it, j)):
                                pe.wait_ge(resid_done, FIRST + oprojs_before(it, j))
                            for t in range(TPS):
                                last = nc.tensor.transpose(ps[0:GMAPS, M_BANK, t * P:(t + 1) * P],
                                                           rowmax[:, k % 2, t, :], ident[:])
                            last.then_inc(maxT_done, 1)
                    if live(unit(it, j, L_PV), UNITS):
                        weigh_values(it, j)
                    n = unit(it, j, L_OT)
                    if live(n, UNITS):
                        pe.wait_ge(ot_copied, n + 1)
                        if past(n):
                            pe.wait_ge(o_copied, n)
                        for t in range(TPS):
                            last = nc.tensor.transpose(ps[:, OT_BANK, t * P:(t + 1) * P],
                                                       ot_sb[:, (j - L_OT) % 2, t * P:(t + 1) * P], ident[:])
                        last.then_inc(ott_done, 1)
                    b = seq(it, j, L_OPT)
                    if (j - L_OPT) % UPS == 0 and live(b, SEQS):
                        pe.wait_ge(normed, FIRST + b + 1)
                        if past(shifts_before(it, j)):
                            pe.wait_ge(shift_lo, min(shifts_before(it, j), GROUPS)
                                       if isinstance(it, int) else shifts_before(it, j))
                        if past(b):
                            pe.wait_ge(resid_done, FIRST + b)
                        flat = o_n.rearrange("p t h d -> p t (h d)")
                        for t in range(TPS):
                            for c in range(2):
                                last = nc.tensor.transpose(ps[:, M_BANK, (2 * t + c) * P:(2 * t + c + 1) * P],
                                                           flat[:, t, c * P:(c + 1) * P], ident[:])
                        last.then_inc(nT_done, 1)
                    b = seq(it, j, L_OPROJ)
                    if (j - L_OPROJ) % UPS == 0 and live(b, SEQS):
                        pe.wait_ge(oT_done, b + 1)
                        for t in range(TPS):
                            for c in range(2):
                                last = nc.tensor.matmul(ps[:, M_BANK, t * D:(t + 1) * D], oT[:, t, c, :],
                                                        wo[:, c, :], start=(c == 0), stop=(c == 1))
                        last.then_inc(oproj_done, 1)

                pe.wait_ge(cleared, 1)
                turns(pe, emit)

        def feed_forward(tag, store):
            BT = 4
            BLOCKS = TILES // BT
            at = 0
            hT, at = carve(at, (2, FCH, BT * P))
            xn, at = carve(at, (2, BT, D))
            xnT, at = carve(at, (2, BT * P))
            f_std, f_rstd = sem(f"{tag}_std"), sem(f"{tag}_rstd")
            f_xn, f_xT, f_xnT = sem(f"{tag}_xn"), sem(f"{tag}_xT"), sem(f"{tag}_xnT")
            f_up, f_gelu, f_down = sem(f"{tag}_up"), sem(f"{tag}_gelu"), sem(f"{tag}_down")
            f_res, f_st, f_mom = sem(f"{tag}_res"), sem(f"{tag}_st"), sem(f"{tag}_mom")
            stored = sem(f"{tag}_stored")

            with nc.Block() as block:
                @block.vector
                def _(dve):
                    dve.wait_ge(f_std, 1)
                    nc.vector.reciprocal(rstd[:], std[:]).then_inc(f_rstd, 1)
                    dve.wait_ge(f_rstd, 1)
                    def turn(it):
                        if past(it):
                            dve.wait_ge(f_xT, 2 * it)
                        for u in range(2):
                            for t in range(BT):
                                tile = BT * (2 * it + u) + t
                                last = nc.vector.tensor_scalar(xn[:, u, t, :], xs[:, tile, :],
                                                               moments[:, tile, 0:1], rstd[:, bass.ds(tile, 1)],
                                                               op0=ALU.subtract, op1=ALU.mult)
                            last.then_inc(f_xn, 1)
                        for u in range(2):
                            k = 2 * it + u
                            x4 = xs[:, bass.ds(BT * k, BT), :].rearrange("p t d -> p (t d)")
                            dve.wait_ge(f_down, k + 1)
                            nc.vector.tensor_tensor(x4, ps[:, 6 + u, :], x4, op=ALU.add).then_inc(f_res, 1)
                            if not store:
                                dve.wait_ge(f_res, k + 1)
                                token_moments(dve, tick_dve, BT * k, BT, f_st, f_mom, k)

                    repeat(dve, BLOCKS // 2, turn)

                @block.scalar
                def _(act):
                    nc.scalar.activation(std[:], moments[:, :, 1], ACT.Sqrt, bias=eps[:, 0:1]).then_inc(f_std, 1)

                    def turn(it):
                        for u in range(2):
                            act.wait_ge(f_xT, 2 * it + u + 1)
                            nc.scalar.copy(xnT[:, u, :], ps[:, u, :]).then_inc(f_xnT, 1)
                        for u in range(2):
                            k = 2 * it + u
                            if past(it):
                                act.wait_ge(f_down, 2 * it)
                            for c in range(FCH):
                                act.wait_ge(f_up, FCH * k + c + 1)
                                nc.scalar.activation(hT[:, u, c, :], ps[:, 2 + c, :],
                                                     ACT.Gelu_apprx_tanh).then_inc(f_gelu, 1)

                    repeat(act, BLOCKS // 2, turn)

                @block.tensor
                def _(pe):
                    def turn(it):
                        for u in range(2):
                            pe.wait_ge(f_xn, 2 * it + u + 1)
                            if past(it):
                                pe.wait_ge(f_xnT, 2 * it)
                            for t in range(BT):
                                last = nc.tensor.transpose(ps[:, u, t * P:(t + 1) * P], xn[:, u, t, :], ident[:])
                            last.then_inc(f_xT, 1)
                        for u in range(2):
                            k = 2 * it + u
                            pe.wait_ge(f_xnT, k + 1)
                            for c in range(FCH):
                                if u or past(it):
                                    pe.wait_ge(f_gelu, FCH * (k - 1) + c + 1)
                                nc.tensor.matmul(ps[:, 2 + c, :], w1[:, c * P:(c + 1) * P], xnT[:, u, :],
                                                 start=True, stop=True).then_inc(f_up, 1)
                        for u in range(2):
                            k = 2 * it + u
                            pe.wait_ge(f_gelu, FCH * (k + 1))
                            if past(it):
                                pe.wait_ge(f_res, 2 * it)
                            for t in range(BT):
                                for c in range(FCH):
                                    last = nc.tensor.matmul(ps[:, 6 + u, t * D:(t + 1) * D],
                                                            hT[:, u, c, t * P:(t + 1) * P], w2[:, c, :],
                                                            start=(c == 0), stop=(c == FCH - 1))
                            last.then_inc(f_down, 1)

                    repeat(pe, BLOCKS // 2, turn)

                if store:
                    @block.sync
                    def _(sp):
                        with sp.Fori(0, BLOCKS) as k:
                            sp.wait_ge(f_res, k + 1)
                            sp.dma_start(out_tiles[:, bass.ds(BT * k, BT), :], xs[:, bass.ds(BT * k, BT), :])\
                              .then_inc(stored, 16)
                        sp.wait_ge(stored, 16 * BLOCKS)

        def linear_attend():
            E1 = DH + 1
            EG = 3
            at = 0
            xn, at = carve(at, (2, TPS, D))
            xnT, at = carve(at, (2, TPS * P))
            low, at = carve(at, (2, TPS, 2 * D))
            phi, at = carve(at, (2, TPS, 2 * D))
            vb, at = carve(at, (2, TPS, D))
            kv, at = carve(at, (2, TPS, E1, D))
            prod, at = carve(at, (2, E1, D))
            nd, at = carve(at, (2, TPS, E1, HEADS))
            inv, at = carve(at, (2, TPS, HEADS))
            o, at = carve(at, (2, TPS, D))
            oT_l, at = carve(at, (2, TPS * P))
            names = ("std rstd xn xT xnT qkv neg exp phi v kv pre prod nd inv oraw o oT oTs out res st mom").split()
            L = {k: sem(f"l_{k}") for k in names}
            PROJ, SUM, BACK = 1, 2, 3

            def slots(eng, emit):
                for m in range(4):
                    emit(m // 2, m % 2)
                with eng.Fori(2, SEQS // 2) as it:
                    for u in range(2):
                        emit(it, u)
                for m in range(BACK):
                    emit(SEQS // 2 + m // 2, m % 2)

            with nc.Block() as block:
                @block.gpsimd
                def _(pool):
                    pool.sem_inc(L["oraw"], FIRST)

                    def emit(it, u):
                        b, w = 2 * it + u - BACK, (u - BACK) % 2
                        if live(b, SEQS):
                            pool.wait_ge(L["inv"], b + 1)
                            if past(b - 1):
                                pool.wait_ge(L["oT"], FIRST + b - 1)
                            for t in range(TPS):
                                last = nc.gpsimd.tensor_tensor(
                                    o[:, w, t, :].rearrange("p (h e) -> p e h", e=DH), nd[:, w, t, 0:DH, :],
                                    inv[:, w, t, :].unsqueeze(1).to_broadcast([P, DH, HEADS]), op=ALU.mult)
                            last.then_inc(L["oraw"], 1)
                            pool.wait_ge(L["oraw"], FIRST + b + 1)
                            carry_wait(pool, tick_pool)
                            nc.gpsimd.tensor_scalar(o[:, w], o[:, w], LIN_EPS, None, op0=ALU.add)\
                                .then_inc(L["o"], 1)
                        b, w = 2 * it + u - PROJ, (u - PROJ) % 2
                        if live(b, SEQS):
                            for t in range(TPS):
                                pool.wait_ge(L["phi"], TPS * b + t + 1)
                                pool.wait_ge(L["v"], TPS * b + t + 1)
                                if past(b - 1):
                                    pool.wait_ge(L["pre"], 2 * EG * (b - 1))
                                kh = phi[:, w, t, D:2 * D].rearrange("p (h d) -> p h d", d=DH)
                                vh = vb[:, w, t, :].rearrange("p (h e) -> p e h", e=DH)
                                nc.gpsimd.tensor_tensor(
                                    kv[:, w, t, 0:DH, :].rearrange("p e (h d) -> p e h d", d=DH),
                                    kh.unsqueeze(1).to_broadcast([P, DH, HEADS, DH]),
                                    vh.unsqueeze(3).to_broadcast([P, DH, HEADS, DH]), op=ALU.mult)\
                                    .then_inc(L["kv"], 1)
                                nc.gpsimd.tensor_copy(kv[:, w, t, DH, :], phi[:, w, t, D:2 * D])\
                                    .then_inc(L["kv"], 1)

                    slots(pool, emit)

                @block.scalar
                def _(act):
                    nc.scalar.activation(std[:], moments[:, :, 1], ACT.Sqrt, bias=eps[:, 0:1]).then_inc(L["std"], 1)

                    def emit(it, u):
                        b, w = 2 * it + u - PROJ, (u - PROJ) % 2
                        if live(b, SEQS):
                            for t in range(TPS):
                                act.wait_ge(L["qkv"], TPS * b + t + 1)
                                if past(b - 1):
                                    act.wait_ge(L["phi"], TPS * (b - 1))
                                nc.scalar.activation(low[:, w, t, :], ps[:, 1 + t, 0:2 * D], ACT.Relu,
                                                     scale=-1.0).then_inc(L["neg"], 1)
                                if past(b - 1):
                                    act.wait_ge(L["kv"], 2 * TPS * (b - 1))
                                nc.scalar.copy(vb[:, w, t, :], ps[:, 1 + t, 2 * D:3 * D]).then_inc(L["v"], 1)
                                act.wait_ge(L["neg"], TPS * b + t + 1)
                                nc.scalar.activation(low[:, w, t, :], low[:, w, t, :], ACT.Exp, scale=-1.0)\
                                    .then_inc(L["exp"], 1)
                        b = 2 * it + u
                        if live(b, SEQS):
                            act.wait_ge(L["xT"], b + 1)
                            if past(b - 1):
                                act.wait_ge(L["qkv"], TPS * (b - 1))
                            nc.scalar.copy(xnT[:, u, :], ps[:, 0, 0:TPS * P]).then_inc(L["xnT"], 1)
                        b, w = 2 * it + u - BACK, (u - BACK) % 2
                        if live(b, SEQS):
                            act.wait_ge(L["oT"], FIRST + b + 1)
                            if past(b - 1):
                                act.wait_ge(L["out"], FIRST + b - 1)
                            nc.scalar.copy(oT_l[:, w, :], ps[:, 7, 0:TPS * P]).then_inc(L["oTs"], 1)

                    slots(act, emit)

                @block.vector
                def _(dve):
                    dve.wait_ge(L["std"], 1)
                    nc.vector.reciprocal(rstd[:], std[:]).then_inc(L["rstd"], 1)
                    dve.wait_ge(L["rstd"], 1)

                    def weigh(it, u, i):
                        b, w = 2 * it + u - SUM, (u - SUM) % 2
                        if live(b, SEQS):
                            t, e = i // EG, i % EG
                            dve.wait_ge(L["pre"], 2 * EG * b + i + 1)
                            if past(TPS * b + t - 1):
                                dve.wait_ge(L["nd"], TPS * b + t - 1)
                            nc.vector.tensor_tensor(
                                prod[:, t, EG * e:EG * e + EG, :],
                                ps[:, 3 + (2 * EG * w + i) % 4, 0:EG * D].rearrange("p (e d) -> p e d", e=EG),
                                phi[:, w, t, 0:D].unsqueeze(1).to_broadcast([P, EG, D]),
                                op=ALU.mult).then_inc(L["prod"], 1)

                    def sum_width(it, u, t):
                        b, w = 2 * it + u - SUM, (u - SUM) % 2
                        if live(b, SEQS):
                            dve.wait_ge(L["prod"], 2 * EG * b + EG * (t + 1))
                            if past(b - 1):
                                dve.wait_ge(L["oraw"], FIRST + b - 1)
                            nc.vector.tensor_reduce(
                                out=nd[:, w, t].rearrange("p e h -> p (e h)"),
                                in_=prod[:, t].rearrange("p e (h d) -> p (e h) d", d=DH), axis=AX,
                                op=ALU.add).then_inc(L["nd"], 1)

                    def elu(it, u, t):
                        b, w = 2 * it + u - PROJ, (u - PROJ) % 2
                        if live(b, SEQS):
                            dve.wait_ge(L["exp"], TPS * b + t + 1)
                            if past(b - 1):
                                dve.wait_ge(L["kv"], 2 * TPS * (b - 1))
                                dve.wait_ge(L["prod"], 2 * EG * (b - 1))
                            nc.vector.scalar_tensor_tensor(
                                out=phi[:, w, t, :], in0=ps[:, 1 + t, 0:2 * D], scalar=0.0,
                                in1=low[:, w, t, :], op0=ALU.max, op1=ALU.add).then_inc(L["phi"], 1)

                    def emit(it, u):
                        b = 2 * it + u
                        if live(b, SEQS):
                            if past(b - 1):
                                dve.wait_ge(L["xT"], b - 1)
                            for t in range(TPS):
                                tile = TPS * b + t
                                last = nc.vector.tensor_scalar(xn[:, u, t, :], xs[:, tile, :],
                                                               moments[:, tile, 0:1], rstd[:, bass.ds(tile, 1)],
                                                               op0=ALU.subtract, op1=ALU.mult)
                            last.then_inc(L["xn"], 1)
                        weigh(it, u, 0)
                        elu(it, u, 0)
                        elu(it, u, 1)
                        weigh(it, u, 1)
                        weigh(it, u, 2)
                        sum_width(it, u, 0)
                        for i in range(EG, 2 * EG):
                            weigh(it, u, i)
                        sum_width(it, u, 1)
                        b, w = 2 * it + u - SUM, (u - SUM) % 2
                        if live(b, SEQS):
                            dve.wait_ge(L["nd"], TPS * (b + 1))
                            nc.vector.reciprocal(inv[:, w], nd[:, w, :, DH, :]).then_inc(L["inv"], 1)
                        b = 2 * it + u - BACK
                        if live(b, SEQS):
                            dve.wait_ge(L["out"], FIRST + b + 1)
                            x2 = xs[:, bass.ds(2 * b, 2), :].rearrange("p t d -> p (t d)")
                            nc.vector.tensor_tensor(x2, ps[:, 7, 256:256 + TPS * D], x2, op=ALU.add)\
                                .then_inc(L["res"], 1)
                            dve.wait_ge(L["res"], b + 1)
                            token_moments(dve, tick_dve, TPS * b, TPS, L["st"], L["mom"], b)

                    slots(dve, emit)

                @block.tensor
                def _(pe):
                    pe.sem_inc(L["out"], FIRST)
                    pe.sem_inc(L["oT"], FIRST)

                    def running_sums(it, u, i):
                        b, w = 2 * it + u - SUM, (u - SUM) % 2
                        if live(b, SEQS):
                            t, e = i // EG, i % EG
                            pe.wait_ge(L["kv"], 2 * TPS * b + 2 * (t + 1))
                            if past(2 * EG * b + i - 3):
                                pe.wait_ge(L["prod"], 2 * EG * b + i - 3)
                            bank = ps[:, 3 + (2 * EG * w + i) % 4, 0:EG * D]
                            rows = kv[:, w, t, EG * e:EG * e + EG, :].rearrange("p e d -> p (e d)")
                            last = nc.tensor.matmul(bank, upto[:], rows, start=True, stop=(t == 0))
                            if t == 1:
                                rows = kv[:, w, 0, EG * e:EG * e + EG, :].rearrange("p e d -> p (e d)")
                                last = nc.tensor.matmul(bank, ones[:], rows, start=False, stop=True)
                            last.then_inc(L["pre"], 1)

                    def emit(it, u):
                        b, w = 2 * it + u - PROJ, (u - PROJ) % 2
                        if live(b, SEQS):
                            for t in range(TPS):
                                pe.wait_ge(L["xnT"], b + 1)
                                if past(b):
                                    pe.wait_ge(L["phi"], TPS * b)
                                    pe.wait_ge(L["v"], TPS * b)
                                nc.tensor.matmul(ps[:, 1 + t, 0:3 * D], xnT[:, w, t * P:(t + 1) * P],
                                                 wbT[:, 0:3, :].rearrange("p a b -> p (a b)"),
                                                 start=True, stop=True).then_inc(L["qkv"], 1)
                        for i in range(EG):
                            running_sums(it, u, i)
                        b = 2 * it + u
                        if live(b, SEQS):
                            pe.wait_ge(L["xn"], b + 1)
                            if past(b):
                                pe.wait_ge(L["xnT"], b)
                            for t in range(TPS):
                                last = nc.tensor.transpose(ps[:, 0, t * P:(t + 1) * P], xn[:, u, t, :], ident[:])
                            last.then_inc(L["xT"], 1)
                        running_sums(it, u, EG)
                        b, w = 2 * it + u - BACK, (u - BACK) % 2
                        if live(b, SEQS):
                            pe.wait_ge(L["o"], b + 1)
                            if past(b):
                                pe.wait_ge(L["res"], b)
                            for t in range(TPS):
                                last = nc.tensor.transpose(ps[:, 7, t * P:(t + 1) * P], o[:, w, t, :], ident[:])
                            last.then_inc(L["oT"], 1)
                        running_sums(it, u, EG + 1)
                        running_sums(it, u, EG + 2)
                        if live(b, SEQS):
                            pe.wait_ge(L["oTs"], b + 1)
                            for t in range(TPS):
                                last = nc.tensor.matmul(ps[:, 7, 256 + t * D:256 + (t + 1) * D],
                                                        oT_l[:, w, t * P:(t + 1) * P], wbT[:, 3, :],
                                                        start=True, stop=True)
                            last.then_inc(L["out"], 1)

                    slots(pe, emit)

        feed_forward("f1", False)
        linear_attend()
        feed_forward("f2", True)


_INS = ['L0_attn_a_X', 'L0_attn_a_Wq', 'L0_attn_a_Wk', 'L0_attn_a_Wv', 'L0_attn_a_Wo',
        'L0_attn_a_lambda_q1', 'L0_attn_a_lambda_k1', 'L0_attn_a_lambda_q2', 'L0_attn_a_lambda_k2',
        'L0_attn_a_rms_scale', 'L0_attn_b_Wq', 'L0_attn_b_Wk', 'L0_attn_b_Wv', 'L0_attn_b_Wo',
        'L0_ffn_fc1_A', 'L0_ffn_fc1_B', 'L0_ffn_fc2_A', 'L0_ffn_fc2_B', 'L0_ffn_fc1_logits',
        'L0_ffn_fc2_logits']
_OUTS = [((SEQS, SEQ, D), 'float32')]


def kernel(**inputs):
    import numpy as _np
    import concourse.bacc as _bacc
    from concourse import mybir as _mybir
    from concourse.bass_utils import run_bass_kernel_spmd as _run

    nc = _bacc.Bacc("TRN2", target_bir_lowering=False, num_devices=1)
    arrays, args = {}, []
    for name in _INS:
        a = _np.ascontiguousarray(inputs[name])
        arrays[f"in_{name}_dram"] = a
        args.append(nc.dram_tensor(f"in_{name}_dram", a.shape, _mybir.dt.from_np(a.dtype), kind="ExternalInput").ap())
    for i, (shape, dtype) in enumerate(_OUTS):
        dt = _mybir.dt.from_np(_np.dtype(dtype))
        args.append(nc.dram_tensor(f"out_{i}_dram", shape, dt, kind="ExternalOutput").ap())
    hybrid_kernel(nc, *args)
    r = _run(nc, [arrays], core_ids=[0])
    return r.results[0]["out_0_dram"]
```

```python
from contextlib import ExitStack

import numpy as np

import concourse.bass as bass
from concourse import mybir

F32 = mybir.dt.float32
BF16 = mybir.dt.bfloat16
I32 = mybir.dt.int32
ALU = mybir.AluOpType
ACT = mybir.ActivationFunctionType
AX = mybir.AxisListType.X

P = 128
SEQS, SEQ, D = 8, 256, 128
TILES = SEQS * SEQ // P
FIRST = 1
TPS = SEQ // P
HEADS, DH = 16, 8
DV = 2 * DH
MAPS = 2 * HEADS
F = 512
FCH = F // P
PRIMS, R = 32, 64
KR = PRIMS * R // P
LN_EPS = 1e-5
RMS_EPS = 1e-5
LIN_EPS = 1e-12
LAMBDA_INIT = 0.8
SCALE = float(1.0 / np.sqrt(DH))
NEG = -1e30
LOWEST = -3e38

Q_PART = (0, 0, 1, 1, 0, 2)
K_PART = (0, 1, 0, 1, 2, 0)
TERMS = len(Q_PART)
SHIFT_ROWS = 2
SROWS = 96
XROWS = P

GMAPS = 16
GROUPS = SEQS * MAPS // GMAPS
UMAPS = 4
UNITS = SEQS * MAPS // UMAPS
UPG = GMAPS // UMAPS
UPS = MAPS // UMAPS
SLOTS = 16
BANKS_U = 3
PROBS = 4
L_SHIFT, L_EXP, L_PV, L_OT, L_VAUG = 4, 6, 8, 9, 5
L_DEN, L_DIFF, L_SQ, L_MS, L_NORM, L_OPT, L_OPROJ, L_STAT = 16, 17, 19, 19, 22, 22, 23, 23
ROOT_SEED = 0x5F3759DF
ROOT_STEPS, ROOT_FIRST = 11, 2
POINTS = 4


def live(index, count):
    return not isinstance(index, int) or 0 <= index < count


def past(value):
    return not isinstance(value, int) or value > 0


def repeat(eng, turns, turn):
    turn(0)
    with eng.Fori(1, turns) as it:
        turn(it)


def hybrid_kernel(nc, X, Wq, Wk, Wv, Wo, lq1, lk1, lq2, lk2, rms_scale, bWq, bWk, bWv, bWo,
                  fc1_A, fc1_B, fc2_A, fc2_B, fc1_logits, fc2_logits, out):
    x_tiles = X.rearrange("b (t p) d -> p (b t) d", p=P)
    out_tiles = out.rearrange("b (t p) d -> p (b t) d", p=P)
    parts_dram = nc.dram_tensor("qk_parts", (SEQS, 12, P, SEQ), BF16, kind="Internal").ap()

    with ExitStack() as ctx:
        def sb(name, shape, dt=F32):
            return ctx.enter_context(nc.sbuf_tensor(name, shape, dt))

        def sem(name):
            return ctx.enter_context(nc.semaphore(name))

        ps = ctx.enter_context(nc.psum_tensor("ps", [P, 8, 512], F32))

        xs = sb("xs", [P, TILES, D])
        moments = sb("moments", [P, TILES, 2])
        stats = sb("stats", [P, TILES, 6])
        shift_ln = sb("shift_ln", [P, TILES])
        moments_new = sb("moments_new", [P, 8, 2])
        rstd = sb("rstd", [P, TILES])
        std = sb("std", [P, TILES])
        eps = sb("eps", [P, 1])
        junk = sb("junk", [P, 16])
        ident = sb("ident", [P, P])
        ident_bf = sb("ident_bf", [P, P], BF16)
        future = sb("future", [P, P])
        future_bf = sb("future_bf", [P, 2, P], BF16)
        upto = sb("upto", [P, P])
        ones = sb("ones", [P, P])
        wqkv = sb("wqkv", [P, 3, 2 * D])
        wo_raw = sb("wo_raw", [P, 2, D])
        wo = sb("wo", [P, 2, D])
        rms_col = sb("rms_col", [P, 1])
        wb_raw = sb("wb_raw", [P, 4, D])
        wbT = sb("wbT", [P, 4, D])
        lam_in = sb("lam_in", [P, 4, HEADS * DH])
        lam_prod = sb("lam_prod", [P, 2, HEADS * DH])
        lam_sum = sb("lam_sum", [P, 2, HEADS])
        lam_exp = sb("lam_exp", [P, 2, HEADS])
        lam = sb("lam", [P, HEADS])
        logits = sb("logits", [P, 2, PRIMS])
        lg_negmax = sb("lg_negmax", [P, 2])
        lg_exp = sb("lg_exp", [P, 2, PRIMS])
        lg_sum = sb("lg_sum", [P, 2])
        lg_inv = sb("lg_inv", [P, 2])
        mix = sb("mix", [P, 2, PRIMS])
        mix_col = sb("mix_col", [P, 2, KR])
        w1 = sb("w1", [P, F])
        w2 = sb("w2", [P, FCH, D])
        values = sb("values", [P, TILES, HEADS, DV + 1])
        xn1 = sb("xn1", [P, 2, TPS, D])
        xnT1 = sb("xnT1", [P, 2, SEQ])
        qk_parts = sb("qk_parts_sb", [P, 2, 12, SEQ], BF16)
        qk_rest = sb("qk_rest", [P, 2, 2, 512])
        a1T = sb("a1T", [P, KR, P])
        a2T = sb("a2T", [P, 4, F])
        stack01 = sb("stack01", [P, 2, 2, GMAPS, SEQ], BF16)
        arena = sb("arena", [P, 20992])

        def carve(at, shape, dt=F32, parts=P):
            n = int(np.prod(shape))
            words = n if dt == F32 else n // 2
            ap = arena[0:parts, at:at + words]
            if dt != F32:
                ap = ap.bitcast(dt)
            names = "abcdef"[:len(shape)]
            if len(shape) > 1:
                ap = ap.rearrange(f"p ({' '.join(names)}) -> p {' '.join(names)}",
                                  **{k: s for k, s in zip(names[1:], shape[1:])})
            return ap, at + words

        a1, at = carve(0, (PRIMS * R,))
        b1, at = carve(at, (KR, F))
        a2, at = carve(at, (FCH, PRIMS, R))
        b2, at = carve(at, (KR, D))

        stack23, at = carve(0, (2, 2, GMAPS, SEQ), BF16)
        vaug, at = carve(at, (2, TPS, HEADS, DV + 1))
        probs, at = carve(at, (PROBS, BANKS_U, 512))
        ot_sb, at = carve(at, (2, SEQ))
        o_sb, at = carve(at, (2, TPS, MAPS, DV + 1))
        rowmax, at = carve(at, (2, TPS, GMAPS))
        shift, at = carve(at, (2, SHIFT_ROWS, SEQ), BF16, GMAPS)
        rden, at = carve(at, (TPS, MAPS))
        rden2, at = carve(at, (TPS, HEADS))
        o1, at = carve(at, (TPS, HEADS, DV))
        o2, at = carve(at, (TPS, HEADS, DV))
        o_n, at = carve(at, (TPS, HEADS, DV))
        msum, at = carve(at, (TPS * HEADS,))
        mrms, at = carve(at, (TPS * HEADS,))
        root_half, at = carve(at, (TPS * HEADS,))
        root_tmp, at = carve(at, (TPS * HEADS,))
        oT, at = carve(at, (TPS, 2, P))

        def q_stack(slot):
            return stack01[:, slot, 0] if slot < 2 else stack23[:, slot - 2, 0]

        def k_stack(slot):
            return stack01[:, slot, 1] if slot < 2 else stack23[:, slot - 2, 1]

        junk_columns = iter(range(16))

        def load_table(act, function):
            column = next(junk_columns)
            nc.scalar.activation(junk[:, column:column + 1], eps[:], function)

        def fill_stacks(pool, slot, filled, before):
            pair = float(np.array([0x3F803F80], np.uint32).view(np.float32)[0])
            q, k = (s.rearrange("p m t -> p (m t)").bitcast(F32) for s in (q_stack(slot), k_stack(slot)))
            nc.gpsimd.memset(q, 0.0).then_inc(filled, 1)
            nc.gpsimd.memset(k, pair).then_inc(filled, 1)
            pool.wait_ge(filled, before + 2)
            nc.gpsimd.memset(k[0:SROWS], 0.0).then_inc(filled, 1)

        x_in = [sem(f"x_in{i}") for i in range(4)]
        w_in = sem("w_in")
        tick_pool, tick_dve = sem("tick_pool"), sem("tick_dve")
        small_in = sem("small_in")
        rms_in = sem("rms_in")
        fc1_a_in, fc2_b_in = sem("fc1_a_in"), sem("fc2_b_in")
        fc1_b_in = [sem(f"fc1_b_in{i}") for i in range(4)]
        fc2_a_in = [sem(f"fc2_a_in{i}") for i in range(4)]
        consts = sem("consts")
        eps_done = sem("eps_done")
        stats_done = sem("stats_done")
        moments_done = sem("moments_done")
        std_done = sem("std_done")
        rstd_done = sem("rstd_done")
        xn_done = sem("xn_done")
        xT_done = sem("xT_done")
        xnT_done = sem("xnT_done")
        proj_done = sem("proj_done")
        high_done = sem("high_done")
        rest_done = sem("rest_done")
        mid_done = sem("mid_done")
        low_done = sem("low_done")
        v_done = sem("v_done")
        parts_out = [sem(f"parts_out{i}") for i in range(2)]
        stack_in = [sem(f"stack_in{i}") for i in range(4)]
        s_lg = sem("s_lg")
        s_lge = sem("s_lge")
        s_mix = sem("s_mix")
        s_lam = sem("s_lam")
        s_lame = sem("s_lame")
        wbT_ps = sem("wbT_ps")
        wbT_done = sem("wbT_done")
        wo_done = sem("wo_done")
        fT_ps = sem("fT_ps")
        fT_done = sem("fT_done")
        fT_done_act = sem("fT_done_act")
        acc_done = sem("acc_done")
        w12_done = sem("w12_done")

        def load_stack(eng, g, slot):
            half = slot % 2
            seq = (g - half) // 2 if isinstance(g, int) else g
            for t in range(TERMS):
                for side, part in ((0, Q_PART[t]), (1, K_PART[t])):
                    src = parts_dram[seq, 4 * part + 2 * side + half].rearrange("(m d) t -> d m t", d=DH)
                    dst = q_stack(slot) if side == 0 else k_stack(slot)
                    eng.dma_start(dst[DH * t:DH * (t + 1)], src).then_inc(stack_in[slot], 16)

        def carry_wait(eng, tick):
            eng.sem_inc(tick, 1)

        def token_moments(dve, tick, tile, n, stats_sem, aggr_sem, k, first=0, at=0):
            if past(k):
                dve.wait_ge(aggr_sem, first + 2 * k)
            carry_wait(dve, tick)
            for t in range(n):
                last = nc.vector.bn_stats(stats[:, at + t, :], xs[:, tile + t, :])
            last.then_inc(stats_sem, 1)
            dve.wait_ge(stats_sem, k + 1)
            carry_wait(dve, tick)
            for t in range(n):
                last = nc.vector.bn_aggr(moments_new[:, at + t, :], stats[:, at + t, :])
            last.then_inc(aggr_sem, 1)
            dve.wait_ge(aggr_sem, first + 2 * k + 1)
            nc.vector.tensor_scalar(moments[:, bass.ds(tile, n), :], moments_new[:, at:at + n, :], 1.0, None,
                                    op0=ALU.mult).then_inc(aggr_sem, 1)

        FGROUPS = 4 + KR

        with nc.Block() as block:
            @block.sync
            def _(sp):
                sp.dma_start(xs[:, 0:4, :], x_tiles[:, 0:4, :]).then_inc(x_in[0], 16)
                for i, w in enumerate((Wq, Wk, Wv)):
                    sp.dma_start(wqkv[:, i, :], w).then_inc(w_in, 16)
                for i in range(1, 4):
                    sp.dma_start(xs[:, 4 * i:4 * i + 4, :], x_tiles[:, 4 * i:4 * i + 4, :]).then_inc(x_in[i], 16)
                sp.dma_start(a1, fc1_A.rearrange("k d r -> d k r")).then_inc(fc1_a_in, 16)
                for i, w in enumerate((bWq, bWk, bWv, bWo)):
                    sp.dma_start(wb_raw[:, i, :], w).then_inc(small_in, 16)
                sp.dma_start(wo_raw[:, :, :], Wo.rearrange("(c p) n -> p c n", p=P)).then_inc(small_in, 16)
                for i, w in enumerate((lq1, lk1, lq2, lk2)):
                    sp.dma_start(lam_in[:, i, :],
                                 w.rearrange("h d -> (h d)").partition_broadcast(P)).then_inc(small_in, 16)
                for i, w in enumerate((fc1_logits, fc2_logits)):
                    sp.dma_start(logits[:, i, :], w.partition_broadcast(P)).then_inc(small_in, 16)
                for i in range(P // DV):
                    sp.dma_start(rms_col[DV * i:DV * (i + 1), :],
                                 rms_scale.rearrange("(p a) -> p a", a=1)).then_inc(rms_in, 16)

                def load_fc1_b(quarter):
                    c = KR // 4 * quarter
                    sp.dma_start(b1[:, c:c + KR // 4], fc1_B.rearrange("k r f -> (k r) f")
                                 .rearrange("(c p) f -> p c f", p=P)[:, c:c + KR // 4])\
                      .then_inc(fc1_b_in[quarter], 16)

                def load_fc2_a(quarter):
                    c = slice(PRIMS // 4 * quarter, PRIMS // 4 * (quarter + 1))
                    for j in range(FCH):
                        sp.dma_start(a2[:, j, c], fc2_A[c, j * P:(j + 1) * P].rearrange("k p r -> p k r"))\
                          .then_inc(fc2_a_in[quarter], 16)

                load_fc1_b(0)
                for b in range(SEQS):
                    sp.wait_ge(low_done, 2 * b + 2)
                    sp.dma_start(parts_dram[b].rearrange("c p t -> p c t"), qk_parts[:, b % 2])\
                      .then_inc(parts_out[b % 2], 16)
                    if b < 3:
                        load_fc1_b(1 + b)
                    if b == 4:
                        sp.dma_start(b2, fc2_B.rearrange("k r f -> (k r) f").rearrange("(c p) f -> p c f", p=P))\
                          .then_inc(fc2_b_in, 16)
                    if b == 5:
                        load_fc2_a(0)
                for quarter in range(1, 4):
                    load_fc2_a(quarter)
                for u in range(2):
                    sp.wait_ge(parts_out[u], 16 * SEQS // 2)
                sp.wait_ge(consts, 12)
                for g in range(2):
                    load_stack(sp, g, g)

            @block.gpsimd
            def _(pool):
                nc.gpsimd.memset(eps[:], LN_EPS).then_inc(eps_done, 1)
                nc.gpsimd.memset(ident[:], 0.0).then_inc(consts, 1)
                pool.wait_ge(consts, 1)
                nc.gpsimd.affine_select(out=ident[:], in_=ident[:], compare_op=ALU.not_equal, fill=1.0,
                                        base=0, pattern=[[-1, P]], channel_multiplier=1).then_inc(consts, 1)
                nc.gpsimd.memset(upto[:], 1.0)
                nc.gpsimd.memset(ones[:], 1.0)
                nc.gpsimd.memset(future[:], 0.0)
                nc.gpsimd.memset(future_bf[:], 0.0).then_inc(consts, 1)
                pool.wait_ge(consts, 3)
                nc.gpsimd.affine_select(out=upto[:], in_=upto[:], compare_op=ALU.is_ge, fill=0.0,
                                        base=0, pattern=[[1, P]], channel_multiplier=-1).then_inc(consts, 1)
                nc.gpsimd.affine_select(out=future_bf[:], in_=future_bf[:], compare_op=ALU.is_ge, fill=NEG,
                                        base=0, pattern=[[0, 2], [-1, P]], channel_multiplier=1)
                nc.gpsimd.affine_select(out=future[:], in_=future[:], compare_op=ALU.is_ge, fill=NEG,
                                        base=0, pattern=[[-1, P]], channel_multiplier=1).then_inc(consts, 1)
                nc.gpsimd.tensor_copy(ident_bf[:], ident[:]).then_inc(consts, 1)
                nc.gpsimd.memset(values[:, :, :, DV], 1.0)
                for slot in range(2):
                    fill_stacks(pool, slot, consts, 6 + 3 * slot)
                def turn(it):
                    for u in range(2):
                        for side in range(2):
                            pool.wait_ge(mid_done, 2 * (2 * it + u) + side + 1)
                            nc.gpsimd.tensor_tensor(
                                qk_parts[:, u, 8 + 2 * side:10 + 2 * side, :].rearrange("p c t -> p (c t)"),
                                qk_rest[:, u, side, :],
                                qk_parts[:, u, 4 + 2 * side:6 + 2 * side, :].rearrange("p c t -> p (c t)"),
                                op=ALU.subtract).then_inc(low_done, 1)

                repeat(pool, SEQS // 2, turn)

            @block.scalar
            def _(act):
                act.wait_ge(eps_done, 1)
                load_table(act, ACT.Sqrt)
                for i in range(4):
                    c = slice(4 * i, 4 * i + 4)
                    act.wait_ge(moments_done, 4 * i + 4)
                    nc.scalar.activation(std[:, c], moments[:, c, 1], ACT.Sqrt, bias=eps[:, 0:1]).then_inc(std_done, 1)
                load_table(act, ACT.Exp)
                def turn(it):
                    for u in range(2):
                        b = 2 * it + u
                        act.wait_ge(xT_done, b + 1)
                        nc.scalar.copy(xnT1[:, u, :], ps[:, 4 * u, 0:SEQ]).then_inc(xnT_done, 1)
                    for u in range(2):
                        b = 2 * it + u
                        if past(it):
                            act.wait_ge(parts_out[u], 16 * it)
                        for side in range(2):
                            act.wait_ge(proj_done, 3 * b + side + 1)
                            nc.scalar.copy(
                                qk_parts[:, u, 2 * side:2 * side + 2, :].rearrange("p c t -> p (c t)"),
                                ps[:, 4 * u + 1 + side, :]).then_inc(high_done, 1)
                        act.wait_ge(proj_done, 3 * b + 3)
                        for t in range(TPS):
                            last = nc.scalar.copy(values[:, TPS * b + t, :, 0:DV],
                                                  ps[:, 4 * u + 3, t * 256:(t + 1) * 256]
                                                  .rearrange("p (h d) -> p h d", h=HEADS))
                        last.then_inc(v_done, 1)

                turn(0)
                for i in range(2):
                    act.wait_ge(s_lg, 2)
                    nc.scalar.activation(lg_exp[:, i, :], logits[:, i, :], ACT.Exp, bias=lg_negmax[:, i:i + 1],
                                         accum_out=lg_sum[:, i:i + 1]).then_inc(s_lge, 1)
                act.wait_ge(s_lam, 2)
                nc.scalar.activation(lam_exp[:], lam_sum[:], ACT.Exp).then_inc(s_lame, 1)
                with act.Fori(1, SEQS // 2) as it:
                    turn(it)
                act.wait_ge(wbT_ps, 1)
                nc.scalar.copy(wbT[:].rearrange("p a b -> p (a b)"), ps[:, 4, :]).then_inc(wbT_done, 1)
                act.wait_ge(s_mix, 7)
                for i in range(5, FGROUPS, 2):
                    act.wait_ge(fT_ps, i + 1)
                    if i >= 8:
                        act.wait_ge(acc_done, i - 3)
                    nc.scalar.activation(a2T[:, (i - 4) % 4, :], ps[:, i % 2, :], ACT.Copy,
                                         scale=mix_col[:, 1, i - 4:i - 3]).then_inc(fT_done_act, 1)
                act.wait_ge(acc_done, FGROUPS)
                nc.scalar.copy(w2[:].rearrange("p a b -> p (a b)"), ps[:, 3, :]).then_inc(w12_done, 1)

            @block.vector
            def _(dve):
                def first_moments(i):
                    dve.wait_ge(x_in[i], 16)
                    for t in range(4 * i, 4 * i + 4):
                        nc.vector.bn_stats(stats[:, t, :], xs[:, t, :]).then_inc(stats_done, 1)
                    dve.wait_ge(stats_done, 4 * i + 4)
                    for t in range(4 * i, 4 * i + 4):
                        nc.vector.bn_aggr(moments[:, t, :], stats[:, t, :]).then_inc(moments_done, 1)

                def first_rstd(i):
                    c = slice(4 * i, 4 * i + 4)
                    dve.wait_ge(std_done, i + 1)
                    nc.vector.reciprocal(rstd[:, c], std[:, c]).then_inc(rstd_done, 1)

                def rows(it):
                    dve.wait_ge(rstd_done, it + 1)
                    if past(it):
                        dve.wait_ge(xT_done, 2 * it)
                    for u in range(2):
                        for t in range(TPS):
                            tile = 2 * (2 * it + u) + t
                            last = nc.vector.tensor_scalar(xn1[:, u, t, :], xs[:, tile, :],
                                                           moments[:, tile, 0:1], rstd[:, bass.ds(tile, 1)],
                                                           op0=ALU.subtract, op1=ALU.mult)
                        last.then_inc(xn_done, 1)

                def split(it, u):
                    b = 2 * it + u
                    for side in range(2):
                        dve.wait_ge(high_done, 2 * b + side + 1)
                        if past(b):
                            dve.wait_ge(low_done, 2 * b)
                        nc.vector.tensor_tensor(
                            qk_rest[:, u, side, :], ps[:, 4 * u + 1 + side, :],
                            qk_parts[:, u, 2 * side:2 * side + 2, :].rearrange("p c t -> p (c t)"),
                            op=ALU.subtract).then_inc(rest_done, 1)
                    for side in range(2):
                        dve.wait_ge(rest_done, 2 * b + side + 1)
                        nc.vector.tensor_copy(
                            qk_parts[:, u, 4 + 2 * side:6 + 2 * side, :].rearrange("p c t -> p (c t)"),
                            qk_rest[:, u, side, :]).then_inc(mid_done, 1)

                first_moments(0)
                first_rstd(0)
                rows(0)
                first_moments(1)
                first_moments(2)
                first_moments(3)
                for i in range(1, 4):
                    first_rstd(i)
                split(0, 0)
                dve.wait_ge(small_in, 16 * 11)
                for i in range(2):
                    nc.vector.tensor_reduce(out=lg_negmax[:, i:i + 1], in_=logits[:, i, :], axis=AX, op=ALU.max,
                                            negate=True).then_inc(s_lg, 1)
                for i in range(2):
                    nc.vector.tensor_tensor(lam_prod[:, i, :], lam_in[:, 2 * i, :], lam_in[:, 2 * i + 1, :],
                                            op=ALU.mult).then_inc(s_mix, 1)
                for i in range(2):
                    dve.wait_ge(s_mix, i + 1)
                    nc.vector.tensor_reduce(out=lam_sum[:, i, :],
                                            in_=lam_prod[:, i, :].rearrange("p (h d) -> p h d", d=DH),
                                            axis=AX, op=ALU.add).then_inc(s_lam, 1)
                dve.wait_ge(s_lge, 2)
                nc.vector.reciprocal(lg_inv[:], lg_sum[:]).then_inc(s_mix, 1)
                dve.wait_ge(s_mix, 3)
                for i in range(2):
                    nc.vector.tensor_scalar(mix[:, i, :], lg_exp[:, i, :], lg_inv[:, i:i + 1], None,
                                            op0=ALU.mult).then_inc(s_mix, 1)
                dve.wait_ge(s_mix, 5)
                for k in range(2):
                    half = slice(64 * k, 64 * k + 64)
                    nc.vector.tensor_copy(mix_col[half], mix[half].rearrange("p i (c k) -> p i c k", k=2)[:, :, :, k])\
                        .then_inc(s_mix, 1)
                dve.wait_ge(s_lame, 1)
                nc.vector.scalar_tensor_tensor(out=lam[:], in0=lam_exp[:, 0, :], scalar=LAMBDA_INIT,
                                               in1=lam_exp[:, 1, :], op0=ALU.add, op1=ALU.subtract)\
                    .then_inc(s_lam, 1)
                dve.wait_ge(rms_in, 16 * P // DV)
                nc.vector.tensor_scalar(wo[:], wo_raw[:], rms_col[:, 0:1], 1.0 - LAMBDA_INIT,
                                        op0=ALU.mult, op1=ALU.mult).then_inc(wo_done, 1)
                with dve.Fori(1, SEQS // 2) as it:
                    rows(it)
                    split(it - 1, 1)
                    split(it, 0)
                split(SEQS // 2 - 1, 1)
                dve.wait_ge(s_mix, 7)
                for i in [0, 1, 2, 3] + list(range(4, FGROUPS, 2)):
                    dve.wait_ge(fT_ps, i + 1)
                    if i < 4:
                        nc.vector.tensor_tensor(
                            a1T[:, 4 * i:4 * i + 4, :], ps[:, i % 2, :].rearrange("p (c d) -> p c d", c=4),
                            mix_col[:, 0, 4 * i:4 * i + 4].unsqueeze(2).to_broadcast([P, 4, P]),
                            op=ALU.mult).then_inc(fT_done, 1)
                    else:
                        if i >= 8:
                            dve.wait_ge(acc_done, i - 3)
                        nc.vector.tensor_scalar(a2T[:, (i - 4) % 4, :], ps[:, i % 2, :],
                                                mix_col[:, 1, i - 4:i - 3], None,
                                                op0=ALU.mult).then_inc(fT_done, 1)
                dve.wait_ge(acc_done, 4)
                nc.vector.tensor_copy(w1[:], ps[:, 2, :]).then_inc(w12_done, 1)

            @block.tensor
            def _(pe):
                pe.wait_ge(consts, 2)
                pe.wait_ge(w_in, 16 * 3)
                def turn(it):
                    for u in range(2):
                        b = 2 * it + u
                        pe.wait_ge(xn_done, b + 1)
                        if past(it):
                            pe.wait_ge(xnT_done, 2 * it - 1 + u)
                        for t in range(TPS):
                            last = nc.tensor.transpose(ps[:, 4 * u, t * P:(t + 1) * P], xn1[:, u, t, :], ident[:])
                        last.then_inc(xT_done, 1)
                    for u in range(2):
                        b = 2 * it + u
                        pe.wait_ge(xnT_done, b + 1)
                        if past(it):
                            pe.wait_ge(rest_done, 4 * it - 2 + 2 * u)
                        for side in range(2):
                            for c in range(2):
                                last = nc.tensor.matmul(ps[:, 4 * u + 1 + side, c * SEQ:(c + 1) * SEQ],
                                                        wqkv[:, side, c * P:(c + 1) * P], xnT1[:, u, :],
                                                        start=True, stop=True)
                            last.then_inc(proj_done, 1)
                        if past(it):
                            pe.wait_ge(v_done, 2 * it - 1 + u)
                        for t in range(TPS):
                            last = nc.tensor.matmul(ps[:, 4 * u + 3, t * 256:(t + 1) * 256],
                                                    xnT1[:, u, t * P:(t + 1) * P], wqkv[:, 2, :],
                                                    start=True, stop=True)
                        last.then_inc(proj_done, 1)

                repeat(pe, SEQS // 2, turn)
                pe.wait_ge(xnT_done, SEQS)
                pe.wait_ge(rest_done, 2 * SEQS - 2)
                pe.wait_ge(v_done, SEQS - 1)
                pe.wait_ge(small_in, 16 * 11)
                for i in range(4):
                    last = nc.tensor.transpose(ps[:, 4, i * P:(i + 1) * P], wb_raw[:, i, :], ident[:])
                last.then_inc(wbT_ps, 1)

                def factor_transposes(i):
                    if i >= 2:
                        if i - 2 < 4 or i % 2 == 0:
                            pe.wait_ge(fT_done, min(i - 1, 4) + max(0, (i - 2 - 4) // 2 + 1))
                        else:
                            pe.wait_ge(fT_done_act, (i - 2 - 5) // 2 + 1)
                    for j in range(4):
                        if i < 4:
                            c = 4 * i + j
                            src = a1[:, c * P:(c + 1) * P]
                        else:
                            src = a2[:, j, 2 * (i - 4):2 * (i - 3)].rearrange("p k r -> p (k r)")
                        last = nc.tensor.transpose(ps[:, i % 2, j * P:(j + 1) * P], src, ident[:])
                    last.then_inc(fT_ps, 1)

                def factor_products(i):
                    if i < 4 or i % 2 == 0:
                        pe.wait_ge(fT_done, min(i + 1, 4) + max(0, (i - 4) // 2 + 1))
                    else:
                        pe.wait_ge(fT_done_act, (i - 5) // 2 + 1)
                    for j in range(4):
                        if i < 4:
                            c = 4 * i + j
                            last = nc.tensor.matmul(ps[:, 2, :], a1T[:, c, :], b1[:, c, :],
                                                    start=(c == 0), stop=(c == KR - 1))
                        else:
                            c = i - 4
                            last = nc.tensor.matmul(ps[:, 3, j * P:(j + 1) * P], a2T[:, c % 4, j * P:(j + 1) * P],
                                                    b2[:, c, :], start=(c == 0 and j == 0),
                                                    stop=(c == KR - 1), skip_group_check=True)
                    last.then_inc(acc_done, 1)

                for i in range(FGROUPS + 2):
                    if i == 0:
                        pe.wait_ge(fc1_a_in, 16)
                    if 2 <= i < 6:
                        pe.wait_ge(fc1_b_in[i - 2], 16)
                    if i >= 4 and (i - 4) % 4 == 0 and i < FGROUPS:
                        pe.wait_ge(fc2_a_in[(i - 4) // 4], 16 * FCH)
                    if i == 6:
                        pe.wait_ge(fc2_b_in, 16)
                    if i < FGROUPS:
                        factor_transposes(i)
                    if i >= 2:
                        factor_products(i - 2)

        filled_23 = sem("filled_23")
        vaug_done = sem("vaug_done")
        cleared = sem("cleared")
        shift_in = [sem(f"shift_in{i}") for i in range(4)]
        scored = sem("scored")
        maxed = sem("maxed")
        maxT_done = sem("maxT_done")
        shift_hi = sem("shift_hi")
        shift_lo = sem("shift_lo")
        scoredT = sem("scoredT")
        exp_done = sem("exp_done")
        masked = sem("masked")
        pv_done = sem("pv_done")
        ot_copied = sem("ot_copied")
        ott_done = sem("ott_done")
        o_copied = sem("o_copied")
        rden_done = sem("rden_done")
        post = sem("post")
        sq_done = sem("sq_done")
        ms_raw = sem("ms_raw")
        ms_done = sem("ms_done")
        normed = sem("normed")
        nT_done = sem("nT_done")
        oT_done = sem("oT_done")
        oproj_done = sem("oproj_done")
        resid_done = sem("resid_done")
        st2_done = sem("st2_done")
        mom2_done = sem("mom2_done")
        root = sem("root")

        S_BANK, T_BANK, O_BANK, M_BANK = 0, 3, 5, 7

        TAIL = UPS + 1
        TAIL_OUT = L_OPT - UPS

        def turns(eng, emit, amid):
            for j in range(SLOTS):
                emit(0, j)
            with eng.Fori(1, UNITS // SLOTS) as it:
                for j in range(SLOTS):
                    emit(it, j)
            for j in range(L_STAT - UPS + 1):
                amid(j)
                emit(UNITS // SLOTS, j)

        def unit(it, j, lag):
            return SLOTS * it + j - lag

        def group(it, j, lag):
            return (SLOTS // UPG) * it + (j - lag) // UPG

        def seq(it, j, lag):
            return (SLOTS // UPS) * it + (j - lag) // UPS

        def shifts_before(it, j):
            return (SLOTS // UPG) * it + (j - L_SHIFT - 1) // UPG + 1

        def attend_sync(sp):
            sp.wait_ge(filled_23, 3)
            load_stack(sp, 2, 2)

            def store_shift(g, slot):
                sp.wait_ge(shift_lo, g + 1)
                for part in range(SHIFT_ROWS):
                    sp.dma_start(q_stack(slot)[SROWS + part:SROWS + part + 1], shift[:, slot % 2, part, :])\
                      .then_inc(shift_in[slot], 16)

            store_shift(0, 0)
            sp.wait_ge(filled_23, 6)
            load_stack(sp, 3, 3)
            with sp.Fori(0, GROUPS // 4 - 1) as it:
                for k in range(4):
                    g = 4 * it + k
                    store_shift(g + 1, (k + 1) % 4)
                    sp.wait_ge(scoredT, BANKS_U * UPG * (g + 1))
                    load_stack(sp, 2 * (it + 1) + k // 2, k)
            for g in range(GROUPS - 4, GROUPS - 1):
                store_shift(g + 1, (g + 1) % 4)

        def attend_gpsimd(pool, amid):
            def normalise(it, j):
                b = seq(it, j, L_NORM)
                if (j - L_NORM) % UPS == 0 and live(b, SEQS):
                    pool.wait_ge(root, FIRST + ROOT_STEPS * (b + 1))
                    nc.gpsimd.tensor_tensor(
                        o_n.rearrange("p t h d -> p (t h) d"), o1.rearrange("p t h d -> p (t h) d"),
                        mrms.unsqueeze(2).to_broadcast([P, TPS * HEADS, DV]),
                        op=ALU.mult).then_inc(normed, 1)

            for started in (post, normed):
                pool.sem_inc(started, FIRST)
            for slot in (2, 3):
                fill_stacks(pool, slot, filled_23, 3 * (slot - 2))

            def emit(it, j):
                n = unit(it, j, L_EXP)
                if live(n, UNITS):
                    r = (j - L_EXP) % PROBS
                    for s in range(BANKS_U):
                        pool.wait_ge(exp_done, BANKS_U * n + s + 1)
                        carry_wait(pool, tick_pool)
                        if s < 2:
                            diag = probs[:, r, s, :].rearrange("p (m q) -> p m q", m=2)[:, :, 0:P]
                        else:
                            diag = probs[:, r, s, :].rearrange("p (m q) -> p m q", m=UMAPS)
                        nc.gpsimd.affine_select(out=diag, in_=diag, compare_op=ALU.is_ge, fill=0.0, base=0,
                                                pattern=[[0, 2 if s < 2 else UMAPS], [1, P]],
                                                channel_multiplier=-1).then_inc(masked, 1)
                        if s == 1:
                            normalise(it, j)
                else:
                    normalise(it, j)
                b = seq(it, j, L_DEN)
                if (j - L_DEN) % UPS == 0 and live(b, SEQS):
                    v = (j - L_DEN) // UPS % 2
                    num = o_sb[:, v].rearrange("p t (h c) d -> p (t h) c d", c=2)
                    inv = rden.rearrange("p t (h c) -> p (t h) c", c=2)
                    pool.wait_ge(rden_done, b + 1)
                    if past(b):
                        pool.wait_ge(post, FIRST + 4 * b)
                        pool.wait_ge(normed, FIRST + b)
                    nc.gpsimd.tensor_tensor(rden2, rden.rearrange("p t (h c) -> p t h c", c=2)[:, :, :, 1],
                                            lam[:].unsqueeze(1).to_broadcast([P, TPS, HEADS]),
                                            op=ALU.mult).then_inc(post, 1)
                    nc.gpsimd.tensor_tensor(o1.rearrange("p t h d -> p (t h) d"), num[:, :, 0, 0:DV],
                                            inv[:, :, 0:1].to_broadcast([P, TPS * HEADS, DV]),
                                            op=ALU.mult).then_inc(post, 1)
                b = seq(it, j, L_DIFF)
                if (j - L_DIFF) % UPS == 0 and live(b, SEQS):
                    v = (j - L_DIFF) // UPS % 2
                    num = o_sb[:, v].rearrange("p t (h c) d -> p (t h) c d", c=2)
                    pool.wait_ge(post, FIRST + 4 * b + 1)
                    nc.gpsimd.tensor_tensor(
                        o2.rearrange("p t h d -> p (t h) d"), num[:, :, 1, 0:DV],
                        rden2.rearrange("p t h -> p (t h)").unsqueeze(2).to_broadcast([P, TPS * HEADS, DV]),
                        op=ALU.mult).then_inc(post, 1)
                    pool.wait_ge(post, FIRST + 4 * b + 3)
                    nc.gpsimd.tensor_tensor(o1, o1, o2, op=ALU.subtract).then_inc(post, 1)

            turns(pool, emit, amid)

        def attend_scalar(act, amid):
            def emit(it, j):
                n = unit(it, j, L_EXP)
                g = group(it, j, L_SHIFT)
                if live(n, UNITS):
                    r = (j - L_EXP) % PROBS
                    if past(n - PROBS + 1):
                        act.wait_ge(pv_done, n - PROBS + 1)
                    for s in range(BANKS_U):
                        act.wait_ge(scoredT, BANKS_U * n + s + 1)
                        bank = T_BANK + (j - L_EXP + s) % 2
                        nc.scalar.activation(probs[:, r, s, :], ps[:, bank, :], ACT.Exp,
                                             scale=SCALE).then_inc(exp_done, 1)
                        if s == 0 and (j - L_SHIFT) % UPG == 0 and live(g, GROUPS):
                            shift_high(it, j)
                        if s == 0:
                            squares(it, j)
                if not live(n, UNITS) and (j - L_SHIFT) % UPG == 0 and live(g, GROUPS):
                    shift_high(it, j)
                if not live(n, UNITS):
                    squares(it, j)
                n = unit(it, j, L_PV)
                if live(n, UNITS):
                    r = (j - L_PV) % 2
                    act.wait_ge(pv_done, n + 1)
                    if past(n - 1):
                        act.wait_ge(ott_done, n - 1)
                    nc.scalar.copy(ot_sb[:, r, :], ps[:, O_BANK + r, 0:SEQ]).then_inc(ot_copied, 1)
                n = unit(it, j, L_OT)
                if live(n, UNITS):
                    u, v = (j - L_OT) % UPS, (j - L_OT) // UPS % 2
                    act.wait_ge(ott_done, n + 1)
                    b = seq(it, j, L_OT)
                    if u == 0 and past(b - 1):
                        act.wait_ge(post, FIRST + 4 * (b - 1))
                    src = ps[:, M_BANK, 0:TPS * P].rearrange("p (t m d) -> p t m d", t=TPS, m=UMAPS)
                    nc.scalar.copy(o_sb[:, v, :, UMAPS * u:UMAPS * u + UMAPS, :],
                                   src[:, :, :, 0:DV + 1]).then_inc(o_copied, 1)
                columns(it, j)
                b = seq(it, j, L_VAUG)
                if (j - L_VAUG) % UPS == 0 and live(b, SEQS):
                    if past(b - 1):
                        act.wait_ge(pv_done, UPS * (b - 1))
                    nc.scalar.copy(vaug[:, (j - L_VAUG) // UPS % 2].rearrange("p t h d -> p t (h d)"),
                                   values[:, bass.ds(TPS * b, TPS), :, :].rearrange("p t h d -> p t (h d)"))\
                        .then_inc(vaug_done, 1)

            def squares(it, j):
                b = seq(it, j, L_SQ)
                if (j - L_SQ) % UPS == 0 and live(b, SEQS):
                    act.wait_ge(post, FIRST + 4 * b + 4)
                    if past(b):
                        act.wait_ge(nT_done, FIRST + b)
                    nc.scalar.activation(o_n.rearrange("p t h d -> p (t h d)"),
                                         o1.rearrange("p t h d -> p (t h d)"), ACT.Square).then_inc(sq_done, 1)

            def columns(it, j):
                b = seq(it, j, L_OPT)
                if (j - L_OPT) % UPS == 0 and live(b, SEQS):
                    act.wait_ge(nT_done, FIRST + b + 1)
                    nc.scalar.copy(oT.rearrange("p a b c -> p (a b c)"), ps[:, M_BANK, :])\
                        .then_inc(oT_done, 1)

            def shift_high(it, j):
                g, k = group(it, j, L_SHIFT), (j - L_SHIFT) // UPG
                act.wait_ge(maxT_done, g + 1)
                if past(g - 1):
                    act.wait_ge(shift_in[(k - 2) % 4], 32 * (it + (k - 2) // 4 + 1))
                nc.scalar.activation(shift[:, k % 2, 0, :], ps[0:GMAPS, M_BANK, 0:SEQ], ACT.Copy,
                                     scale=-1.0).then_inc(shift_hi, 1)

            turns(act, emit, amid)

        def attend_vector(dve, amid):
            for started in (ms_raw, resid_done, mom2_done, root):
                dve.sem_inc(started, FIRST)
            nc.vector.memset(ps[:, O_BANK:O_BANK + 2, 0:SEQ], 0.0).then_inc(cleared, 1)

            def shift_low(it, j):
                g = group(it, j, L_SHIFT)
                if (j - L_SHIFT) % UPG == 0 and live(g, GROUPS):
                    k = (j - L_SHIFT) // UPG
                    dve.wait_ge(shift_hi, g + 1)
                    nc.vector.scalar_tensor_tensor(
                        out=shift[:, k % 2, 1, :], in0=ps[0:GMAPS, M_BANK, 0:SEQ], scalar=-1.0,
                        in1=shift[:, k % 2, 0, :], op0=ALU.mult, op1=ALU.subtract).then_inc(shift_lo, 1)

            def residual(it, j):
                b = seq(it, j, L_OPROJ)
                if (j - L_OPROJ) % UPS == 0 and live(b, SEQS):
                    dve.wait_ge(oproj_done, b + 1)
                    x2 = xs[:, bass.ds(2 * b, 2), :].rearrange("p t d -> p (t d)")
                    nc.vector.tensor_tensor(x2, ps[:, M_BANK, 0:TPS * D], x2, op=ALU.add)\
                        .then_inc(resid_done, 1)

            def mean_squares(it, j):
                b = seq(it, j, L_MS)
                if (j - L_MS) % UPS == 0 and live(b, SEQS):
                    dve.wait_ge(sq_done, b + 1)
                    if past(b):
                        dve.wait_ge(root, FIRST + ROOT_STEPS * b)
                    nc.vector.tensor_reduce(out=msum, in_=o_n.rearrange("p t h d -> p (t h) d"), axis=AX,
                                            op=ALU.add).then_inc(ms_raw, 1)
                    dve.wait_ge(ms_raw, FIRST + b + 1)
                    nc.vector.tensor_scalar(msum, msum, 1.0 / DV, RMS_EPS, op0=ALU.mult,
                                            op1=ALU.add).then_inc(ms_done, 1)

            def root_step(it, j, point):
                for step in range(ROOT_STEPS):
                    at = 2 + step
                    lag = L_MS + at // POINTS
                    b = seq(it, j, lag)
                    if at % POINTS != point or (j - lag) % UPS or not live(b, SEQS):
                        continue
                    dve.wait_ge(root, FIRST + ROOT_STEPS * b + step)
                    if step == 0:
                        dve.wait_ge(ms_done, b + 1)
                        nc.vector.tensor_scalar(root_half, msum, -0.5, None, op0=ALU.mult)
                        last = nc.vector.tensor_scalar(root_tmp.bitcast(I32), msum.bitcast(I32), 1, None,
                                                       op0=ALU.logical_shift_right)
                    elif step == 1:
                        if past(b):
                            dve.wait_ge(normed, FIRST + b)
                        last = nc.vector.tensor_scalar(mrms.bitcast(I32), root_tmp.bitcast(I32), -1.0,
                                                       float(ROOT_SEED), op0=ALU.mult, op1=ALU.add)
                    elif (step - ROOT_FIRST) % 3 == 0:
                        last = nc.vector.tensor_tensor(root_tmp, mrms, mrms, op=ALU.mult)
                    elif (step - ROOT_FIRST) % 3 == 1:
                        last = nc.vector.tensor_tensor(root_tmp, root_tmp, root_half, op=ALU.mult)
                    else:
                        last = nc.vector.scalar_tensor_tensor(out=mrms, in0=root_tmp, scalar=1.5, in1=mrms,
                                                              op0=ALU.add, op1=ALU.mult)
                    last.then_inc(root, 1)

            def emit(it, j):
                n = unit(it, j, 0)
                if live(n, UNITS):
                    uu, gs = j % UPG, j // UPG % 2
                    for s in range(BANKS_U):
                        bank = S_BANK + s
                        dve.wait_ge(scored, BANKS_U * n + s + 1)
                        if s == 0:
                            carry_wait(dve, tick_dve)
                            for m in range(UMAPS):
                                block = ps[:, bank, m * P:(m + 1) * P]
                                at = UMAPS * uu + m
                                last = nc.vector.tensor_tensor_reduce(
                                    out=block, in0=block, in1=future[:], scale=1.0, scalar=LOWEST, op0=ALU.add,
                                    op1=ALU.max, accum_out=rowmax[:, gs, 0, at:at + 1])
                        else:
                            at = UMAPS * uu + 2 * s - 2
                            last = nc.vector.tensor_reduce(
                                out=rowmax[:, gs, 1, at:at + 2], in_=ps[:, bank, :].rearrange("p (m k) -> p m k", m=2),
                                axis=AX, op=ALU.max)
                        last.then_inc(maxed, 1)
                        if s == 0:
                            shift_low(it, j)
                            residual(it, j)
                        if s == 1:
                            mean_squares(it, j)
                        root_step(it, j, s)
                else:
                    shift_low(it, j)
                    residual(it, j)
                    mean_squares(it, j)
                    for s in range(BANKS_U):
                        root_step(it, j, s)
                b = seq(it, j, L_DEN)
                if (j - L_DEN) % UPS == 0 and live(b, SEQS):
                    v = (j - L_DEN) // UPS % 2
                    dve.wait_ge(o_copied, UPS * (b + 1))
                    if past(b):
                        dve.wait_ge(post, FIRST + 4 * b)
                    nc.vector.reciprocal(rden, o_sb[:, v, :, :, DV]).then_inc(rden_done, 1)
                root_step(it, j, POINTS - 1)
                b = seq(it, j, L_STAT)
                if (j - L_STAT) % UPS == 0 and live(b, SEQS):
                    dve.wait_ge(resid_done, FIRST + b + 1)
                    token_moments(dve, tick_dve, TPS * b, TPS, st2_done, mom2_done, b, FIRST)

            turns(dve, emit, amid)

        def attend_tensor(pe, amid):
            pe.sem_inc(nT_done, FIRST)

            def score_bank(it, j, s):
                n = unit(it, j, 0)
                slot, m0 = j // UPG % 4, UMAPS * (j % UPG)
                q, k = q_stack(slot), k_stack(slot)
                bank = ps[:, S_BANK + s, :]
                if s == 0 and j % UPG == 0:
                    pe.wait_ge(stack_in[slot], 2 * TERMS * 16 * (it + 1))
                if past(n):
                    pe.wait_ge(maxed, BANKS_U * (n - 1) + s + 1)
                if s == 0:
                    for m in range(UMAPS):
                        last = nc.tensor.matmul(bank[:, m * P:(m + 1) * P], q[0:SROWS, m0 + m, 0:P],
                                                k[0:SROWS, m0 + m, 0:P], start=True, stop=True)
                    last.then_inc(scored, 1)
                else:
                    for m in range(2):
                        nc.tensor.matmul(bank[:, m * SEQ:(m + 1) * SEQ], q[0:SROWS, m0 + 2 * s - 2 + m, P:SEQ],
                                         k[0:SROWS, m0 + 2 * s - 2 + m, :], start=(m == 0), stop=False,
                                         skip_group_check=True)
                    nc.tensor.matmul(bank.rearrange("p (m k) -> p m k", m=2)[:, :, P:SEQ], ident_bf[:],
                                     future_bf[:], start=False, stop=True,
                                     skip_group_check=True).then_inc(scored, 1)

            def shifted_bank(it, j, s):
                n = unit(it, j, L_EXP)
                jj = j - L_EXP
                slot, m0 = jj // UPG % 4, UMAPS * (jj % UPG)
                q, k = q_stack(slot), k_stack(slot)
                bank = ps[:, T_BANK + (jj + s) % 2, :]
                if s == 0 and jj % UPG == 0:
                    pe.wait_ge(shift_in[slot], 32 * (it + jj // SLOTS + 1))
                if past(BANKS_U * n + s - 1):
                    pe.wait_ge(exp_done, BANKS_U * n + s - 1)
                if s < 2:
                    for m in range(2):
                        last = nc.tensor.matmul(bank[:, m * SEQ:(m + 1) * SEQ], k[0:XROWS, m0 + 2 * s + m, 0:P],
                                                q[0:XROWS, m0 + 2 * s + m, :], start=True, stop=True)
                else:
                    for m in range(UMAPS):
                        last = nc.tensor.matmul(bank[:, m * P:(m + 1) * P], k[0:XROWS, m0 + m, P:SEQ],
                                                q[0:XROWS, m0 + m, P:SEQ], start=True, stop=True)
                last.then_inc(scoredT, 1)

            def weigh_values(it, j, t):
                n = unit(it, j, L_PV)
                jj = j - L_PV
                p, r, v = jj % PROBS, jj % 2, jj // UPS % 2
                if t == 0:
                    pe.wait_ge(masked, BANKS_U * (n + 1))
                    if jj % UPS == 0:
                        pe.wait_ge(vaug_done, seq(it, j, L_PV) + 1)
                    if past(n - 1):
                        pe.wait_ge(ot_copied, n - 1)
                for m in range(UMAPS):
                    head = 2 * (jj % UPS) + m // 2
                    if t == 0:
                        nc.tensor.matmul(ps[32 * m:32 * m + DV + 1, O_BANK + r, 0:SEQ], vaug[:, v, 0, head, :],
                                         probs[:, p, m // 2, m % 2 * SEQ:m % 2 * SEQ + SEQ],
                                         start=True, stop=False, skip_group_check=True)
                    else:
                        last = nc.tensor.matmul(ps[32 * m:32 * m + DV + 1, O_BANK + r, P:SEQ],
                                                vaug[:, v, 1, head, :], probs[:, p, 2, m * P:(m + 1) * P],
                                                start=False, stop=True, skip_group_check=True)
                if t == 1:
                    last.then_inc(pv_done, 1)

            def emit(it, j):
                for s in range(BANKS_U):
                    if live(unit(it, j, 0), UNITS):
                        score_bank(it, j, s)
                    if live(unit(it, j, L_EXP), UNITS):
                        shifted_bank(it, j, s)
                    g = group(it, j, L_SHIFT)
                    if s == 0 and (j - L_SHIFT) % UPG == 0 and live(g, GROUPS):
                        k = (j - L_SHIFT) // UPG
                        pe.wait_ge(maxed, BANKS_U * UPG * (g + 1))
                        if past(shifts_before(it, j)):
                            pe.wait_ge(shift_lo, shifts_before(it, j))
                        transposes_copied(it, j)
                        for t in range(TPS):
                            last = nc.tensor.transpose(ps[0:GMAPS, M_BANK, t * P:(t + 1) * P],
                                                       rowmax[:, k % 2, t, :], ident[:])
                        last.then_inc(maxT_done, 1)
                    if s < TPS and live(unit(it, j, L_PV), UNITS):
                        weigh_values(it, j, s)
                    if s == 0:
                        output_projection(it, j)
                n = unit(it, j, L_OT)
                if live(n, UNITS):
                    g, b = group(it, j, L_SHIFT), seq(it, j, L_OPT + 1)
                    if (j - L_SHIFT) % UPG == 0 and live(g, GROUPS):
                        pe.wait_ge(shift_lo, g + 1)
                    if (j - L_OPT - 1) % UPS == 0 and live(b, SEQS):
                        pe.wait_ge(oT_done, b + 1)
                    b = seq(it, j, L_OPROJ)
                    if (j - L_OPROJ) % UPS == 0 and live(b, SEQS):
                        pe.wait_ge(resid_done, FIRST + b + 1)
                    pe.wait_ge(ot_copied, n + 1)
                    if past(n):
                        pe.wait_ge(o_copied, n)
                    for t in range(TPS):
                        last = nc.tensor.transpose(ps[:, M_BANK, t * P:(t + 1) * P],
                                                   ot_sb[:, (j - L_OT) % 2, t * P:(t + 1) * P], ident[:])
                    last.then_inc(ott_done, 1)
                b = seq(it, j, L_OPT)
                if (j - L_OPT) % UPS == 0 and live(b, SEQS):
                    pe.wait_ge(normed, FIRST + b + 1)
                    transposes_copied(it, j + 1)
                    if past(b):
                        pe.wait_ge(resid_done, FIRST + b)
                    flat = o_n.rearrange("p t h d -> p t (h d)")
                    for t in range(TPS):
                        for c in range(2):
                            last = nc.tensor.transpose(ps[:, M_BANK, (2 * t + c) * P:(2 * t + c + 1) * P],
                                                       flat[:, t, c * P:(c + 1) * P], ident[:])
                    last.then_inc(nT_done, 1)

            def transposes_copied(it, j):
                n = unit(it, j, L_OT)
                n = min(n, UNITS) if isinstance(n, int) else n
                if past(n):
                    pe.wait_ge(o_copied, n)

            def output_projection(it, j):
                b = seq(it, j, L_OPROJ)
                if (j - L_OPROJ) % UPS == 0 and live(b, SEQS):
                    pe.wait_ge(oT_done, b + 1)
                    transposes_copied(it, j)
                    for t in range(TPS):
                        for c in range(2):
                            last = nc.tensor.matmul(ps[:, M_BANK, t * D:(t + 1) * D], oT[:, t, c, :],
                                                    wo[:, c, :], start=(c == 0), stop=(c == 1))
                    last.then_inc(oproj_done, 1)

            pe.wait_ge(cleared, 1)
            turns(pe, emit, amid)

        BT = 4
        BLOCKS = TILES // BT
        SPB = BT // TPS
        at = 0
        hT, at = carve(at, (2, FCH, BT * P))
        f_xn, at = carve(at, (2, BT, D))
        f_xnT, at = carve(at, (2, BT * P))
        feed_end = at

        def feed_sems(tag):
            return {k: sem(f"{tag}_{k}") for k in "std rstd ln xn xT xnT up gelu down res st mom stored".split()}

        F1, F2 = feed_sems("f1"), feed_sems("f2")

        def block_std(act, S, *blocks):
            for k in blocks:
                c = slice(BT * k, BT * k + BT)
                nc.scalar.activation(std[:, c], moments[:, c, 1], ACT.Sqrt, bias=eps[:, 0:1]).then_inc(S["std"], 1)

        def block_rstd(dve, S, *blocks):
            for k in blocks:
                c = slice(BT * k, BT * k + BT)
                dve.wait_ge(S["std"], k + 1)
                nc.vector.reciprocal(rstd[:, c], std[:, c]).then_inc(S["rstd"], 1)
                dve.wait_ge(S["rstd"], k + 1)
                nc.vector.scalar_tensor_tensor(out=shift_ln[:, c], in0=moments[:, c, 0], scalar=-1.0,
                                               in1=rstd[:, c], op0=ALU.mult, op1=ALU.mult).then_inc(S["ln"], 1)

        def normed_rows(act, out_tile, tile):
            return nc.scalar.activation(out_tile, xs[:, tile, :], ACT.Identity, bias=shift_ln[:, bass.ds(tile, 1)],
                                        scale=rstd[:, bass.ds(tile, 1)])

        def feed_rows_scalar(act, S, k):
            act.wait_ge(S["ln"], k + 1)
            if k >= 2:
                act.wait_ge(S["xT"], k - 1)
            for t in range(BT):
                last = normed_rows(act, f_xn[:, k % 2, t, :], BT * k + t)
            last.then_inc(S["xn"], 1)

        def feed_columns_scalar(act, S, k):
            act.wait_ge(S["xT"], k + 1)
            if k >= 2:
                act.wait_ge(S["up"], FCH * (k - 1))
            nc.scalar.copy(f_xnT[:, k % 2, :], ps[:, k % 2, :]).then_inc(S["xnT"], 1)

        def feed_gelu_scalar(act, S, k):
            if k >= 2:
                act.wait_ge(S["down"], k - 1)
            for c in range(FCH):
                act.wait_ge(S["up"], FCH * k + c + 1)
                nc.scalar.activation(hT[:, k % 2, c, :], ps[:, 2 + c, :], ACT.Gelu_apprx_tanh)\
                    .then_inc(S["gelu"], 1)

        def feed_residual_vector(dve, S, k):
            x4 = xs[:, BT * k:BT * k + BT, :].rearrange("p t d -> p (t d)")
            dve.wait_ge(S["down"], k + 1)
            nc.vector.tensor_tensor(x4, ps[:, 6 + k % 2, :], x4, op=ALU.add).then_inc(S["res"], 1)
            if S is F1:
                dve.wait_ge(S["res"], k + 1)
                token_moments(dve, tick_dve, BT * k, BT, S["st"], S["mom"], k, at=TPS)

        def feed_transpose_tensor(pe, S, k):
            pe.wait_ge(S["xn"], k + 1)
            if k >= 2:
                pe.wait_ge(S["xnT"], k - 1)
            for t in range(BT):
                last = nc.tensor.transpose(ps[:, k % 2, t * P:(t + 1) * P], f_xn[:, k % 2, t, :], ident[:])
            last.then_inc(S["xT"], 1)

        def feed_up_tensor(pe, S, k):
            pe.wait_ge(S["xnT"], k + 1)
            for c in range(FCH):
                if k > 0:
                    pe.wait_ge(S["gelu"], FCH * (k - 1) + c + 1)
                nc.tensor.matmul(ps[:, 2 + c, :], w1[:, c * P:(c + 1) * P], f_xnT[:, k % 2, :],
                                 start=True, stop=True).then_inc(S["up"], 1)

        def feed_down_tensor(pe, S, k):
            pe.wait_ge(S["gelu"], FCH * (k + 1))
            if k >= 2:
                pe.wait_ge(S["res"], k - 1)
            for t in range(BT):
                for c in range(FCH):
                    last = nc.tensor.matmul(ps[:, 6 + k % 2, t * D:(t + 1) * D],
                                            hT[:, k % 2, c, t * P:(t + 1) * P], w2[:, c, :],
                                            start=(c == 0), stop=(c == FCH - 1))
            last.then_inc(S["down"], 1)

        def feed_store_sync(sp):
            for k in range(TILES // BT):
                sp.wait_ge(F2["res"], k + 1)
                sp.dma_start(out_tiles[:, BT * k:BT * k + BT, :], xs[:, BT * k:BT * k + BT, :])\
                  .then_inc(F2["stored"], 16)
            sp.wait_ge(F2["stored"], 16 * TILES // BT)


        E1 = DH + 1
        EG = 3
        at = feed_end
        xn, at = carve(at, (2, TPS, D))
        xnT, at = carve(at, (2, TPS * P))
        low, at = carve(at, (2, TPS, 2 * D))
        phi, at = carve(at, (2, TPS, 2 * D))
        vb, at = carve(at, (2, TPS, D))
        kv, at = carve(at, (2, TPS, E1, D))
        prod, at = carve(at, (2, E1, D))
        nd, at = carve(at, (2, TPS, E1, HEADS))
        inv, at = carve(at, (2, TPS, HEADS))
        o, at = carve(at, (2, TPS, D))
        oT_l, at = carve(at, (2, TPS * P))
        names = ("std rstd ln xn xT xnT qkv neg exp phi v kv pre prod nd inv oraw o oT oTs out res st mom").split()
        L = {k: sem(f"l_{k}") for k in names}
        PROJ, SUM, BACK = 1, 2, 3

        def slots(eng, emit, amid):
            for m in range(4):
                amid(m)
                emit(m // 2, m % 2)
            amid(4)
            with eng.Fori(2, SEQS // 2) as it:
                for u in range(2):
                    emit(it, u)
            for m in range(BACK):
                amid(SEQS + m)
                emit(SEQS // 2 + m // 2, m % 2)

        def linear_gpsimd(pool, amid):
            pool.sem_inc(L["oraw"], FIRST)

            def emit(it, u):
                b, w = 2 * it + u - BACK, (u - BACK) % 2
                if live(b, SEQS):
                    pool.wait_ge(L["inv"], b + 1)
                    if past(b - 1):
                        pool.wait_ge(L["oT"], FIRST + b - 1)
                    for t in range(TPS):
                        last = nc.gpsimd.tensor_tensor(
                            o[:, w, t, :].rearrange("p (h e) -> p e h", e=DH), nd[:, w, t, 0:DH, :],
                            inv[:, w, t, :].unsqueeze(1).to_broadcast([P, DH, HEADS]), op=ALU.mult)
                    last.then_inc(L["oraw"], 1)
                    pool.wait_ge(L["oraw"], FIRST + b + 1)
                    carry_wait(pool, tick_pool)
                    nc.gpsimd.tensor_scalar(o[:, w], o[:, w], LIN_EPS, None, op0=ALU.add)\
                        .then_inc(L["o"], 1)
                b, w = 2 * it + u - PROJ, (u - PROJ) % 2
                if live(b, SEQS):
                    for t in range(TPS):
                        pool.wait_ge(L["phi"], TPS * b + t + 1)
                        pool.wait_ge(L["v"], TPS * b + t + 1)
                        if past(b - 1):
                            pool.wait_ge(L["pre"], 2 * EG * (b - 1))
                        kh = phi[:, w, t, D:2 * D].rearrange("p (h d) -> p h d", d=DH)
                        vh = vb[:, w, t, :].rearrange("p (h e) -> p e h", e=DH)
                        nc.gpsimd.tensor_tensor(
                            kv[:, w, t, 0:DH, :].rearrange("p e (h d) -> p e h d", d=DH),
                            kh.unsqueeze(1).to_broadcast([P, DH, HEADS, DH]),
                            vh.unsqueeze(3).to_broadcast([P, DH, HEADS, DH]), op=ALU.mult)\
                            .then_inc(L["kv"], 1)
                        nc.gpsimd.tensor_copy(kv[:, w, t, DH, :], phi[:, w, t, D:2 * D])\
                            .then_inc(L["kv"], 1)

            slots(pool, emit, amid)

        def linear_scalar(act, amid):
            def emit(it, u):
                b = 2 * it + u
                if live(b, SEQS):
                    if past(b - 1):
                        act.wait_ge(L["xT"], b - 1)
                    for t in range(TPS):
                        tile = TPS * b + t
                        last = normed_rows(act, xn[:, u, t, :], tile)
                    last.then_inc(L["xn"], 1)
                b, w = 2 * it + u - PROJ, (u - PROJ) % 2
                if live(b, SEQS):
                    for t in range(TPS):
                        act.wait_ge(L["qkv"], TPS * b + t + 1)
                        if past(b - 1):
                            act.wait_ge(L["phi"], TPS * (b - 1))
                        nc.scalar.activation(low[:, w, t, :], ps[:, 1 + t, 0:2 * D], ACT.Relu,
                                             scale=-1.0).then_inc(L["neg"], 1)
                        if past(b - 1):
                            act.wait_ge(L["kv"], 2 * TPS * (b - 1))
                        nc.scalar.copy(vb[:, w, t, :], ps[:, 1 + t, 2 * D:3 * D]).then_inc(L["v"], 1)
                        act.wait_ge(L["neg"], TPS * b + t + 1)
                        nc.scalar.activation(low[:, w, t, :], low[:, w, t, :], ACT.Exp, scale=-1.0)\
                            .then_inc(L["exp"], 1)
                b = 2 * it + u
                if live(b, SEQS):
                    act.wait_ge(L["xT"], b + 1)
                    if past(b - 1):
                        act.wait_ge(L["qkv"], TPS * (b - 1))
                    nc.scalar.copy(xnT[:, u, :], ps[:, 0, 0:TPS * P]).then_inc(L["xnT"], 1)
                b, w = 2 * it + u - BACK, (u - BACK) % 2
                if live(b, SEQS):
                    act.wait_ge(L["oT"], FIRST + b + 1)
                    if past(b - 1):
                        act.wait_ge(L["out"], FIRST + b - 1)
                    nc.scalar.copy(oT_l[:, w, :], ps[:, 7, 0:TPS * P]).then_inc(L["oTs"], 1)

            slots(act, emit, amid)

        def linear_vector(dve, amid):
            def weigh(it, u, i):
                b, w = 2 * it + u - SUM, (u - SUM) % 2
                if live(b, SEQS):
                    t, e = i // EG, i % EG
                    dve.wait_ge(L["pre"], 2 * EG * b + i + 1)
                    if past(TPS * b + t - 1):
                        dve.wait_ge(L["nd"], TPS * b + t - 1)
                    nc.vector.tensor_tensor(
                        prod[:, t, EG * e:EG * e + EG, :],
                        ps[:, 3 + (2 * EG * w + i) % 4, 0:EG * D].rearrange("p (e d) -> p e d", e=EG),
                        phi[:, w, t, 0:D].unsqueeze(1).to_broadcast([P, EG, D]),
                        op=ALU.mult).then_inc(L["prod"], 1)

            def sum_width(it, u, t):
                b, w = 2 * it + u - SUM, (u - SUM) % 2
                if live(b, SEQS):
                    dve.wait_ge(L["prod"], 2 * EG * b + EG * (t + 1))
                    if past(b - 1):
                        dve.wait_ge(L["oraw"], FIRST + b - 1)
                    nc.vector.tensor_reduce(
                        out=nd[:, w, t].rearrange("p e h -> p (e h)"),
                        in_=prod[:, t].rearrange("p e (h d) -> p (e h) d", d=DH), axis=AX,
                        op=ALU.add).then_inc(L["nd"], 1)

            def elu(it, u, t):
                b, w = 2 * it + u - PROJ, (u - PROJ) % 2
                if live(b, SEQS):
                    dve.wait_ge(L["exp"], TPS * b + t + 1)
                    if past(b - 1):
                        dve.wait_ge(L["kv"], 2 * TPS * (b - 1))
                        dve.wait_ge(L["prod"], 2 * EG * (b - 1))
                    nc.vector.scalar_tensor_tensor(
                        out=phi[:, w, t, :], in0=ps[:, 1 + t, 0:2 * D], scalar=0.0,
                        in1=low[:, w, t, :], op0=ALU.max, op1=ALU.add).then_inc(L["phi"], 1)

            def emit(it, u):
                weigh(it, u, 0)
                elu(it, u, 0)
                elu(it, u, 1)
                weigh(it, u, 1)
                weigh(it, u, 2)
                sum_width(it, u, 0)
                for i in range(EG, 2 * EG):
                    weigh(it, u, i)
                sum_width(it, u, 1)
                b, w = 2 * it + u - SUM, (u - SUM) % 2
                if live(b, SEQS):
                    dve.wait_ge(L["nd"], TPS * (b + 1))
                    nc.vector.reciprocal(inv[:, w], nd[:, w, :, DH, :]).then_inc(L["inv"], 1)
                b = 2 * it + u - BACK
                if live(b, SEQS):
                    dve.wait_ge(L["out"], FIRST + b + 1)
                    x2 = xs[:, bass.ds(2 * b, 2), :].rearrange("p t d -> p (t d)")
                    nc.vector.tensor_tensor(x2, ps[:, 7, 256:256 + TPS * D], x2, op=ALU.add)\
                        .then_inc(L["res"], 1)
                    dve.wait_ge(L["res"], b + 1)
                    token_moments(dve, tick_dve, TPS * b, TPS, L["st"], L["mom"], b, at=TPS + BT)

            slots(dve, emit, amid)

        def linear_tensor(pe, amid):
            pe.sem_inc(L["out"], FIRST)
            pe.sem_inc(L["oT"], FIRST)

            def running_sums(it, u, i):
                b, w = 2 * it + u - SUM, (u - SUM) % 2
                if live(b, SEQS):
                    t, e = i // EG, i % EG
                    pe.wait_ge(L["kv"], 2 * TPS * b + 2 * (t + 1))
                    if past(2 * EG * b + i - 3):
                        pe.wait_ge(L["prod"], 2 * EG * b + i - 3)
                    bank = ps[:, 3 + (2 * EG * w + i) % 4, 0:EG * D]
                    rows = kv[:, w, t, EG * e:EG * e + EG, :].rearrange("p e d -> p (e d)")
                    last = nc.tensor.matmul(bank, upto[:], rows, start=True, stop=(t == 0))
                    if t == 1:
                        rows = kv[:, w, 0, EG * e:EG * e + EG, :].rearrange("p e d -> p (e d)")
                        last = nc.tensor.matmul(bank, ones[:], rows, start=False, stop=True)
                    last.then_inc(L["pre"], 1)

            def emit(it, u):
                b, w = 2 * it + u - PROJ, (u - PROJ) % 2
                if live(b, SEQS):
                    for t in range(TPS):
                        pe.wait_ge(L["xnT"], b + 1)
                        if past(b):
                            pe.wait_ge(L["phi"], TPS * b)
                            pe.wait_ge(L["v"], TPS * b)
                        nc.tensor.matmul(ps[:, 1 + t, 0:3 * D], xnT[:, w, t * P:(t + 1) * P],
                                         wbT[:, 0:3, :].rearrange("p a b -> p (a b)"),
                                         start=True, stop=True).then_inc(L["qkv"], 1)
                for i in range(EG):
                    running_sums(it, u, i)
                b = 2 * it + u
                if live(b, SEQS):
                    pe.wait_ge(L["xn"], b + 1)
                    if past(b):
                        pe.wait_ge(L["xnT"], b)
                    for t in range(TPS):
                        last = nc.tensor.transpose(ps[:, 0, t * P:(t + 1) * P], xn[:, u, t, :], ident[:])
                    last.then_inc(L["xT"], 1)
                running_sums(it, u, EG)
                b, w = 2 * it + u - BACK, (u - BACK) % 2
                if live(b, SEQS):
                    pe.wait_ge(L["o"], b + 1)
                    if past(b):
                        pe.wait_ge(L["res"], b)
                    for t in range(TPS):
                        last = nc.tensor.transpose(ps[:, 7, t * P:(t + 1) * P], o[:, w, t, :], ident[:])
                    last.then_inc(L["oT"], 1)
                running_sums(it, u, EG + 1)
                running_sums(it, u, EG + 2)
                if live(b, SEQS):
                    pe.wait_ge(L["oTs"], b + 1)
                    for t in range(TPS):
                        last = nc.tensor.matmul(ps[:, 7, 256 + t * D:256 + (t + 1) * D],
                                                oT_l[:, w, t * P:(t + 1) * P], wbT[:, 3, :],
                                                start=True, stop=True)
                    last.then_inc(L["out"], 1)

            slots(pe, emit, amid)

        with nc.Block() as block:
            @block.sync
            def _(sp):
                attend_sync(sp)
                feed_store_sync(sp)

            @block.gpsimd
            def _(pool):
                attend_gpsimd(pool, lambda slot: None)
                linear_gpsimd(pool, lambda slot: None)

            @block.scalar
            def _(act):
                def amid_attend(slot):
                    if slot == TAIL - 3:
                        act.wait_ge(mom2_done, FIRST + 2 * SPB * 3)
                        block_std(act, F1, 0, 1, 2)
                    if slot == TAIL - 2:
                        feed_rows_scalar(act, F1, 0)
                        feed_rows_scalar(act, F1, 1)
                    if slot == TAIL - 1:
                        feed_columns_scalar(act, F1, 0)
                        feed_columns_scalar(act, F1, 1)
                        load_table(act, ACT.Gelu_apprx_tanh)
                    if slot == TAIL + 1:
                        feed_gelu_scalar(act, F1, 0)
                    if slot == TAIL_OUT:
                        feed_rows_scalar(act, F1, 2)
                        feed_gelu_scalar(act, F1, 1)
                        feed_columns_scalar(act, F1, 2)
                    if slot == TAIL_OUT + 1:
                        feed_gelu_scalar(act, F1, 2)
                        load_table(act, ACT.Sqrt)

                def amid_linear(slot):
                    if slot == 0:
                        act.wait_ge(mom2_done, FIRST + 2 * SEQS)
                        block_std(act, F1, 3)
                        act.wait_ge(F1["mom"], 2)
                        act.wait_ge(F1["rstd"], 2)
                        block_std(act, L, 0)
                        feed_rows_scalar(act, F1, 3)
                        feed_columns_scalar(act, F1, 3)
                        act.wait_ge(L["ln"], 1)
                    if slot == 1:
                        act.wait_ge(F1["mom"], 2 * 2)
                        block_std(act, L, 1)
                        load_table(act, ACT.Gelu_apprx_tanh)
                        feed_gelu_scalar(act, F1, 3)
                        load_table(act, ACT.Exp)
                    if slot == 2:
                        act.wait_ge(L["ln"], 2)
                    if slot == 3:
                        act.wait_ge(F1["mom"], 2 * BLOCKS)
                        act.wait_ge(F1["rstd"], BLOCKS)
                        block_std(act, L, 2, 3)
                        load_table(act, ACT.Exp)
                    if slot == 4:
                        act.wait_ge(L["ln"], BLOCKS)
                    if slot == SEQS:
                        act.wait_ge(L["mom"], 2 * SPB * 2)
                        act.wait_ge(L["rstd"], 2)
                        block_std(act, F2, 0, 1)
                    if slot == SEQS + 1:
                        feed_rows_scalar(act, F2, 0)
                        feed_rows_scalar(act, F2, 1)
                        feed_columns_scalar(act, F2, 0)
                        feed_columns_scalar(act, F2, 1)
                    if slot == SEQS + 2:
                        load_table(act, ACT.Gelu_apprx_tanh)
                        feed_gelu_scalar(act, F2, 0)

                attend_scalar(act, amid_attend)
                linear_scalar(act, amid_linear)
                load_table(act, ACT.Sqrt)
                act.wait_ge(L["mom"], 2 * SEQS)
                act.wait_ge(L["rstd"], BLOCKS)
                block_std(act, F2, 2, 3)
                feed_rows_scalar(act, F2, 2)
                feed_gelu_scalar(act, F2, 1)
                feed_columns_scalar(act, F2, 2)
                feed_rows_scalar(act, F2, 3)
                feed_gelu_scalar(act, F2, 2)
                feed_columns_scalar(act, F2, 3)
                feed_gelu_scalar(act, F2, 3)

            @block.vector
            def _(dve):
                def amid_attend(slot):
                    if slot == TAIL - 2:
                        dve.wait_ge(scoredT, BANKS_U * UNITS)
                        block_rstd(dve, F1, 0, 1, 2)
                    if slot == TAIL_OUT + 1:
                        feed_residual_vector(dve, F1, 0)

                def amid_linear(slot):
                    if slot == 0:
                        block_rstd(dve, F1, 3)
                        dve.wait_ge(F1["xn"], 2)
                        block_rstd(dve, L, 0)
                        feed_residual_vector(dve, F1, 1)
                        block_rstd(dve, L, 1)
                        feed_residual_vector(dve, F1, 2)
                    if slot == 2:
                        feed_residual_vector(dve, F1, 3)
                    if slot == 3:
                        dve.wait_ge(F1["xn"], BLOCKS)
                        block_rstd(dve, L, 2, 3)
                    if slot == SEQS:
                        dve.wait_ge(L["xn"], SPB * 2)
                        block_rstd(dve, F2, 0, 1)

                attend_vector(dve, amid_attend)
                linear_vector(dve, amid_linear)
                dve.wait_ge(L["xn"], SEQS)
                block_rstd(dve, F2, 2, 3)
                for k in range(BLOCKS):
                    feed_residual_vector(dve, F2, k)

            @block.tensor
            def _(pe):
                def amid_attend(slot):
                    if slot == TAIL - 1:
                        pe.wait_ge(maxed, BANKS_U * UNITS)
                        feed_transpose_tensor(pe, F1, 0)
                        feed_transpose_tensor(pe, F1, 1)
                    if slot == TAIL:
                        pe.wait_ge(exp_done, BANKS_U * UNITS)
                        pe.wait_ge(ot_copied, UNITS)
                        feed_up_tensor(pe, F1, 0)
                        feed_up_tensor(pe, F1, 1)
                        feed_transpose_tensor(pe, F1, 2)
                        pe.wait_ge(o_copied, UNITS)
                        feed_down_tensor(pe, F1, 0)
                        feed_up_tensor(pe, F1, 2)

                def amid_linear(slot):
                    if slot == 0:
                        pe.wait_ge(resid_done, FIRST + SEQS)
                        feed_down_tensor(pe, F1, 1)
                        feed_transpose_tensor(pe, F1, 3)
                        feed_down_tensor(pe, F1, 2)
                        pe.wait_ge(F1["xnT"], BLOCKS)
                    if slot == 1:
                        feed_up_tensor(pe, F1, 3)
                        pe.wait_ge(F1["gelu"], FCH * (BLOCKS - 1) + 1)
                    if slot == 2:
                        feed_down_tensor(pe, F1, 3)
                        pe.wait_ge(F1["gelu"], FCH * BLOCKS)
                        pe.wait_ge(F1["res"], BLOCKS - 1)
                    if slot == 3:
                        pe.wait_ge(F1["res"], BLOCKS)
                    if slot == SEQS + 1:
                        pe.wait_ge(L["xnT"], SEQS)
                        pe.wait_ge(L["phi"], TPS * SEQS)
                        feed_transpose_tensor(pe, F2, 0)
                        feed_transpose_tensor(pe, F2, 1)
                    if slot == SEQS + 2:
                        pe.wait_ge(L["prod"], 2 * EG * SEQS)
                        feed_up_tensor(pe, F2, 0)

                attend_tensor(pe, amid_attend)
                linear_tensor(pe, amid_linear)
                feed_up_tensor(pe, F2, 1)
                feed_down_tensor(pe, F2, 0)
                feed_transpose_tensor(pe, F2, 2)
                pe.wait_ge(L["res"], SEQS)
                feed_down_tensor(pe, F2, 1)
                feed_up_tensor(pe, F2, 2)
                feed_transpose_tensor(pe, F2, 3)
                feed_down_tensor(pe, F2, 2)
                feed_up_tensor(pe, F2, 3)
                feed_down_tensor(pe, F2, 3)


_INS = ['L0_attn_a_X', 'L0_attn_a_Wq', 'L0_attn_a_Wk', 'L0_attn_a_Wv', 'L0_attn_a_Wo',
        'L0_attn_a_lambda_q1', 'L0_attn_a_lambda_k1', 'L0_attn_a_lambda_q2', 'L0_attn_a_lambda_k2',
        'L0_attn_a_rms_scale', 'L0_attn_b_Wq', 'L0_attn_b_Wk', 'L0_attn_b_Wv', 'L0_attn_b_Wo',
        'L0_ffn_fc1_A', 'L0_ffn_fc1_B', 'L0_ffn_fc2_A', 'L0_ffn_fc2_B', 'L0_ffn_fc1_logits',
        'L0_ffn_fc2_logits']
_OUTS = [((SEQS, SEQ, D), 'float32')]


def kernel(**inputs):
    import numpy as _np
    import concourse.bacc as _bacc
    from concourse import mybir as _mybir
    from concourse.bass_utils import run_bass_kernel_spmd as _run

    nc = _bacc.Bacc("TRN2", target_bir_lowering=False, num_devices=1)
    arrays, args = {}, []
    for name in _INS:
        a = _np.ascontiguousarray(inputs[name])
        arrays[f"in_{name}_dram"] = a
        args.append(nc.dram_tensor(f"in_{name}_dram", a.shape, _mybir.dt.from_np(a.dtype), kind="ExternalInput").ap())
    for i, (shape, dtype) in enumerate(_OUTS):
        dt = _mybir.dt.from_np(_np.dtype(dtype))
        args.append(nc.dram_tensor(f"out_{i}_dram", shape, dt, kind="ExternalOutput").ap())
    hybrid_kernel(nc, *args)
    r = _run(nc, [arrays], core_ids=[0])
    return r.results[0]["out_0_dram"]
```
